# Optimizing a Trainium2 kernel written in Bass

```python
import numpy as np
import jax
import jax.numpy as jnp

def _softmax(x, axis=-1):
    return jax.nn.softmax(x, axis=axis)
def _gelu(x):
    return jax.nn.gelu(x, approximate=True)
def _silu(x):
    return jax.nn.silu(x)
def _sigmoid(x):
    return jax.nn.sigmoid(x)
def _layernorm(x, axis=-1, eps=1e-5):
    m = jnp.mean(x, axis=axis, keepdims=True)
    v = jnp.var(x, axis=axis, keepdims=True)
    return (x - m) / jnp.sqrt(v + eps)
def _scatter_add(tgt, idx, src, axis=0):
    return tgt.at[idx].add(src)
def _segment_sum(src, seg, n):
    return jax.ops.segment_sum(src, seg, n)

kernel_name = 'mk_conv_seq_d2_conv_nchw512_56f4fe'

def setup_inputs(seed: int = 0):
    np.random.seed(seed)
    _w = jnp.asarray
    def _rec_inputs():
        import jax
        import jax.numpy as jnp
        _gk = jax.random.key(seed)
        x = 7.22e-05 + 1 * jax.random.normal(jax.random.fold_in(_gk, 1), (4, 512, 64, 64), jnp.float32)
        return x
    x = _rec_inputs()
    def _L0_conv_setup():
        import jax, jax.numpy as jnp
        import numpy as np
        from jax import lax
        IN_CH = 512
        OUT_CH = 512
        HEAD_DIM = 8
        NUM_HEADS = IN_CH // HEAD_DIM
        INNER = NUM_HEADS * HEAD_DIM
        KSIZE = 5
        EPS = 1e-15
        BN_EPS = 1e-05
        DN = ('NCHW', 'OIHW', 'NCHW')

        def _forward(hidden_states, wq, wk, wv, dw_kernel, pw_kernel, proj_kernel, bn_gamma, bn_beta, bn_mean, bn_var):
            x = hidden_states
            B, _, H, W = x.shape
            h = jnp.moveaxis(x, 1, -1)
            q = h @ wq.T
            k = h @ wk.T
            v = h @ wv.T
            qkv = jnp.moveaxis(jnp.concatenate([q, k, v], axis=-1), -1, 1)
            dw = lax.conv_general_dilated(qkv, dw_kernel, (1, 1), 'SAME', feature_group_count=3 * INNER, dimension_numbers=DN)
            pw = lax.conv_general_dilated(dw, pw_kernel, (1, 1), 'VALID', feature_group_count=3 * NUM_HEADS, dimension_numbers=DN)
            qkv_all = jnp.concatenate([qkv, pw], axis=1)
            N = H * W
            d = HEAD_DIM
            f = qkv_all.astype(jnp.float32).reshape(B, -1, 3 * d, N)
            query = jax.nn.relu(f[:, :, :d])
            key_ = jax.nn.relu(f[:, :, d:2 * d])
            value = f[:, :, 2 * d:]
            value_pad = jnp.concatenate([value, jnp.ones_like(value[:, :, :1])], axis=2)
            scores = jnp.einsum('bhdn,bhen->bhde', value_pad, key_)
            out = jnp.einsum('bhde,bhen->bhdn', scores, query)
            out = out[:, :, :-1] / (out[:, :, -1:] + EPS)
            out = out.reshape(B, -1, H, W).astype(qkv_all.dtype)
            y = lax.conv_general_dilated(out, proj_kernel, (1, 1), 'VALID', dimension_numbers=DN)
            inv = bn_gamma / jnp.sqrt(bn_var + BN_EPS)
            y = y * inv[None, :, None, None] + (bn_beta - bn_mean * inv)[None, :, None, None]
            return y + x
        key = jax.random.key(seed)
        ks = jax.random.split(key, 10)
        s = 0.02
        return {'hidden_states': jax.random.normal(ks[0], (4, IN_CH, 64, 64), jnp.float32), 'wq': jax.random.normal(ks[1], (INNER, IN_CH), jnp.float32) * s, 'wk': jax.random.normal(ks[2], (INNER, IN_CH), jnp.float32) * s, 'wv': jax.random.normal(ks[3], (INNER, IN_CH), jnp.float32) * s, 'dw_kernel': jax.random.normal(ks[4], (3 * INNER, 1, KSIZE, KSIZE), jnp.float32) * s, 'pw_kernel': jax.random.normal(ks[5], (3 * INNER, HEAD_DIM, 1, 1), jnp.float32) * s, 'proj_kernel': jax.random.normal(ks[6], (OUT_CH, 2 * INNER, 1, 1), jnp.float32) * s, 'bn_gamma': jnp.ones((OUT_CH,), jnp.float32), 'bn_beta': jnp.zeros((OUT_CH,), jnp.float32), 'bn_mean': jnp.zeros((OUT_CH,), jnp.float32), 'bn_var': jnp.ones((OUT_CH,), jnp.float32)}
    _L0_conv_all = _L0_conv_setup()
    _L0_conv_in = {k: v for k, v in _L0_conv_all.items() if k in ('wq', 'wk', 'wv', 'dw_kernel', 'pw_kernel', 'proj_kernel', 'bn_gamma', 'bn_beta', 'bn_mean', 'bn_var', )}
    del _L0_conv_all

    def _L1_conv_setup():
        import jax, jax.numpy as jnp
        import numpy as np
        from jax import lax
        K_SX = jnp.array([[-1.0, 0.0, 1.0], [-2.0, 0.0, 2.0], [-1.0, 0.0, 1.0]], jnp.float32)
        K_SY = jnp.array([[-1.0, -2.0, -1.0], [0.0, 0.0, 0.0], [1.0, 2.0, 1.0]], jnp.float32)
        K_LAP = jnp.array([[0.0, 1.0, 0.0], [1.0, -4.0, 1.0], [0.0, 1.0, 0.0]], jnp.float32)
        K_D1 = jnp.array([[1.0, 0.0, -1.0], [0.0, 0.0, 0.0], [-1.0, 0.0, 1.0]], jnp.float32)
        K_D2 = jnp.array([[-1.0, 0.0, 1.0], [0.0, 0.0, 0.0], [1.0, 0.0, -1.0]], jnp.float32)
        BN_EPS = 1e-05
        LN_EPS = 1e-06

        def dwconv(x, k):
            C = x.shape[1]
            kern = jnp.broadcast_to(k[None, None], (C, 1, 3, 3))
            return lax.conv_general_dilated(x, kern, window_strides=(1, 1), padding='SAME', feature_group_count=C, dimension_numbers=('NCHW', 'OIHW', 'NCHW'))
        key = jax.random.key(seed)
        ks = jax.random.split(key, 6)
        B, C, H, W = (4, 512, 128, 128)
        Cq, Ce = (C // 4, C // 8)
        return {'x': jax.random.normal(ks[0], (B, C, H, W), jnp.float32), 'w_branch': jax.random.normal(ks[1], (4, Cq, C), jnp.float32) * 0.02, 'b_branch': jnp.zeros((4, Cq), jnp.float32), 'bn_gamma': jnp.ones((4, Cq), jnp.float32), 'bn_beta': jnp.zeros((4, Cq), jnp.float32), 'w_att1': jax.random.normal(ks[2], (Ce, C), jnp.float32) * 0.02, 'b_att1': jnp.zeros((Ce,), jnp.float32), 'w_att2': jax.random.normal(ks[3], (C, Ce), jnp.float32) * 0.02, 'b_att2': jnp.zeros((C,), jnp.float32), 'w_fuse': jax.random.normal(ks[4], (C, C), jnp.float32) * 0.02, 'b_fuse': jnp.zeros((C,), jnp.float32), 'ln_gamma': jnp.ones((C,), jnp.float32), 'ln_beta': jnp.zeros((C,), jnp.float32)}
    _L1_conv_all = _L1_conv_setup()
    _L1_conv_in = {k: v for k, v in _L1_conv_all.items() if k in ('w_branch', 'b_branch', 'bn_gamma', 'bn_beta', 'w_att1', 'b_att1', 'w_att2', 'b_att2', 'w_fuse', 'b_fuse', 'ln_gamma', 'ln_beta', )}
    del _L1_conv_all

    return {
        "x": x,
        "L0_conv_wq": _L0_conv_in["wq"],
        "L0_conv_wk": _L0_conv_in["wk"],
        "L0_conv_wv": _L0_conv_in["wv"],
        "L0_conv_dw_kernel": _L0_conv_in["dw_kernel"],
        "L0_conv_pw_kernel": _L0_conv_in["pw_kernel"],
        "L0_conv_proj_kernel": _L0_conv_in["proj_kernel"],
        "L0_conv_bn_gamma": _L0_conv_in["bn_gamma"],
        "L0_conv_bn_beta": _L0_conv_in["bn_beta"],
        "L0_conv_bn_mean": _L0_conv_in["bn_mean"],
        "L0_conv_bn_var": _L0_conv_in["bn_var"],
        "L1_conv_w_branch": _L1_conv_in["w_branch"],
        "L1_conv_b_branch": _L1_conv_in["b_branch"],
        "L1_conv_bn_gamma": _L1_conv_in["bn_gamma"],
        "L1_conv_bn_beta": _L1_conv_in["bn_beta"],
        "L1_conv_w_att1": _L1_conv_in["w_att1"],
        "L1_conv_b_att1": _L1_conv_in["b_att1"],
        "L1_conv_w_att2": _L1_conv_in["w_att2"],
        "L1_conv_b_att2": _L1_conv_in["b_att2"],
        "L1_conv_w_fuse": _L1_conv_in["w_fuse"],
        "L1_conv_b_fuse": _L1_conv_in["b_fuse"],
        "L1_conv_ln_gamma": _L1_conv_in["ln_gamma"],
        "L1_conv_ln_beta": _L1_conv_in["ln_beta"],
    }

def reference(x, L0_conv_wq, L0_conv_wk, L0_conv_wv, L0_conv_dw_kernel, L0_conv_pw_kernel, L0_conv_proj_kernel, L0_conv_bn_gamma, L0_conv_bn_beta, L0_conv_bn_mean, L0_conv_bn_var, L1_conv_w_branch, L1_conv_b_branch, L1_conv_bn_gamma, L1_conv_bn_beta, L1_conv_w_att1, L1_conv_b_att1, L1_conv_w_att2, L1_conv_b_att2, L1_conv_w_fuse, L1_conv_b_fuse, L1_conv_ln_gamma, L1_conv_ln_beta):
    import jax
    import jax.numpy as jnp
    def _L0_conv_ref(hidden_states, wq, wk, wv, dw_kernel, pw_kernel, proj_kernel, bn_gamma, bn_beta, bn_mean, bn_var):
        import jax, jax.numpy as jnp
        import numpy as np
        from jax import lax
        IN_CH = 512
        OUT_CH = 512
        HEAD_DIM = 8
        NUM_HEADS = IN_CH // HEAD_DIM
        INNER = NUM_HEADS * HEAD_DIM
        KSIZE = 5
        EPS = 1e-15
        BN_EPS = 1e-05
        DN = ('NCHW', 'OIHW', 'NCHW')

        def _forward(hidden_states, wq, wk, wv, dw_kernel, pw_kernel, proj_kernel, bn_gamma, bn_beta, bn_mean, bn_var):
            x = hidden_states
            B, _, H, W = x.shape
            h = jnp.moveaxis(x, 1, -1)
            q = h @ wq.T
            k = h @ wk.T
            v = h @ wv.T
            qkv = jnp.moveaxis(jnp.concatenate([q, k, v], axis=-1), -1, 1)
            dw = lax.conv_general_dilated(qkv, dw_kernel, (1, 1), 'SAME', feature_group_count=3 * INNER, dimension_numbers=DN)
            pw = lax.conv_general_dilated(dw, pw_kernel, (1, 1), 'VALID', feature_group_count=3 * NUM_HEADS, dimension_numbers=DN)
            qkv_all = jnp.concatenate([qkv, pw], axis=1)
            N = H * W
            d = HEAD_DIM
            f = qkv_all.astype(jnp.float32).reshape(B, -1, 3 * d, N)
            query = jax.nn.relu(f[:, :, :d])
            key_ = jax.nn.relu(f[:, :, d:2 * d])
            value = f[:, :, 2 * d:]
            value_pad = jnp.concatenate([value, jnp.ones_like(value[:, :, :1])], axis=2)
            scores = jnp.einsum('bhdn,bhen->bhde', value_pad, key_)
            out = jnp.einsum('bhde,bhen->bhdn', scores, query)
            out = out[:, :, :-1] / (out[:, :, -1:] + EPS)
            out = out.reshape(B, -1, H, W).astype(qkv_all.dtype)
            y = lax.conv_general_dilated(out, proj_kernel, (1, 1), 'VALID', dimension_numbers=DN)
            inv = bn_gamma / jnp.sqrt(bn_var + BN_EPS)
            y = y * inv[None, :, None, None] + (bn_beta - bn_mean * inv)[None, :, None, None]
            return y + x
        return _forward(hidden_states, wq, wk, wv, dw_kernel, pw_kernel, proj_kernel, bn_gamma, bn_beta, bn_mean, bn_var)

    def _L1_conv_ref(x, w_branch, b_branch, bn_gamma, bn_beta, w_att1, b_att1, w_att2, b_att2, w_fuse, b_fuse, ln_gamma, ln_beta):
        import jax, jax.numpy as jnp
        import numpy as np
        from jax import lax
        K_SX = jnp.array([[-1.0, 0.0, 1.0], [-2.0, 0.0, 2.0], [-1.0, 0.0, 1.0]], jnp.float32)
        K_SY = jnp.array([[-1.0, -2.0, -1.0], [0.0, 0.0, 0.0], [1.0, 2.0, 1.0]], jnp.float32)
        K_LAP = jnp.array([[0.0, 1.0, 0.0], [1.0, -4.0, 1.0], [0.0, 1.0, 0.0]], jnp.float32)
        K_D1 = jnp.array([[1.0, 0.0, -1.0], [0.0, 0.0, 0.0], [-1.0, 0.0, 1.0]], jnp.float32)
        K_D2 = jnp.array([[-1.0, 0.0, 1.0], [0.0, 0.0, 0.0], [1.0, 0.0, -1.0]], jnp.float32)
        BN_EPS = 1e-05
        LN_EPS = 1e-06

        def dwconv(x, k):
            C = x.shape[1]
            kern = jnp.broadcast_to(k[None, None], (C, 1, 3, 3))
            return lax.conv_general_dilated(x, kern, window_strides=(1, 1), padding='SAME', feature_group_count=C, dimension_numbers=('NCHW', 'OIHW', 'NCHW'))
        B, C, H, W = x.shape
        sobel_h = dwconv(x, K_SX)
        sobel_v = dwconv(x, K_SY)
        sobel = jnp.sqrt(sobel_h ** 2 + sobel_v ** 2 + 1e-08)
        lap = jnp.abs(dwconv(x, K_LAP))
        diag = jnp.maximum(jnp.abs(dwconv(x, K_D1)), jnp.abs(dwconv(x, K_D2)))
        grad = jnp.sqrt(sobel ** 2 + lap ** 2 + 1e-08)
        E = jnp.stack([sobel, lap, diag, grad])
        y = jnp.einsum('kbchw,koc->kbohw', E, w_branch) + b_branch[:, None, :, None, None]
        bn_scale = bn_gamma / jnp.sqrt(1.0 + BN_EPS)
        y = y * bn_scale[:, None, :, None, None] + bn_beta[:, None, :, None, None]
        feat = jax.nn.gelu(y, approximate=False)
        ef = jnp.transpose(feat, (1, 0, 2, 3, 4)).reshape(B, C, H, W)
        pooled = ef.mean(axis=(2, 3))
        h = jax.nn.gelu(pooled @ w_att1.T + b_att1, approximate=False)
        att = jax.nn.sigmoid(h @ w_att2.T + b_att2)
        ef = ef * att[:, :, None, None]
        z = jnp.einsum('bchw,oc->bohw', ef, w_fuse) + b_fuse[None, :, None, None]
        mu = z.mean(axis=1, keepdims=True)
        var = ((z - mu) ** 2).mean(axis=1, keepdims=True)
        zn = (z - mu) / jnp.sqrt(var + LN_EPS)
        out = jax.nn.gelu(zn * ln_gamma[None, :, None, None] + ln_beta[None, :, None, None], approximate=False)
        return out + x

    def _gn(v, G=32, eps=1e-5):
        B_, C_, H_, W_ = v.shape
        g = v.reshape(B_, G, C_ // G, H_, W_)
        m = jnp.mean(g, axis=(2, 3, 4), keepdims=True)
        s = jnp.var(g, axis=(2, 3, 4), keepdims=True)
        return ((g - m) / jnp.sqrt(s + eps)).reshape(v.shape)

    def _ln_c(v, eps=1e-6):
        m = jnp.mean(v, axis=1, keepdims=True)
        s = jnp.var(v, axis=1, keepdims=True)
        return (v - m) / jnp.sqrt(s + eps)

    def _ln_t(v, eps=1e-5):
        m = jnp.mean(v, axis=-1, keepdims=True)
        s = jnp.var(v, axis=-1, keepdims=True)
        return (v - m) / jnp.sqrt(s + eps)

    def _to_tokens(v):
        B_, C_, H_, W_ = v.shape
        return v.reshape(B_, C_, H_ * W_).transpose(0, 2, 1)
    def _from_tokens(t, like):
        B_, C_, H_, W_ = like.shape
        return t.transpose(0, 2, 1).reshape(B_, C_, H_, W_)

    x = _L0_conv_ref(x, L0_conv_wq, L0_conv_wk, L0_conv_wv, L0_conv_dw_kernel, L0_conv_pw_kernel, L0_conv_proj_kernel, L0_conv_bn_gamma, L0_conv_bn_beta, L0_conv_bn_mean, L0_conv_bn_var)
    x = _L1_conv_ref(x, L1_conv_w_branch, L1_conv_b_branch, L1_conv_bn_gamma, L1_conv_bn_beta, L1_conv_w_att1, L1_conv_b_att1, L1_conv_w_att2, L1_conv_b_att2, L1_conv_w_fuse, L1_conv_b_fuse, L1_conv_ln_gamma, L1_conv_ln_beta)
    return x


_drawn_inputs = setup_inputs


def setup_inputs(seed=0):
    import zlib

    import numpy as np

    out = dict(_drawn_inputs(seed))
    spreads = {'L0_conv_bn_gamma': (1.0, 0.6),
     'L0_conv_bn_beta': (0.0, 0.1),
     'L0_conv_bn_mean': (0.0, 0.1),
     'L0_conv_bn_var': (1.0, 0.6),
     'L1_conv_b_branch': (0.0, 0.316),
     'L1_conv_bn_gamma': (1.0, 0.2),
     'L1_conv_bn_beta': (0.0, 0.294),
     'L1_conv_b_att1': (0.0, 0.8),
     'L1_conv_b_att2': (0.0, 0.351),
     'L1_conv_b_fuse': (0.0, 0.1),
     'L1_conv_ln_gamma': (1.0, 0.2),
     'L1_conv_ln_beta': (0.0, 0.1)}
    factors = {'L0_conv_wq': 8.0,
     'L0_conv_wk': 8.0,
     'L0_conv_wv': 8.0,
     'L0_conv_dw_kernel': 8.0,
     'L0_conv_pw_kernel': 8.0,
     'L0_conv_proj_kernel': 7.323,
     'L1_conv_w_att1': 4.003,
     'L1_conv_w_att2': 3.55}
    for name, (base, spread) in spreads.items():
        noise = np.random.default_rng([zlib.crc32(name.encode()), seed]).standard_normal(out[name].shape)
        drawn = base * np.exp(spread * noise) if base else spread * noise
        out[name] = jnp.asarray(drawn.astype(out[name].dtype))
    for name, factor in factors.items():
        out[name] = (out[name] * factor).astype(out[name].dtype)
    return out
```

```python
from contextlib import ExitStack

import concourse.bass as bass
from concourse import mybir

F32 = mybir.dt.float32
ALU = mybir.AluOpType
ACT = mybir.ActivationFunctionType
AX_X = mybir.AxisListType.X

P = 128
B, C, H, W = 4, 512, 64, 64
N = H * W
KT = C // P
HD = 8
HEADS = C // HD
HS = 4
SH = HEADS // HS
CH = 512
NCH = N // CH
CR = CH // W
KS = 5
HALO = KS // 2
SR = P // HD
OR = SR - 2 * HALO
NS = -(-H // OR)
LAST = H - (NS - 1) * OR
WP = W + 2 * HALO
SROW = NS * WP
NPAIR = NS // 2
TURNS = NPAIR * OR // 4
M = HD * OR
GT = KS * OR + HD
NG = 3 * HEADS
IT = B * HS
TILES = 2 * HS
EPS_ATT, EPS_BN, EPS_LN, EPS_GRAD = 1e-15, 1e-5, 1e-6, 1e-8
NE = 4
H2, W2 = H + 2, W + 2
HID = C // 8
START = 1
VEC = ["bn0_gamma", "bn0_beta", "bn0_mean", "bn0_var", "b_branch", "bn1_gamma", "bn1_beta",
       "b_att2", "b_fuse", "ln_gamma", "ln_beta"]


def prepare(nc, banks, io, dram):
    with ExitStack() as ctx:
        def sb(name, shape):
            return ctx.enter_context(nc.sbuf_tensor(name, shape, F32))

        def sem(name):
            return ctx.enter_context(nc.semaphore(name))

        dw_sb = sb("dw_sb", [HD * KS, NG * KS])
        pw_sb = sb("pw_sb", [HD, NG * HD])
        sel_sb = sb("sel_sb", [HD * KS, OR, P])
        rep_sb = sb("rep_sb", [HD, P])
        taps_sb = sb("taps_sb", [P, NG, GT])
        zeros = sb("zeros", [P, 10 * WP])
        loaded = sem("prep_loaded")
        zeroed = sem("prep_zeroed")
        product = sem("prep_product")
        copied = sem("prep_copied")
        stored = sem("prep_stored")
        HG = NG // 2
        sels = [(o, h) for o in range(OR) for h in range(2)]
        NP = len(sels)
        PC = NG * HD // 3

        with nc.Block() as block:
            @block.sync
            def _(sp):
                sp.dma_start(dw_sb[:, :], io["dwT"]).then_inc(loaded, 16)
                sp.dma_start(pw_sb[:, :], io["pwT"]).then_inc(loaded, 16)
                sp.dma_start(sel_sb[:, :, :], io["tap_sel"].rearrange("k (o p) -> k o p", o=OR)).then_inc(loaded, 16)
                sp.dma_start(rep_sb[:, :], io["row_rep"]).then_inc(loaded, 16)
                sp.wait_ge(zeroed, 1)
                for t in (0,):
                    strips = dram["strips"][t]
                    sp.dma_start(strips[:, 0:HALO, 0:WP],
                                 zeros[:, 0:HALO * WP].rearrange("p (r w) -> p r w", w=WP)).then_inc(stored, 16)
                    sp.dma_start(strips[:, LAST + HALO:SR, (NS - 1) * WP:SROW],
                                 zeros[:, 0:(SR - LAST - HALO) * WP].rearrange("p (r w) -> p r w", w=WP)).then_inc(stored, 16)
                for b in range(B):
                    for row in (0, H2 - 1):
                        sp.dma_start(dram["x2"][b].rearrange("m p n -> p m n")[:, :, row * W2:(row + 1) * W2],
                                     zeros[:, 0:KT * W2].rearrange("p (m w) -> p m w", w=W2)).then_inc(stored, 16)
                sp.wait_ge(copied, NP + 3)
                for hs in range(HS):
                    sp.dma_start(dram["taps"][hs],
                                 taps_sb[:, hs * 3 * SH:(hs + 1) * 3 * SH, :].rearrange("p g t -> p (g t)")).then_inc(stored, 16)
                sp.wait_ge(stored, 16 * (2 + 2 * B + HS))

            @block.tensor
            def _(pe):
                pe.wait_ge(loaded, 64)
                for n, (o, h) in enumerate(sels):
                    if n >= 8:
                        pe.wait_ge(copied, n - 7)
                    nc.tensor.matmul(banks[n % 8][:, 0:HG * KS], sel_sb[:, o, :],
                                     dw_sb[:, h * HG * KS:(h + 1) * HG * KS], start=True, stop=True).then_inc(product, 1)
                for n in range(3):
                    pe.wait_ge(copied, NP + n - 7)
                    nc.tensor.matmul(banks[(NP + n) % 8][:, 0:PC], rep_sb[:, :],
                                     pw_sb[:, n * PC:(n + 1) * PC], start=True, stop=True).then_inc(product, 1)

            @block.vector
            def _(dve):
                nc.vector.memset(zeros[:, :], 0.0).then_inc(zeroed, 1)
                for n, (o, h) in enumerate(sels):
                    dve.wait_ge(product, n + 1)
                    nc.vector.tensor_copy(
                        taps_sb[:, h * HG:(h + 1) * HG, o:o + KS * OR - OR + 1:OR],
                        banks[n % 8][:, 0:HG * KS].rearrange("p (g d) -> p g d", d=KS)).then_inc(copied, 1)
                for n in range(3):
                    dve.wait_ge(product, NP + n + 1)
                    nc.vector.tensor_copy(
                        taps_sb[:, n * NG // 3:(n + 1) * NG // 3, KS * OR:GT],
                        banks[(NP + n) % 8][:, 0:PC].rearrange("p (g o) -> p g o", o=HD)).then_inc(copied, 1)


def attention(nc, banks, io, dram):
    with ExitStack() as ctx:
        def sb(name, shape):
            return ctx.enter_context(nc.sbuf_tensor(name, shape, F32))

        def sem(name):
            return ctx.enter_context(nc.semaphore(name))

        XR = 2
        x_sb = sb("x_sb", [P, XR, KT, CH])
        w_sb = sb("w_sb", [P, KT, 3, P])
        taps = sb("taps", [P, 3 * SH, GT])
        q_rows = sb("q_rows", [P, H, WP])
        kv_rows = {t: sb(f"{n}_rows", [P, SR, NPAIR, WP, 2]) for t, n in ((1, "k"), (2, "v"))}
        relu_q = sb("relu_q", [P, H, W])
        key_t = sb("key_t", [P, 2, 4, P])
        value_t = sb("value_t", [P, 2, 4, P + 1])
        ckey_t = sb("ckey_t", [P, NPAIR * OR, P])
        cvalue_t = sb("cvalue_t", [P, NPAIR * OR, P + 1])
        strips = sb("strips", [P, 2, 3, SROW])
        toeplitz = sb("toeplitz", [P, 2, 3, KS * M])
        q_stage = sb("q_stage", [M, 2, NS * W])
        score_n = sb("score_n", [P, 2, P])
        score_d = sb("score_d", [P, 2, P])
        key_sum = sb("key_sum", [P, 1])
        den_sb = sb("den_sb", [P, CH])
        out_sb = sb("out_sb", [P, CH])
        ident = sb("ident", [P, P])
        mask = sb("mask", [P, P])
        first_strip = sb("first_strip", [P, 1])

        const_loaded = sem("att_const_loaded")
        cleared = sem("att_cleared")
        x_loaded = [sem(f"x_loaded{i}") for i in range(XR)]
        w_loaded = sem("w_loaded")
        taps_loaded = sem("taps_loaded")
        qkv_ready = sem("qkv_ready")
        evac = [sem(f"{n}_evacuated") for n in "qkv"]
        relu_q_ready = sem("relu_q_ready")
        strips_written = [sem(f"{n}_strips_written") for n in "qkv"]
        turned = sem("turned")
        key_t_ready = sem("key_t_ready")
        value_t_ready = sem("value_t_ready")
        chunk_scored = sem("chunk_scored")
        scores_ready = sem("scores_ready")
        key_sum_ready = sem("key_sum_ready")
        scores_masked = sem("scores_masked")
        attended = sem("attended")
        den_evac = sem("den_evac")
        inverted = sem("inverted")
        divided = sem("divided")
        out_written = sem("out_written")
        strips_loaded = [sem(f"strips_loaded{i}") for i in range(2)]
        head_done = [sem(f"head_done{i}") for i in range(2)]
        toeplitz_ready = sem("toeplitz_ready")
        cready = [sem(f"conv_{n}_ready") for n in "qk"]
        cevac = [sem(f"conv_{n}_evacuated") for n in "qkv"]
        q_written = [sem(f"q_written{i}") for i in range(2)]
        conv_q_loaded = sem("conv_q_loaded")

        T_Q, T_K, T_V = range(3)
        FIRST_TURN = 3
        WRITES = NS
        KEY_BANK, VALUE_BANK, SCORE_BANK = banks[3], banks[4], banks[5]
        NUM_BANK, DEN_BANK = banks[6], banks[7]

        def at(it, half, j):
            return 2 * NCH * it + NCH * half + j

        def pairs(eng, first, steady, final):
            first()
            with eng.Fori(0, IT - 1) as it:
                steady(it)
            final(IT - 1)

        def rows_of(s):
            r0, r1 = max(OR * s - HALO, 0), min(OR * s - HALO + SR, H)
            return r0, r1, r0 - (OR * s - HALO)

        def last_chunk(s):
            return (rows_of(s)[1] - 1) // CR

        def turn_chunk(g):
            return min(2 * OR * (4 * g // OR) + 2 * OR - 1, H - 1) // CR

        def pieces(j):
            for s in range(NS):
                r0, r1, i0 = rows_of(s)
                a, z = max(r0, CR * j), min(r1, CR * (j + 1))
                if a < z:
                    yield a - CR * j, z - a, i0 + a - r0, s // 2, s % 2

        def spread(engine_op, j, t):
            bank = banks[t][:, :].rearrange("p (r w) -> p r w", w=W)
            for r, n, i, pair, half in pieces(j):
                last = engine_op(kv_rows[t][:, i:i + n, pair, HALO:HALO + W, half], bank[:, r:r + n, :])
            return last

        with nc.Block() as block:
            @block.sync
            def _(sp):
                def load_x(it, j):
                    sp.dma_start(x_sb[:, j % XR, :, :],
                                 io["x"][it // HS].rearrange("(k p) n -> p k n", p=P)[:, :, j * CH:(j + 1) * CH]
                                 ).then_inc(x_loaded[j % XR], 16)

                def load_weights(it):
                    sp.dma_start(w_sb[:, :, :, :].rearrange("p k t m -> p (k t m)"), io["wT"][it % HS]).then_inc(w_loaded, 16)

                def load_taps(it):
                    sp.dma_start(taps[:, :, :].rearrange("p g t -> p (g t)"), dram["taps"][it % HS]).then_inc(taps_loaded, 16)

                def write_strip(it, s):
                    r0, r1, i0 = rows_of(s)
                    sp.wait_ge(evac[T_Q], NCH * it + last_chunk(s) + 1)
                    sp.dma_start(dram["strips"][T_Q][:, i0:i0 + r1 - r0, s * WP:(s + 1) * WP],
                                 q_rows[:, r0:r1, :]).then_inc(strips_written[T_Q], 16)

                def write_pair(it, pair):
                    for t in (T_K, T_V):
                        sp.wait_ge(evac[t], NCH * it + last_chunk(2 * pair + 1) + 1)
                        for i in (0, SR // 2):
                            sp.dma_start(dram["strips"][t][:, i:i + SR // 2, 2 * pair * WP:2 * (pair + 1) * WP],
                                         kv_rows[t][:, i:i + SR // 2, pair, :, :].rearrange("p i w h -> p i (w h)")
                                         ).then_inc(strips_written[t], 16)

                def load_strips(it, jj, par):
                    src = dram["strips"].rearrange("t (j i) r s -> j t (i r) s", i=HD)[2 * jj + par]
                    sp.dma_start(strips[:, par, :, :], src.rearrange("t p s -> p t s")).then_inc(strips_loaded[par], 16)

                def write_q(it, jj, par):
                    sp.wait_ge(cevac[T_Q], START + SH * it + 2 * jj + par + 1)
                    sp.dma_start(dram["conv_q"][2 * jj + par], q_stage[:, par, :]).then_inc(q_written[par], 16)

                def spill(it, half, j):
                    sp.wait_ge(divided, START + at(it, half, j) + 1)
                    sp.dma_start(dram["att"][it // HS][it % HS + HS * half][:, bass.ds(j * CH, CH)],
                                 out_sb[:, :]).then_inc(out_written, 16)

                def plain(it, conv_of):
                    for kind, n in [("x", 2), ("x", 3), ("x", 4), ("s", 0), ("x", 5), ("s", 1), ("p", 0), ("x", 6), ("s", 2),
                                    ("x", 7), ("s", 3), ("p", 1), ("s", 4), ("s", 5), ("p", 2)]:
                        if kind == "x":
                            sp.wait_ge(qkv_ready, 3 * (NCH * it + n - XR + 1))
                            load_x(it, n)
                            if conv_of is not None:
                                spill(conv_of, 1, n - XR)
                        elif kind == "s":
                            write_strip(it, n)
                        else:
                            write_pair(it, n)
                    if conv_of is not None:
                        for j in range(NCH - XR, NCH):
                            spill(conv_of, 1, j)
                    for t in range(3):
                        sp.wait_ge(strips_written[t], 16 * WRITES * (it + 1))
                    for par in range(2):
                        load_strips(it, 0, par)

                def load_next(it):
                    sp.wait_ge(qkv_ready, 3 * NCH * it)
                    load_weights(it)
                    for j in range(XR):
                        load_x(it, j)

                def conv(it, last):
                    with sp.Fori(0, SH // 2 - 1) as jj:
                        for par in range(2):
                            write_q(it, jj, par)
                            sp.wait_ge(head_done[par], START + SH // 2 * it + jj + 1)
                            load_strips(it, jj + 1, par)
                        spill(it, 0, jj)
                    for par in range(2):
                        write_q(it, SH // 2 - 1, par)
                    spill(it, 0, NCH - 1)
                    if not last:
                        sp.wait_ge(toeplitz_ready, SH * (it + 1))
                        load_taps(it + 1)
                    for par in range(2):
                        sp.wait_ge(q_written[par], 16 * START + 16 * (SH // 2) * (it + 1))
                    for s in range(NS):
                        rows = OR if s < NS - 1 else LAST
                        sp.dma_start(relu_q[:, OR * s:OR * s + rows, :],
                                     dram["conv_q"].rearrange("j (o r) s -> (j o) r s", o=HD)[:, 0:rows, s * W:(s + 1) * W]
                                     ).then_inc(conv_q_loaded, 16)

                def first():
                    for s in [out_written] + q_written:
                        sp.sem_inc(s, 16 * START)
                    sp.dma_start(ident[:, :], io["ident"]).then_inc(const_loaded, 16)
                    sp.dma_start(mask[:, :], io["head_mask"]).then_inc(const_loaded, 16)
                    sp.dma_start(first_strip[:, :], io["first_strip"]).then_inc(const_loaded, 16)
                    load_weights(0)
                    load_taps(0)
                    for j in range(XR):
                        load_x(0, j)
                    plain(0, None)

                def steady(it):
                    load_next(it + 1)
                    conv(it, False)
                    plain(it + 1, it)

                def final(it):
                    conv(it, True)
                    for j in range(NCH):
                        spill(it, 1, j)
                    sp.wait_ge(out_written, 16 * START + 16 * at(IT, 0, 0))

                pairs(sp, first, steady, final)

            @block.tensor
            def _(pe):
                def qkv(it, j):
                    pe.wait_ge(x_loaded[j % XR], 16 * (NCH // XR) * it + 16 * (j // XR + 1))
                    for t in range(3):
                        pe.wait_ge(evac[t], NCH * it + j)
                        for k in range(KT):
                            last = nc.tensor.matmul(banks[t][:, :], w_sb[:, k, t, :], x_sb[:, j % XR, k, :],
                                                    start=(k == 0), stop=(k == KT - 1))
                        last.then_inc(qkv_ready, 1)

                def turn(it, g):
                    for t in (T_K, T_V):
                        pe.wait_ge(evac[t], NCH * it + turn_chunk(g) + 1)
                    pe.wait_ge(key_t_ready, TURNS * it + g)
                    pe.wait_ge(value_t_ready, TURNS * it + g)
                    for t, bank in ((T_K, KEY_BANK), (T_V, VALUE_BANK)):
                        for n in range(4):
                            pair, r = divmod(4 * g + n, OR)
                            rows = kv_rows[t][:, HALO + r, pair, HALO:HALO + W, :].rearrange("p w h -> p (w h)")
                            last = nc.tensor.matmul(bank[:, n * P:(n + 1) * P], rows, ident[:, :],
                                                    start=True, stop=True, is_transpose=True)
                    last.then_inc(turned, 1)

                def score(it, g):
                    pe.wait_ge(key_t_ready, TURNS * it + g + 1)
                    pe.wait_ge(value_t_ready, TURNS * it + g + 1)
                    for n in range(4):
                        last = nc.tensor.matmul(SCORE_BANK[:, 0:P + 1], key_t[:, g % 2, n, :], value_t[:, g % 2, n, :],
                                                start=(g == 0 and n == 0), stop=(g == TURNS - 1 and n == 3))
                    last.then_inc(chunk_scored, 1)

                def attend(it, half, j):
                    pe.wait_ge(scores_masked, 2 * it + half + 1)
                    if half == 0:
                        pe.wait_ge(relu_q_ready, NCH * it + j + 1)
                    else:
                        pe.wait_ge(conv_q_loaded, 16 * NS * (it + 1))
                    pe.wait_ge(den_evac, START + at(it, half, j))
                    pe.wait_ge(divided, START + at(it, half, j))
                    q = relu_q[:, bass.ds(j * CR, CR), :]
                    nc.tensor.matmul(DEN_BANK[:, :], score_d[:, half, :], q, start=True, stop=True)
                    nc.tensor.matmul(NUM_BANK[:, :], score_n[:, half, :], q, start=True, stop=True).then_inc(attended, 1)

                def plain(it, conv_of):
                    pe.wait_ge(w_loaded, 16 * (it + 1))
                    for step in range(FIRST_TURN + TURNS + 1):
                        if step < NCH:
                            qkv(it, step)
                            if conv_of is not None:
                                attend(conv_of, 1, step)
                        if 0 <= step - FIRST_TURN < TURNS:
                            turn(it, step - FIRST_TURN)
                        if 0 <= step - FIRST_TURN - 1:
                            score(it, step - FIRST_TURN - 1)

                def conv(it):
                    with pe.Fori(0, SH // 2) as jj:
                        attend(it, 0, jj)
                        for par in range(2):
                            pe.wait_ge(strips_loaded[par], SH // 2 * 16 * it + 16 * jj + 16)
                            pe.wait_ge(toeplitz_ready, SH * it + 2 * jj + par + 1)
                            x_q = strips[:, par, T_Q, :].rearrange("p (s w) -> p s w", w=WP)
                            x = strips[:, par, :, :].rearrange("p t (s n) -> p t s n", s=NPAIR)
                            w = toeplitz[:, par, :, :].rearrange("p t (d m) -> p t d m", m=M)
                            pe.wait_ge(cevac[T_Q], START + SH * it + 2 * jj + par)
                            for d in range(KS):
                                last = nc.tensor.matmul(banks[T_Q][0:M, 0:NS * W], w[:, T_Q, d, :], x_q[:, :, d:d + W],
                                                        start=(d == 0), stop=(d == KS - 1))
                            last.then_inc(cready[T_Q], 1)
                            for t in (T_K, T_V):
                                pe.wait_ge(cevac[t], START + SH * it + 2 * jj + par)
                                for s in range(NPAIR):
                                    for d in range(KS):
                                        last = nc.tensor.matmul(banks[t][:, s * M:(s + 1) * M],
                                                                x[:, t, s, 2 * d:2 * (d + W)], w[:, t, d, :],
                                                                start=(d == 0), stop=(d == KS - 1))
                                last.then_inc(cready[t] if t == T_K else head_done[par], 1)
                    pe.wait_ge(cevac[T_K], START + SH * (it + 1))
                    pe.wait_ge(cevac[T_V], START + SH * (it + 1))
                    for n in range(NPAIR * OR):
                        last = nc.tensor.matmul(SCORE_BANK[:, 0:P + 1], ckey_t[:, n, :], cvalue_t[:, n, :],
                                                start=(n == 0), stop=(n == NPAIR * OR - 1))
                    last.then_inc(scores_ready, 1)

                def first():
                    for s in head_done:
                        pe.sem_inc(s, START)
                    pe.wait_ge(const_loaded, 48)
                    pe.wait_ge(cleared, 1)
                    plain(0, None)

                def steady(it):
                    conv(it)
                    plain(it + 1, it)

                def final(it):
                    conv(it)
                    for j in range(NCH):
                        attend(it, 1, j)

                pairs(pe, first, steady, final)

            @block.scalar
            def _(act):
                def copy(to, source):
                    return nc.scalar.activation(to, source, ACT.Copy)

                def evacuate(it, j):
                    act.wait_ge(qkv_ready, 3 * NCH * it + 3 * j + T_Q + 1)
                    copy(q_rows[:, CR * j:CR * (j + 1), HALO:HALO + W],
                         banks[T_Q][:, :].rearrange("p (r w) -> p r w", w=W)).then_inc(evac[T_Q], 1)
                    act.wait_ge(qkv_ready, 3 * NCH * it + 3 * j + T_K + 1)
                    spread(copy, j, T_K).then_inc(evac[T_K], 1)

                def value_by_position(it, g):
                    act.wait_ge(turned, TURNS * it + g + 1)
                    act.wait_ge(chunk_scored, TURNS * it + max(g - 1, 0))
                    nc.scalar.activation(value_t[:, g % 2, :, 0:P], VALUE_BANK[:, :].rearrange("p (n m) -> p n m", m=P),
                                         ACT.Copy).then_inc(value_t_ready, 1)

                def denominators(it, half, j):
                    act.wait_ge(attended, at(it, half, j) + 1)
                    act.wait_ge(divided, START + at(it, half, j))
                    nc.scalar.activation(den_sb[:, :], DEN_BANK[:, :], ACT.Copy, bias=EPS_ATT).then_inc(den_evac, 1)

                def plain(it, conv_of):
                    for t in (T_Q, T_K):
                        act.wait_ge(strips_written[t], 16 * WRITES * it)
                    for step in range(FIRST_TURN + TURNS):
                        if step < NCH:
                            evacuate(it, step)
                            if conv_of is not None:
                                denominators(conv_of, 1, step)
                        if step >= FIRST_TURN:
                            value_by_position(it, step - FIRST_TURN)

                def conv(it):
                    with act.Fori(0, SH // 2) as jj:
                        denominators(it, 0, jj)
                        for par in range(2):
                            act.wait_ge(cready[T_Q], SH * it + 2 * jj + par + 1)
                            act.wait_ge(q_written[par], 16 * START + SH // 2 * 16 * it + 16 * jj)
                            nc.scalar.activation(q_stage[:, par, :], banks[T_Q][0:M, 0:NS * W], ACT.Relu).then_inc(cevac[T_Q], 1)
                            act.wait_ge(head_done[par], START + SH // 2 * it + jj + 1)
                            to = cvalue_t[:, :, bass.ds((2 * jj + par) * HD, HD)].rearrange("p (s r) o -> p s r o", s=NPAIR)
                            nc.scalar.activation(to, banks[T_V][:, 0:NPAIR * M].rearrange("p (s o r) -> p s r o", o=HD, r=OR),
                                                 ACT.Copy).then_inc(cevac[T_V], 1)

                def first():
                    for s in (cevac[T_Q], cevac[T_V], den_evac):
                        act.sem_inc(s, START)
                    act.wait_ge(cleared, 1)
                    plain(0, None)

                def steady(it):
                    conv(it)
                    plain(it + 1, it)

                def final(it):
                    conv(it)
                    for j in range(NCH):
                        denominators(it, 1, j)

                pairs(act, first, steady, final)

            @block.vector
            def _(dve):
                def keys_by_position(it, g):
                    dve.wait_ge(turned, TURNS * it + g + 1)
                    dve.wait_ge(chunk_scored, TURNS * it + max(g - 1, 0))
                    nc.vector.tensor_scalar(key_t[:, g % 2, :, :].rearrange("p n m -> p (n m)"), KEY_BANK[:, :],
                                            0.0, None, ALU.max).then_inc(key_t_ready, 1)

                def mask_scores(it, half):
                    if half:
                        dve.wait_ge(scores_ready, it + 1)
                    else:
                        dve.wait_ge(chunk_scored, TURNS * (it + 1))
                    nc.vector.tensor_copy(key_sum[:, :], SCORE_BANK[:, P:P + 1]).then_inc(key_sum_ready, 1)
                    nc.vector.tensor_tensor(score_n[:, half, :], SCORE_BANK[:, 0:P], mask[:, :], ALU.mult)
                    dve.wait_ge(key_sum_ready, 2 * it + half + 1)
                    nc.vector.tensor_scalar(score_d[:, half, :], mask[:, :], key_sum[:, 0:1], None,
                                            ALU.mult).then_inc(scores_masked, 1)

                def divide(it, half, j):
                    dve.wait_ge(den_evac, START + at(it, half, j) + 1)
                    nc.vector.reciprocal(den_sb[:, :], den_sb[:, :]).then_inc(inverted, 1)
                    dve.wait_ge(inverted, at(it, half, j) + 1)
                    dve.wait_ge(out_written, 16 * START + 16 * at(it, half, j))
                    nc.vector.tensor_tensor(out_sb[:, :], NUM_BANK[:, :], den_sb[:, :], ALU.mult).then_inc(divided, 1)

                def plain(it, conv_of):
                    dve.wait_ge(strips_written[T_V], 16 * WRITES * it)
                    for step in range(FIRST_TURN + TURNS):
                        if step < NCH:
                            dve.wait_ge(qkv_ready, 3 * NCH * it + 3 * step + T_V + 1)
                            spread(nc.vector.tensor_copy, step, T_V).then_inc(evac[T_V], 1)
                        if step >= FIRST_TURN:
                            keys_by_position(it, step - FIRST_TURN)
                        if step < NCH:
                            if conv_of is not None:
                                divide(conv_of, 1, step)
                            dve.wait_ge(evac[T_Q], NCH * it + step + 1)
                            nc.vector.tensor_scalar(relu_q[:, CR * step:CR * (step + 1), :],
                                                    q_rows[:, CR * step:CR * (step + 1), HALO:HALO + W],
                                                    0.0, None, ALU.max).then_inc(relu_q_ready, 1)
                    mask_scores(it, 0)

                def conv(it):
                    with dve.Fori(0, SH // 2) as jj:
                        divide(it, 0, jj)
                        for par in range(2):
                            dve.wait_ge(cready[T_K], SH * it + 2 * jj + par + 1)
                            to = ckey_t[:, :, bass.ds((2 * jj + par) * HD, HD)].rearrange("p (s r) o -> p s r o", s=NPAIR)
                            of = banks[T_K][:, 0:NPAIR * M].rearrange("p (s o r) -> p s r o", o=HD, r=OR)
                            nc.vector.tensor_scalar(to[:, 0:NPAIR - 1, :, :], of[:, 0:NPAIR - 1, :, :], 0.0, None, ALU.max)
                            nc.vector.tensor_scalar(to[:, NPAIR - 1, 0:LAST, :], of[:, NPAIR - 1, 0:LAST, :], 0.0, None, ALU.max)
                            nc.vector.tensor_scalar(to[:, NPAIR - 1, LAST:OR, :], of[:, NPAIR - 1, LAST:OR, :], 0.0,
                                                    first_strip[:, 0:1], ALU.max, ALU.mult).then_inc(cevac[T_K], 1)
                    mask_scores(it, 1)

                def first():
                    for s in (cevac[T_K], divided):
                        dve.sem_inc(s, START)
                    nc.vector.memset(q_rows[:, :, 0:HALO], 0.0)
                    nc.vector.memset(q_rows[:, :, HALO + W:WP], 0.0)
                    for t in (T_K, T_V):
                        nc.vector.memset(kv_rows[t][:, :, :, :, :].rearrange("p i s w h -> p (i s w h)"), 0.0)
                    nc.vector.memset(value_t[:, :, :, P:P + 1], 1.0)
                    nc.vector.memset(cvalue_t[:, :, P:P + 1], 1.0).then_inc(cleared, 1)
                    dve.wait_ge(cleared, 1)
                    dve.wait_ge(const_loaded, 48)
                    plain(0, None)

                def steady(it):
                    conv(it)
                    plain(it + 1, it)

                def final(it):
                    conv(it)
                    for j in range(NCH):
                        divide(it, 1, j)

                pairs(dve, first, steady, final)

            @block.gpsimd
            def _(pool):
                with pool.Fori(0, IT) as it:
                    with pool.Fori(0, SH // 2) as jj:
                        for par in range(2):
                            pool.wait_ge(taps_loaded, 16 * (it + 1))
                            pool.wait_ge(head_done[par], START + SH // 2 * it + jj)
                            for t in range(3):
                                g = taps[:, :, :].rearrange("p (j t) n -> p j t n", t=3)[:, 2 * jj + par, t, :]
                                tap = g[:, 0:KS * OR].rearrange("p (d r) -> p d r", r=OR)[:, :, None, :].to_broadcast([P, KS, HD, OR])
                                point = g[:, KS * OR:GT][:, None, :, None].to_broadcast([P, KS, HD, OR])
                                last = nc.gpsimd.tensor_tensor(
                                    toeplitz[:, par, t, :].rearrange("p (d o r) -> p d o r", o=HD, r=OR), tap, point, ALU.mult)
                            last.then_inc(toeplitz_ready, 1)


def project(nc, banks, io, dram):
    with ExitStack() as ctx:
        def sb(name, shape):
            return ctx.enter_context(nc.sbuf_tensor(name, shape, F32))

        def sem(name):
            return ctx.enter_context(nc.semaphore(name))

        w_sb = sb("proj_w", [P, TILES, C])
        att = sb("proj_att", [P, 2, TILES, CH])
        x_sb = sb("proj_x", [P, 2, KT, CH])
        x2_sb = sb("proj_x2", [P, 2, KT, CR * W2])
        vec = sb("proj_vec", [P, len(VEC), KT])
        scale = sb("proj_scale", [P, KT])
        root = sb("proj_root", [P, KT])
        shift = sb("proj_shift", [P, KT])
        eps = sb("proj_eps", [P, 1])
        const_loaded = sem("proj_const_loaded")
        set_up = sem("proj_set_up")
        rooted = sem("proj_rooted")
        scaled = sem("proj_scaled")
        att_loaded = [sem(f"att_loaded{i}") for i in range(2)]
        res_loaded = [sem(f"res_loaded{i}") for i in range(2)]
        projected = sem("projected")
        shifted = sem("shifted")
        summed = [[sem(f"summed{par}{m}") for m in range(KT)] for par in range(2)]
        x2_written = [sem(f"x2_written{i}") for i in range(2)]
        CHUNKS = B * NCH

        def v(name):
            return vec[:, VEC.index(name), :]

        with nc.Block() as block:
            @block.sync
            def _(sp):
                for s in x2_written:
                    sp.sem_inc(s, 16 * START)
                sp.dma_start(w_sb[:, :, :].rearrange("p t o -> p (t o)"), io["projT"]).then_inc(const_loaded, 16)
                sp.dma_start(vec[:, :, :].rearrange("p v m -> p (v m)"), io["vec"]).then_inc(const_loaded, 16)

                def load(i, par):
                    c = 2 * i + par
                    n = (c % NCH) * CH
                    sp.dma_start(att[:, par, :, :], dram["att"][c // NCH].rearrange("t p n -> p t n")[:, :, bass.ds(n, CH)]
                                 ).then_inc(att_loaded[par], 16)
                    sp.dma_start(x_sb[:, par, :, :], io["x"][c // NCH].rearrange("(k p) n -> p k n", p=P)[:, :, bass.ds(n, CH)]
                                 ).then_inc(res_loaded[par], 16)

                def store(i, par):
                    c = 2 * i + par
                    n = (c % NCH) * (CR * W2) + W2
                    for m in range(KT):
                        sp.wait_ge(summed[par][m], START + i + 1)
                    sp.dma_start(dram["x2"][c // NCH].rearrange("m p n -> p m n")[:, :, bass.ds(n, CR * W2)],
                                 x2_sb[:, par, :, :]).then_inc(x2_written[par], 16)

                for par in range(2):
                    load(0, par)
                with sp.Fori(0, CHUNKS // 2 - 1) as i:
                    for par in range(2):
                        store(i, par)
                        load(i + 1, par)
                for par in range(2):
                    store(CHUNKS // 2 - 1, par)
                for par in range(2):
                    sp.wait_ge(x2_written[par], 16 * START + 16 * CHUNKS // 2)

            @block.tensor
            def _(pe):
                pe.wait_ge(const_loaded, 32)
                with pe.Fori(0, CHUNKS // 2) as i:
                    for par in range(2):
                        pe.wait_ge(att_loaded[par], 16 * i + 16)
                        for m in range(KT):
                            pe.wait_ge(summed[par][m], START + i)
                            for k in range(TILES):
                                last = nc.tensor.matmul(banks[KT * par + m][:, :], w_sb[:, k, m * P:(m + 1) * P],
                                                        att[:, par, k, :], start=(k == 0), stop=(k == TILES - 1))
                            last.then_inc(projected, 1)

            @block.scalar
            def _(act):
                act.wait_ge(set_up, 1)
                nc.scalar.activation(root[:, :], v("bn0_var"), ACT.Sqrt, bias=eps[:, 0:1]).then_inc(rooted, 1)
                act.wait_ge(scaled, 3)
                with act.Fori(0, CHUNKS // 2) as i:
                    for par in range(2):
                        act.wait_ge(res_loaded[par], 16 * i + 16)
                        for m in range(KT):
                            nc.scalar.activation(x_sb[:, par, m, :], x_sb[:, par, m, :], ACT.Identity,
                                                 bias=shift[:, m:m + 1]).then_inc(shifted, 1)

            @block.vector
            def _(dve):
                for s in summed[0] + summed[1]:
                    dve.sem_inc(s, START)
                nc.vector.memset(x2_sb[:, :, :, :].rearrange("p a m n -> p (a m n)"), 0.0)
                nc.vector.memset(eps[:, :], EPS_BN)
                dve.wait_ge(const_loaded, 32)
                nc.vector.tensor_copy(shift[:, :], v("bn0_mean")).then_inc(set_up, 1)
                dve.wait_ge(rooted, 1)
                nc.vector.reciprocal(scale[:, :], root[:, :]).then_inc(scaled, 1)
                dve.wait_ge(scaled, 1)
                nc.vector.tensor_tensor(scale[:, :], scale[:, :], v("bn0_gamma"), ALU.mult).then_inc(scaled, 1)
                dve.wait_ge(scaled, 2)
                nc.vector.tensor_tensor(root[:, :], scale[:, :], shift[:, :], ALU.mult).then_inc(rooted, 1)
                dve.wait_ge(rooted, 2)
                nc.vector.tensor_tensor(shift[:, :], v("bn0_beta"), root[:, :], ALU.subtract).then_inc(scaled, 1)
                with dve.Fori(0, CHUNKS // 2) as i:
                    for par in range(2):
                        dve.wait_ge(x2_written[par], 16 * START + 16 * i)
                        for m in range(KT):
                            c = KT * 2 * i + KT * par + m
                            dve.wait_ge(shifted, c + 1)
                            dve.wait_ge(projected, c + 1)
                            nc.vector.scalar_tensor_tensor(
                                out=x2_sb[:, par, m, :].rearrange("p (r w) -> p r w", w=W2)[:, :, 1:W + 1],
                                in0=banks[KT * par + m][:, :].rearrange("p (r w) -> p r w", w=W), scalar=scale[:, m:m + 1],
                                in1=x_sb[:, par, m, :].rearrange("p (r w) -> p r w", w=W),
                                op0=ALU.mult, op1=ALU.add).then_inc(summed[par][m], 1)


def edges(nc, banks, io, dram, out):
    with ExitStack() as ctx:
        def sb(name, shape):
            return ctx.enter_context(nc.sbuf_tensor(name, shape, F32))

        def sem(name):
            return ctx.enter_context(nc.semaphore(name))

        XR = CR + 2
        feat = sb("feat", [P, NE, N])
        xb = sb("xb", [P, KT, XR * W2])
        dx = sb("dx", [P, 2, XR, W])
        side = sb("side", [P, 2, XR, W])
        smooth = sb("smooth", [P, 2, XR, W])
        sobel_h = sb("sobel_h", [P, 2, CR, W])
        sobel_v = sb("sobel_v", [P, 2, CR, W])
        lap = sb("lap", [P, 2, CR, W])
        diag = sb("diag", [P, 2, CR, W])
        lap_sq = sb("lap_sq", [P, 2, CR, W])
        edge = sb("edge", [P, 2, NE, CH])
        w_branch = sb("w_branch", [P, KT, NE, P])
        w_fuse = sb("w_fuse", [P, KT, C])
        w_image = sb("w_image", [P, KT, C])
        w_att1 = sb("w_att1", [P, KT, HID])
        w_att2 = sb("w_att2", [HID, C])
        b_att1 = sb("b_att1", [HID, 1])
        vec = sb("edge_vec", [P, len(VEC), KT])
        bn_scale = sb("bn_scale", [P, NE])
        bn_shift = sb("bn_shift", [P, NE])
        z_shift = sb("z_shift", [P, KT])
        row_sum = sb("row_sum", [P, KT])
        pool_sum = sb("pool_sum", [P, NE, NCH])
        pooled = sb("pooled", [P, NE])
        hidden = sb("hidden", [HID, 1])
        gate = sb("gate", [P, KT])
        mean_w = sb("mean_w", [P, P])
        centred = sb("centred", [P, 2, KT, CH])
        square = sb("square", [P, KT, CH])
        std = sb("std", [P, CH])
        rstd = sb("rstd", [P, CH])
        x_out = sb("x_out", [P, 2, KT, CR * W2])
        eps = sb("edge_eps", [P, 3])

        const_loaded = sem("edge_const_loaded")
        ready = sem("edge_const_ready")
        mean_ready = sem("mean_ready")
        xb_loaded = [sem(f"xb_loaded{k}") for k in range(KT)]
        xb_used = [sem(f"xb_used{k}") for k in range(KT)]
        names = ["side", "vert", "dx", "smooth", "diag", "rows", "sobel_v", "sobel_h", "cross",
                 "squares", "sum", "sum_lap", "edges"]
        done = {n: sem(f"{n}_done") for n in names}
        branched = sem("branched")
        feat_ready = sem("feat_ready")
        pool_summed = sem("pool_summed")
        pooled_ready = sem("pooled_ready")
        hidden_mm = sem("hidden_mm")
        hidden_ready = sem("hidden_ready")
        gate_mm = sem("gate_mm")
        gate_ready = sem("gate_ready")
        image_ready = sem("image_ready")
        fused = sem("fused")
        z_evac = [sem(f"z_evac{m}") for m in range(KT)]
        squared = sem("squared")
        var_ready = sem("var_ready")
        std_ready = sem("std_ready")
        rstd_ready = sem("rstd_ready")
        normed = [sem("normed_v"), sem("normed_p")]
        activated = sem("activated")
        out_ready = sem("out_ready")
        x_out_loaded = [sem(f"x_out_loaded{i}") for i in range(2)]
        stored = [sem(f"out_stored{i}") for i in range(2)]

        Z_BANKS, VAR_BANK = banks[4:8], banks[0]

        def v(name):
            return vec[:, VEC.index(name), :]

        def before(b, j, k):
            return KT * NCH * b + KT * j + max(k - 1, 0)

        with nc.Block() as block:
            @block.sync
            def _(sp):
                for s in stored:
                    sp.sem_inc(s, 16 * START)
                for dst, src in ((w_branch[:, :, :, :].rearrange("p k e o -> p (k e o)"), io["branchT"]),
                                 (w_fuse[:, :, :].rearrange("p k o -> p (k o)"), io["fuseT"]),
                                 (w_att1[:, :, :].rearrange("p k o -> p (k o)"), io["att1T"]),
                                 (w_att2[:, :], io["att2T"]), (b_att1[:, :], io["b_att1"]),
                                 (vec[:, :, :].rearrange("p v m -> p (v m)"), io["vec"])):
                    sp.dma_start(dst, src).then_inc(const_loaded, 16)

                def load_out(b, j):
                    sp.dma_start(x_out[:, j % 2, :, :],
                                 dram["x2"][b].rearrange("m p n -> p m n")[:, :, (CR * j + 1) * W2:(CR * j + 1 + CR) * W2]
                                 ).then_inc(x_out_loaded[j % 2], 16)

                with sp.Fori(0, B) as b:
                    with sp.Fori(0, NCH) as j:
                        for k in range(KT):
                            sp.wait_ge(xb_used[k], START + NCH * b + j)
                            sp.dma_start(xb[:, k, :], dram["x2"][b][k][:, bass.ds(j * (CR * W2), XR * W2)]).then_inc(xb_loaded[k], 16)
                    for j in range(NCH):
                        if j < 2:
                            sp.wait_ge(out_ready, START + KT * NCH * b)
                            load_out(b, j)
                    for j in range(NCH):
                        sp.wait_ge(out_ready, START + KT * NCH * b + KT * (j + 1))
                        sp.dma_start(out[b].rearrange("(m p) n -> p m n", p=P)[:, :, j * CH:(j + 1) * CH],
                                     centred[:, j % 2, :, :]).then_inc(stored[j % 2], 16)
                        if j + 2 < NCH:
                            load_out(b, j + 2)
                for i in range(2):
                    sp.wait_ge(stored[i], 16 * START + 16 * B * NCH // 2)

            @block.tensor
            def _(pe):
                for s in (branched, fused, var_ready):
                    pe.sem_inc(s, START)
                pe.wait_ge(ready, 2)
                for k in range(KT):
                    last = nc.tensor.matmul(banks[4][:, 0:1], mean_w[:, :], v("b_fuse")[:, k:k + 1],
                                            start=(k == 0), stop=(k == KT - 1))
                last.then_inc(mean_ready, 1)

                def fuse(b, j):
                    for m in range(KT):
                        pe.wait_ge(z_evac[m], START + NCH * b + j)
                        for k in range(KT):
                            last = nc.tensor.matmul(Z_BANKS[m][:, :], w_image[:, k, m * P:(m + 1) * P],
                                                    feat[:, k, j * CH:(j + 1) * CH], start=(k == 0), stop=(k == KT - 1))
                        last.then_inc(fused, 1)

                def variance(b, j):
                    pe.wait_ge(std_ready, START + NCH * b + j)
                    for m in range(KT):
                        pe.wait_ge(squared, KT * NCH * b + KT * j + m + 1)
                        last = nc.tensor.matmul(VAR_BANK[:, :], mean_w[:, :], square[:, m, :],
                                                start=(m == 0), stop=(m == KT - 1))
                    last.then_inc(var_ready, 1)

                with pe.Fori(0, B) as b:
                    with pe.Fori(0, NCH) as j:
                        pe.wait_ge(std_ready, START + NCH * b)
                        pe.wait_ge(feat_ready, START + NE * NCH * b + NE * j)
                        for k in range(KT):
                            pe.wait_ge(done["edges"], START + KT * NCH * b + KT * j + k + 1)
                            for e in range(NE):
                                last = nc.tensor.matmul(banks[e][:, :], w_branch[:, k, e, :], edge[:, k % 2, e, :],
                                                        start=(k == 0), stop=(k == KT - 1))
                            last.then_inc(branched, 1)
                    pe.wait_ge(pooled_ready, b + 1)
                    for k in range(KT):
                        last = nc.tensor.matmul(banks[1][0:HID, 0:1], w_att1[:, k, :], pooled[:, k:k + 1],
                                                start=(k == 0), stop=(k == KT - 1))
                    last.then_inc(hidden_mm, 1)
                    pe.wait_ge(hidden_ready, b + 1)
                    for m in range(KT):
                        last = nc.tensor.matmul(banks[2][:, m:m + 1], w_att2[:, m * P:(m + 1) * P], hidden[:, 0:1],
                                                start=True, stop=True)
                    last.then_inc(gate_mm, 1)
                    pe.wait_ge(image_ready, KT * (b + 1))
                    for j in range(NCH + 1):
                        if j < NCH:
                            fuse(b, j)
                        if j >= 1:
                            variance(b, j - 1)

            @block.scalar
            def _(act):
                for s in [done["squares"], done["edges"], feat_ready, std_ready] + z_evac:
                    act.sem_inc(s, START)
                act.wait_ge(ready, 5)

                def squares(b, j, k):
                    s = k % 2
                    n = KT * NCH * b + KT * j + k + 1
                    act.wait_ge(branched, START + before(b, j, k))
                    act.wait_ge(done["sum_lap"], START + before(b, j, k))
                    act.wait_ge(done["diag"], n)
                    nc.scalar.activation(edge[:, s, 2, :].rearrange("p (r w) -> p r w", w=W), diag[:, s, :, :], ACT.Abs)
                    act.wait_ge(done["sobel_h"], n)
                    nc.scalar.activation(sobel_h[:, s, :, :], sobel_h[:, s, :, :], ACT.Square)
                    nc.scalar.activation(sobel_v[:, s, :, :], sobel_v[:, s, :, :], ACT.Square)
                    act.wait_ge(xb_used[k], START + NCH * b + j + 1)
                    nc.scalar.activation(lap_sq[:, s, :, :], lap[:, s, :, :], ACT.Square)
                    nc.scalar.activation(edge[:, s, 1, :].rearrange("p (r w) -> p r w", w=W), lap[:, s, :, :],
                                         ACT.Abs).then_inc(done["squares"], 1)

                def roots(b, j, k):
                    s = k % 2
                    n = KT * NCH * b + KT * j + k + 1
                    act.wait_ge(done["sum"], n)
                    nc.scalar.activation(edge[:, s, 0, :].rearrange("p (r w) -> p r w", w=W), sobel_v[:, s, :, :], ACT.Sqrt,
                                         bias=eps[:, 0:1])
                    act.wait_ge(done["sum_lap"], START + n)
                    nc.scalar.activation(edge[:, s, 3, :].rearrange("p (r w) -> p r w", w=W), lap_sq[:, s, :, :], ACT.Sqrt,
                                         bias=eps[:, 1:2]).then_inc(done["edges"], 1)

                def centre(b, j):
                    act.wait_ge(stored[j % 2], 16 * START + 16 * (NCH // 2) * b + 16 * (j // 2))
                    for m in range(KT):
                        act.wait_ge(fused, START + KT * NCH * b + KT * j + m + 1)
                        if m == 0:
                            act.wait_ge(var_ready, START + NCH * b + j)
                        nc.scalar.activation(square[:, m, :], Z_BANKS[m][:, :], ACT.Square,
                                             bias=z_shift[:, m:m + 1]).then_inc(squared, 1)
                        nc.scalar.activation(centred[:, j % 2, m, :], Z_BANKS[m][:, :], ACT.Identity,
                                             bias=z_shift[:, m:m + 1]).then_inc(z_evac[m], 1)

                def finish(b, j):
                    act.wait_ge(var_ready, START + NCH * b + j + 1)
                    act.wait_ge(rstd_ready, START + NCH * b + j)
                    nc.scalar.activation(std[:, :], VAR_BANK[:, :], ACT.Sqrt, bias=eps[:, 2:3]).then_inc(std_ready, 1)
                    for m in range(KT):
                        act.wait_ge(normed[m % 2], START + KT // 2 * (NCH * b + j) + m // 2 + 1)
                        nc.scalar.activation(centred[:, j % 2, m, :], centred[:, j % 2, m, :], ACT.Gelu,
                                             scale=v("ln_gamma")[:, m:m + 1], bias=v("ln_beta")[:, m:m + 1]).then_inc(activated, 1)

                with act.Fori(0, B) as b:
                    act.wait_ge(fused, START + KT * NCH * b)
                    with act.Fori(0, NCH) as j:
                        for k in range(KT + 1):
                            if k < KT:
                                squares(b, j, k)
                            if k >= 1:
                                roots(b, j, k - 1)
                        act.wait_ge(branched, START + KT * NCH * b + KT * j + KT)
                        for e in range(NE):
                            nc.scalar.activation(feat[:, e, bass.ds(j * CH, CH)], banks[e][:, :], ACT.Gelu,
                                                 scale=bn_scale[:, e:e + 1], bias=bn_shift[:, e:e + 1],
                                                 accum_out=pool_sum[:, e, bass.ds(j, 1)]).then_inc(feat_ready, 1)
                    act.wait_ge(hidden_mm, b + 1)
                    nc.scalar.activation(hidden[:, :], banks[1][0:HID, 0:1], ACT.Gelu, bias=b_att1[:, 0:1]).then_inc(hidden_ready, 1)
                    act.wait_ge(gate_mm, b + 1)
                    for m in range(KT):
                        nc.scalar.activation(gate[:, m:m + 1], banks[2][:, m:m + 1], ACT.Sigmoid,
                                             bias=v("b_att2")[:, m:m + 1]).then_inc(gate_ready, 1)
                    for j in range(NCH + 1):
                        if j < NCH:
                            centre(b, j)
                        if j >= 1:
                            finish(b, j - 1)

            @block.vector
            def _(dve):
                for s in [done["cross"], rstd_ready, normed[0], out_ready] + xb_used:
                    dve.sem_inc(s, START)
                nc.vector.memset(mean_w[:, :], 1.0 / C).then_inc(ready, 1)
                nc.vector.memset(eps[:, 0:1], EPS_GRAD)
                nc.vector.memset(eps[:, 1:2], 2 * EPS_GRAD)
                nc.vector.memset(eps[:, 2:3], EPS_LN)
                dve.wait_ge(const_loaded, 96)
                nc.vector.tensor_scalar(bn_scale[:, :], v("bn1_gamma"), float((1.0 + EPS_BN) ** -0.5), None,
                                        ALU.mult).then_inc(ready, 1)
                dve.wait_ge(ready, 2)
                nc.vector.tensor_tensor(bn_shift[:, :], bn_scale[:, :], v("b_branch"), ALU.mult).then_inc(ready, 1)
                dve.wait_ge(ready, 3)
                nc.vector.tensor_tensor(bn_shift[:, :], bn_shift[:, :], v("bn1_beta"), ALU.add).then_inc(ready, 1)
                dve.wait_ge(mean_ready, 1)
                nc.vector.tensor_scalar(z_shift[:, :], v("b_fuse"), banks[4][:, 0:1], None, ALU.subtract).then_inc(ready, 1)
                nc.vector.tensor_reduce(row_sum[:, :], w_fuse[:, :, :], AX_X, ALU.add).then_inc(ready, 1)
                dve.wait_ge(ready, 6)
                nc.vector.tensor_scalar(row_sum[:, :], row_sum[:, :], 1.0 / C, None, ALU.mult).then_inc(ready, 1)
                dve.wait_ge(ready, 7)
                for k in range(KT):
                    nc.vector.tensor_scalar(w_fuse[:, k, :], w_fuse[:, k, :], row_sum[:, k:k + 1], None,
                                            ALU.subtract).then_inc(ready, 1)

                def stencils(b, j, k):
                    s = k % 2
                    u = KT * NCH * b + KT * j + k
                    x = xb[:, k, :].rearrange("p (r w) -> p r w", w=W2)
                    dve.wait_ge(xb_loaded[k], 16 * NCH * b + 16 * j + 16)
                    nc.vector.tensor_tensor(dx[:, s, :, :], x[:, :, 2:W2], x[:, :, 0:W], ALU.subtract).then_inc(done["dx"], 1)
                    dve.wait_ge(done["side"], u + 1)
                    nc.vector.scalar_tensor_tensor(out=smooth[:, s, :, :], in0=x[:, :, 1:W + 1], scalar=2.0, in1=side[:, s, :, :],
                                                   op0=ALU.mult, op1=ALU.add).then_inc(done["smooth"], 1)
                    dve.wait_ge(done["dx"], u + 1)
                    dve.wait_ge(done["squares"], START + before(b, j, k))
                    nc.vector.tensor_tensor(diag[:, s, :, :], dx[:, s, 2:XR, :], dx[:, s, 0:CR, :], ALU.subtract).then_inc(done["diag"], 1)
                    dve.wait_ge(done["edges"], START + before(b, j, k))
                    nc.vector.tensor_tensor(sobel_h[:, s, :, :], dx[:, s, 2:XR, :], dx[:, s, 0:CR, :], ALU.add).then_inc(done["rows"], 1)
                    dve.wait_ge(done["smooth"], u + 1)
                    nc.vector.tensor_tensor(sobel_v[:, s, :, :], smooth[:, s, 2:XR, :], smooth[:, s, 0:CR, :],
                                            ALU.subtract).then_inc(done["sobel_v"], 1)
                    dve.wait_ge(done["rows"], u + 1)
                    nc.vector.scalar_tensor_tensor(out=sobel_h[:, s, :, :], in0=dx[:, s, 1:XR - 1, :], scalar=2.0,
                                                   in1=sobel_h[:, s, :, :], op0=ALU.mult, op1=ALU.add).then_inc(done["sobel_h"], 1)
                    dve.wait_ge(done["vert"], u + 1)
                    nc.vector.tensor_tensor(lap[:, s, :, :], lap[:, s, :, :], side[:, s, 1:XR - 1, :], ALU.add).then_inc(done["cross"], 1)
                    dve.wait_ge(done["cross"], START + u + 1)
                    nc.vector.scalar_tensor_tensor(out=lap[:, s, :, :], in0=x[:, 1:XR - 1, 1:W + 1], scalar=-4.0,
                                                   in1=lap[:, s, :, :], op0=ALU.mult, op1=ALU.add).then_inc(xb_used[k], 1)

                def norm(b, j):
                    dve.wait_ge(std_ready, START + NCH * b + j + 1)
                    dve.wait_ge(normed[1], START + KT // 2 * (NCH * b + j))
                    nc.vector.reciprocal(rstd[:, :], std[:, :]).then_inc(rstd_ready, 1)
                    dve.wait_ge(rstd_ready, START + NCH * b + j + 1)
                    for m in (0, 2):
                        dve.wait_ge(z_evac[m], START + NCH * b + j + 1)
                        nc.vector.tensor_tensor(centred[:, j % 2, m, :], centred[:, j % 2, m, :], rstd[:, :],
                                                ALU.mult).then_inc(normed[0], 1)

                def residual(b, j):
                    dve.wait_ge(x_out_loaded[j % 2], 16 * (NCH // 2) * b + 16 * (j // 2) + 16)
                    for m in range(KT):
                        dve.wait_ge(activated, KT * NCH * b + KT * j + m + 1)
                        y = centred[:, j % 2, m, :].rearrange("p (r w) -> p r w", w=W)
                        nc.vector.tensor_tensor(y, y, x_out[:, j % 2, m, :].rearrange("p (r w) -> p r w", w=W2)[:, :, 1:W + 1],
                                                ALU.add).then_inc(out_ready, 1)

                with dve.Fori(0, B) as b:
                    with dve.Fori(0, NCH) as j:
                        for k in range(KT):
                            stencils(b, j, k)
                    dve.wait_ge(feat_ready, START + NE * NCH * b + NE * NCH)
                    nc.vector.tensor_reduce(row_sum[:, :], pool_sum[:, :, :], AX_X, ALU.add).then_inc(pool_summed, 1)
                    dve.wait_ge(pool_summed, b + 1)
                    nc.vector.tensor_scalar(pooled[:, :], row_sum[:, :], 1.0 / N, None, ALU.mult).then_inc(pooled_ready, 1)
                    dve.wait_ge(gate_ready, KT * (b + 1))
                    for k in range(KT):
                        nc.vector.tensor_scalar(w_image[:, k, :], w_fuse[:, k, :], gate[:, k:k + 1], None,
                                                ALU.mult).then_inc(image_ready, 1)
                    for j in range(NCH):
                        norm(b, j)
                        residual(b, j)

            @block.gpsimd
            def _(pool):
                def neighbours(b, j, k):
                    s = k % 2
                    x = xb[:, k, :].rearrange("p (r w) -> p r w", w=W2)
                    pool.wait_ge(xb_loaded[k], 16 * NCH * b + 16 * j + 16)
                    pool.wait_ge(done["cross"], START + before(b, j, k))
                    nc.gpsimd.tensor_tensor(side[:, s, :, :], x[:, :, 0:W], x[:, :, 2:W2], ALU.add).then_inc(done["side"], 1)
                    pool.wait_ge(done["squares"], START + before(b, j, k))
                    nc.gpsimd.tensor_tensor(lap[:, s, :, :], x[:, 0:CR, 1:W + 1], x[:, 2:XR, 1:W + 1], ALU.add).then_inc(done["vert"], 1)

                def sums(b, j, k):
                    s = k % 2
                    n = KT * NCH * b + KT * j + k + 1
                    pool.wait_ge(done["squares"], START + n)
                    nc.gpsimd.tensor_tensor(sobel_v[:, s, :, :], sobel_v[:, s, :, :], sobel_h[:, s, :, :], ALU.add).then_inc(done["sum"], 1)
                    pool.wait_ge(done["sum"], n)
                    nc.gpsimd.tensor_tensor(lap_sq[:, s, :, :], lap_sq[:, s, :, :], sobel_v[:, s, :, :], ALU.add).then_inc(done["sum_lap"], 1)

                for s in (done["sum_lap"], normed[1]):
                    pool.sem_inc(s, START)
                with pool.Fori(0, B) as b:
                    with pool.Fori(0, NCH) as j:
                        for k in range(KT + 1):
                            if k < KT:
                                neighbours(b, j, k)
                            if k >= 1:
                                sums(b, j, k - 1)
                    for j in range(NCH):
                        pool.wait_ge(rstd_ready, START + NCH * b + j + 1)
                        for m in (1, 3):
                            pool.wait_ge(z_evac[m], START + NCH * b + j + 1)
                            nc.gpsimd.tensor_tensor(centred[:, j % 2, m, :], centred[:, j % 2, m, :], rstd[:, :],
                                                    ALU.mult).then_inc(normed[1], 1)


def program(nc, io, out):
    dram = {
        "taps": nc.dram_tensor("taps_dram", [HS, P, 3 * SH * GT], F32, kind="Internal").ap(),
        "strips": nc.dram_tensor("strips_dram", [3, P, SR, SROW], F32, kind="Internal").ap(),
        "conv_q": nc.dram_tensor("conv_q_dram", [SH, M, NS * W], F32, kind="Internal").ap(),
        "att": nc.dram_tensor("att_dram", [B, TILES, P, N], F32, kind="Internal").ap(),
        "x2": nc.dram_tensor("x2_dram", [B, KT, P, H2 * W2], F32, kind="Internal").ap(),
    }
    with ExitStack() as ctx:
        banks = [ctx.enter_context(nc.psum_tensor(f"bank{i}", [P, CH], F32)) for i in range(8)]
        prepare(nc, banks, io, dram)
        attention(nc, banks, io, dram)
        project(nc, banks, io, dram)
        edges(nc, banks, io, dram, out)


def kernel(x, L0_conv_wq, L0_conv_wk, L0_conv_wv, L0_conv_dw_kernel, L0_conv_pw_kernel, L0_conv_proj_kernel,
           L0_conv_bn_gamma, L0_conv_bn_beta, L0_conv_bn_mean, L0_conv_bn_var, L1_conv_w_branch, L1_conv_b_branch,
           L1_conv_bn_gamma, L1_conv_bn_beta, L1_conv_w_att1, L1_conv_b_att1, L1_conv_w_att2, L1_conv_b_att2,
           L1_conv_w_fuse, L1_conv_b_fuse, L1_conv_ln_gamma, L1_conv_ln_beta):
    import numpy as np
    import concourse.bacc as bacc
    from concourse.bass_utils import run_bass_kernel_spmd

    def a(t):
        return np.asarray(t)

    w = np.concatenate([a(L0_conv_wq), a(L0_conv_wk), a(L0_conv_wv)], 0)
    tap_sel = np.zeros((HD, KS, OR, HD, SR), np.float32)
    row_rep = np.zeros((HD, HD, SR), np.float32)
    for i in range(HD):
        row_rep[i, i, :] = 1
        for dy in range(KS):
            for r in range(OR):
                tap_sel[i, dy, r, i, r + dy] = 1
    vectors = [a(L0_conv_bn_gamma), a(L0_conv_bn_beta), a(L0_conv_bn_mean), a(L0_conv_bn_var),
               a(L1_conv_b_branch).reshape(C), a(L1_conv_bn_gamma).reshape(C), a(L1_conv_bn_beta).reshape(C),
               a(L1_conv_b_att2), a(L1_conv_b_fuse), a(L1_conv_ln_gamma), a(L1_conv_ln_beta)]
    arrays = {
        "x": a(x).reshape(B, C, N),
        "wT": w.reshape(HS, SH, 3, HD, KT, P).transpose(0, 5, 4, 2, 1, 3).reshape(HS, P, KT * 3 * P),
        "dwT": a(L0_conv_dw_kernel).reshape(NG, HD, KS, KS).transpose(1, 2, 0, 3).reshape(HD * KS, NG * KS),
        "pwT": a(L0_conv_pw_kernel).reshape(NG, HD, HD).transpose(2, 0, 1).reshape(HD, NG * HD),
        "projT": a(L0_conv_proj_kernel).reshape(C, TILES, P).transpose(2, 1, 0).reshape(P, TILES * C),
        "branchT": a(L1_conv_w_branch).reshape(NE, P, KT, P).transpose(3, 2, 0, 1).reshape(P, KT * NE * P),
        "fuseT": a(L1_conv_w_fuse).reshape(C, KT, P).transpose(2, 1, 0).reshape(P, KT * C),
        "att1T": a(L1_conv_w_att1).reshape(HID, KT, P).transpose(2, 1, 0).reshape(P, KT * HID),
        "att2T": a(L1_conv_w_att2).T,
        "b_att1": a(L1_conv_b_att1).reshape(HID, 1),
        "vec": np.stack(vectors).reshape(len(VEC), KT, P).transpose(2, 0, 1).reshape(P, len(VEC) * KT),
        "tap_sel": tap_sel.reshape(HD * KS, OR * P),
        "row_rep": row_rep.reshape(HD, P),
        "ident": np.eye(P, dtype=np.float32),
        "first_strip": (np.arange(P).reshape(P, 1) % 2 == 0).astype(np.float32),
        "head_mask": np.kron(np.eye(SH, dtype=np.float32), np.ones((HD, HD), np.float32)),
    }
    nc = bacc.Bacc("TRN2", target_bir_lowering=False, num_devices=1)
    feeds, io = {}, {}
    for name, value in arrays.items():
        feeds[f"in_{name}"] = np.ascontiguousarray(value)
        io[name] = nc.dram_tensor(f"in_{name}", value.shape, F32, kind="ExternalInput").ap()
    out = nc.dram_tensor("out", (B, C, N), F32, kind="ExternalOutput").ap()
    program(nc, io, out)
    result = run_bass_kernel_spmd(nc, [feeds], core_ids=[0])
    return result.results[0]["out"].reshape(B, C, H, W)
```

```python
from contextlib import ExitStack

import concourse.bass as bass
from concourse import mybir

F32 = mybir.dt.float32
ALU = mybir.AluOpType
ACT = mybir.ActivationFunctionType
AX_X = mybir.AxisListType.X

P = 128
B, C, H, W = 4, 512, 64, 64
N = H * W
KT = C // P
HD = 8
HEADS = C // HD
HS = 4
SH = HEADS // HS
CH = 512
NCH = N // CH
CR = CH // W
KS = 5
HALO = KS // 2
TS = 4
PL = TS * TS
TG = (H + 2 * HALO) // TS
TN = TG * TG
TO = H // TS
TT = TO * TO
HV = TT // P
HT = P // TO
SHIFTS = [(a, b) for a in range(2) for b in range(2)]
M = HD * PL
NTAP = len(SHIFTS) * PL
GT = NTAP + HD
BLOCKS = TN * PL // P
SKIP = TN * PL % P
TURNS = BLOCKS // 4
NG = 3 * HEADS
PARTS = [(0, TG // 2), (TG // 2, 3 * TG // 4), (3 * TG // 4, TG)]
IT = B * HS
TILES = 2 * HS
EPS_ATT, EPS_BN, EPS_LN, EPS_GRAD = 1e-15, 1e-5, 1e-6, 1e-8
NE = 4
H2, W2 = H + 2, W + 2
HID = C // 8
START = 1
VEC = ["bn0_gamma", "bn0_beta", "bn0_mean", "bn0_var", "b_branch", "bn1_gamma", "bn1_beta",
       "b_att2", "b_fuse", "ln_gamma", "ln_beta"]


def prepare(nc, banks, io, dram):
    with ExitStack() as ctx:
        def sb(name, shape):
            return ctx.enter_context(nc.sbuf_tensor(name, shape, F32))

        def sem(name):
            return ctx.enter_context(nc.semaphore(name))

        dw_sb = sb("dw_sb", [HD * KS, NG * KS])
        pw_sb = sb("pw_sb", [HD, NG * HD])
        sel_sb = sb("sel_sb", [HD * KS, TS, 2 * TS, P])
        rep_sb = sb("rep_sb", [HD, P])
        taps_sb = sb("taps_sb", [P, NG, GT])
        zeros = sb("zeros", [P, KT * W2])
        loaded = sem("prep_loaded")
        zeroed = sem("prep_zeroed")
        product = sem("prep_product")
        copied = sem("prep_copied")
        stored = sem("prep_stored")
        points = [(a, b, oy, ox) for a, b in SHIFTS for oy in range(TS) for ox in range(TS)]
        NP = NTAP // 2
        PC = NG * HD // 3

        with nc.Block() as block:
            @block.sync
            def _(sp):
                sp.dma_start(dw_sb[:, :], io["dwT"]).then_inc(loaded, 16)
                sp.dma_start(pw_sb[:, :], io["pwT"]).then_inc(loaded, 16)
                sp.dma_start(sel_sb[:, :, :, :].rearrange("k r o p -> k (r o p)"), io["tap_sel"]).then_inc(loaded, 16)
                sp.dma_start(rep_sb[:, :], io["row_rep"]).then_inc(loaded, 16)
                sp.wait_ge(zeroed, 1)
                for b in range(B):
                    for row in (0, H2 - 1):
                        sp.dma_start(dram["x2"][b].rearrange("m p n -> p m n")[:, :, row * W2:(row + 1) * W2],
                                     zeros[:, 0:KT * W2].rearrange("p (m w) -> p m w", w=W2)).then_inc(stored, 16)
                sp.wait_ge(copied, NP + 3)
                for hs in range(HS):
                    sp.dma_start(dram["taps"][hs],
                                 taps_sb[:, hs * 3 * SH:(hs + 1) * 3 * SH, :].rearrange("p g t -> p (g t)")).then_inc(stored, 16)
                sp.wait_ge(stored, 16 * (2 * B + HS))

            @block.tensor
            def _(pe):
                pe.wait_ge(loaded, 64)
                for n in range(NP):
                    if n >= 8:
                        pe.wait_ge(copied, n - 7)
                    for i in range(2):
                        a, b, oy, ox = points[2 * n + i]
                        cols = [(dx, dx - TS * b + ox) for dx in range(KS) if 0 <= dx - TS * b + ox < TS]
                        for dx, rx in cols:
                            last = nc.tensor.matmul(banks[n % 8][:, i * NG:(i + 1) * NG], sel_sb[:, rx, TS * a + oy, :],
                                                    dw_sb[:, :].rearrange("k (g d) -> k g d", d=KS)[:, :, dx],
                                                    start=(dx == cols[0][0]), stop=(dx == cols[-1][0]))
                    last.then_inc(product, 1)
                for n in range(3):
                    pe.wait_ge(copied, NP + n - 7)
                    nc.tensor.matmul(banks[(NP + n) % 8][:, 0:PC], rep_sb[:, :],
                                     pw_sb[:, n * PC:(n + 1) * PC], start=True, stop=True).then_inc(product, 1)

            @block.vector
            def _(dve):
                nc.vector.memset(zeros[:, :], 0.0).then_inc(zeroed, 1)
                for n in range(NP):
                    dve.wait_ge(product, n + 1)
                    nc.vector.tensor_copy(taps_sb[:, :, 2 * n:2 * n + 2],
                                          banks[n % 8][:, 0:2 * NG].rearrange("p (n g) -> p g n", g=NG)).then_inc(copied, 1)
                for n in range(3):
                    dve.wait_ge(product, NP + n + 1)
                    nc.vector.tensor_copy(
                        taps_sb[:, n * NG // 3:(n + 1) * NG // 3, NTAP:GT],
                        banks[(NP + n) % 8][:, 0:PC].rearrange("p (g o) -> p g o", o=HD)).then_inc(copied, 1)


def attention(nc, banks, io, dram):
    with ExitStack() as ctx:
        def sb(name, shape):
            return ctx.enter_context(nc.sbuf_tensor(name, shape, F32))

        def sem(name):
            return ctx.enter_context(nc.semaphore(name))

        XR = 2
        x_sb = sb("x_sb", [P, XR, KT, CH])
        w_sb = sb("w_sb", [P, KT, 3, P])
        taps = sb("taps", [P, 3 * SH, GT])
        tiles = [sb(f"{n}_tiles", [P, PL, TN]) for n in "qkv"]
        relu_q = sb("relu_q", [P, PL, TT])
        key_t = sb("key_t", [P, 2, 4, P])
        value_t = sb("value_t", [P, 2, 4, P + 1])
        ckey_t = sb("ckey_t", [P, HV * PL, P])
        cvalue_t = sb("cvalue_t", [P, HV * PL, P + 1])
        loaded = sb("loaded", [P, 2, 3, TN])
        columns = sb("columns", [P, 2, 2, HV + 1, TG * HT])
        toeplitz = sb("toeplitz", [P, 2, 3, len(SHIFTS) * M])
        q_stage = sb("q_stage", [M, 2, TT])
        score_n = sb("score_n", [P, 2, P])
        score_d = sb("score_d", [P, 2, P])
        key_sum = sb("key_sum", [P, 1])
        den_sb = sb("den_sb", [P, CH])
        out_sb = sb("out_sb", [P, CH])
        ident = sb("ident", [P, P])
        mask = sb("mask", [P, P])

        const_loaded = sem("att_const_loaded")
        cleared = sem("att_cleared")
        x_loaded = [sem(f"x_loaded{i}") for i in range(XR)]
        w_loaded = sem("w_loaded")
        taps_loaded = sem("taps_loaded")
        qkv_ready = sem("qkv_ready")
        evac = [sem(f"{n}_evacuated") for n in "qkv"]
        relu_q_ready = sem("relu_q_ready")
        tiles_written = [sem(f"{n}_tiles_written") for n in "qkv"]
        turned = sem("turned")
        key_t_ready = sem("key_t_ready")
        value_t_ready = sem("value_t_ready")
        chunk_scored = sem("chunk_scored")
        scores_ready = sem("scores_ready")
        key_sum_ready = sem("key_sum_ready")
        scores_masked = sem("scores_masked")
        attended = sem("attended")
        den_evac = sem("den_evac")
        inverted = sem("inverted")
        divided = sem("divided")
        out_written = sem("out_written")
        tiles_loaded = [sem(f"tiles_loaded{i}") for i in range(2)]
        columns_ready = [sem(f"columns_ready{i}") for i in range(2)]
        head_done = [sem(f"head_done{i}") for i in range(2)]
        toeplitz_ready = sem("toeplitz_ready")
        cready = [sem(f"conv_{n}_ready") for n in "qk"]
        cevac = [sem(f"conv_{n}_evacuated") for n in "qkv"]
        q_written = [sem(f"q_written{i}") for i in range(2)]
        conv_q_loaded = sem("conv_q_loaded")

        T_Q, T_K, T_V = range(3)
        FIRST_TURN = NCH
        WRITES = len(PARTS)
        KEY_BANK, VALUE_BANK, SCORE_BANK = banks[3], banks[4], banks[5]
        NUM_BANK, DEN_BANK = banks[6], banks[7]

        def at(it, half, j):
            return 2 * NCH * it + NCH * half + j

        def pairs(eng, first, steady, final):
            first()
            with eng.Fori(0, IT - 1) as it:
                steady(it)
            final(IT - 1)

        def last_chunk(part):
            return min(TS * PARTS[part][1] - HALO - 1, H - 1) // CR

        def spread(engine_op, j, t):
            for r, n, y, a in ((0, TS - HALO, HALO, 2 * j), (TS - HALO, TS, 0, 2 * j + 1), (CR - HALO, HALO, 0, 2 * j + 2)):
                for x in range(2):
                    last = engine_op(
                        tiles[t][:, :, :].rearrange("p (i h k) (a c) -> p h i k a c", h=2, k=TS // 2, c=TG)
                        [:, 1 - x, y:y + n, :, a, x:x + TO],
                        banks[t][:, :].rearrange("p (i c g k) -> p g i k c", c=TO, g=2, k=TS // 2)[:, x, r:r + n, :, :])
            return last

        def eighths(j):
            for y, x, a in [(y, x, a) for y in range(2) for x in range(2) for a in range(CR // TS)]:
                yield (tiles[0][:, :, :].rearrange("p (g i h k) (a c) -> p g h i k a c", g=2, i=2, h=2, c=TG)
                       [:, 1 - y, 1 - x, :, :, 2 * j + y + a, x:x + TO],
                       relu_q[:, :, :].rearrange("p (g i h k) (a c) -> p g h i k a c", g=2, i=2, h=2, c=TO)
                       [:, y, x, :, :, 2 * j + a, :])

        with nc.Block() as block:
            @block.sync
            def _(sp):
                def load_x(it, j):
                    sp.dma_start(x_sb[:, j % XR, :, :],
                                 io["x"][it // HS].rearrange("(k p) n -> p k n", p=P)[:, :, j * CH:(j + 1) * CH]
                                 ).then_inc(x_loaded[j % XR], 16)

                def load_weights(it):
                    sp.dma_start(w_sb[:, :, :, :].rearrange("p k t m -> p (k t m)"), io["wT"][it % HS]).then_inc(w_loaded, 16)

                def load_taps(it):
                    sp.dma_start(taps[:, :, :].rearrange("p g t -> p (g t)"), dram["taps"][it % HS]).then_inc(taps_loaded, 16)

                def write_part(it, part):
                    a, z = PARTS[part]
                    for t in range(3):
                        sp.wait_ge(evac[t], NCH * it + last_chunk(part) + 1)
                        sp.dma_start(dram["tiles"][t][:, :, a * TG:z * TG],
                                     tiles[t][:, :, a * TG:z * TG]).then_inc(tiles_written[t], 16)

                def load_tiles(it, jj, par):
                    src = dram["tiles"].rearrange("t (j i) r s -> j t (i r) s", i=HD)[2 * jj + par]
                    sp.dma_start(loaded[:, par, :, :], src.rearrange("t p s -> p t s")).then_inc(tiles_loaded[par], 16)

                def write_q(it, jj, par):
                    sp.wait_ge(cevac[T_Q], START + SH * it + 2 * jj + par + 1)
                    sp.dma_start(dram["conv_q"][2 * jj + par], q_stage[:, par, :]).then_inc(q_written[par], 16)

                def spill(it, half, j):
                    sp.wait_ge(divided, START + at(it, half, j) + 1)
                    sp.dma_start(dram["att"][it // HS][it % HS + HS * half][:, bass.ds(j * CH, CH)],
                                 out_sb[:, :]).then_inc(out_written, 16)

                def plain(it, conv_of):
                    for kind, n in [("x", 2), ("x", 3), ("x", 4), ("x", 5), ("p", 0), ("x", 6), ("x", 7), ("p", 1), ("p", 2)]:
                        if kind == "x":
                            sp.wait_ge(qkv_ready, 3 * (NCH * it + n - XR + 1))
                            load_x(it, n)
                            if conv_of is not None:
                                spill(conv_of, 1, n - XR)
                        else:
                            write_part(it, n)
                    if conv_of is not None:
                        for j in range(NCH - XR, NCH):
                            spill(conv_of, 1, j)
                    for t in range(3):
                        sp.wait_ge(tiles_written[t], 16 * WRITES * (it + 1))
                    for par in range(2):
                        load_tiles(it, 0, par)

                def load_next(it):
                    sp.wait_ge(qkv_ready, 3 * NCH * it)
                    load_weights(it)
                    for j in range(XR):
                        load_x(it, j)

                def conv(it, last):
                    with sp.Fori(0, SH // 2 - 1) as jj:
                        for par in range(2):
                            write_q(it, jj, par)
                            sp.wait_ge(head_done[par], START + SH // 2 * it + jj + 1)
                            load_tiles(it, jj + 1, par)
                        spill(it, 0, jj)
                    for par in range(2):
                        write_q(it, SH // 2 - 1, par)
                    spill(it, 0, NCH - 1)
                    if not last:
                        sp.wait_ge(toeplitz_ready, SH * (it + 1))
                        load_taps(it + 1)
                    for par in range(2):
                        sp.wait_ge(q_written[par], 16 * START + 16 * (SH // 2) * (it + 1))
                    sp.dma_start(relu_q[:, :, :],
                                 dram["conv_q"].rearrange("j (o r) s -> (j o) r s", o=HD)).then_inc(conv_q_loaded, 16)

                def first():
                    for s in [out_written] + q_written:
                        sp.sem_inc(s, 16 * START)
                    sp.dma_start(ident[:, :], io["ident"]).then_inc(const_loaded, 16)
                    sp.dma_start(mask[:, :], io["head_mask"]).then_inc(const_loaded, 16)
                    load_weights(0)
                    load_taps(0)
                    for j in range(XR):
                        load_x(0, j)
                    plain(0, None)

                def steady(it):
                    load_next(it + 1)
                    conv(it, False)
                    plain(it + 1, it)

                def final(it):
                    conv(it, True)
                    for j in range(NCH):
                        spill(it, 1, j)
                    sp.wait_ge(out_written, 16 * START + 16 * at(IT, 0, 0))

                pairs(sp, first, steady, final)

            @block.tensor
            def _(pe):
                def qkv(it, j):
                    pe.wait_ge(x_loaded[j % XR], 16 * (NCH // XR) * it + 16 * (j // XR + 1))
                    for t in range(3):
                        pe.wait_ge(evac[t], NCH * it + j)
                        for k in range(KT):
                            last = nc.tensor.matmul(banks[t][:, :], w_sb[:, k, t, :], x_sb[:, j % XR, k, :],
                                                    start=(k == 0), stop=(k == KT - 1))
                        last.then_inc(qkv_ready, 1)

                def turn(it, g):
                    for t in (T_K, T_V):
                        pe.wait_ge(evac[t], NCH * (it + 1))
                    pe.wait_ge(key_t_ready, TURNS * it + g)
                    pe.wait_ge(value_t_ready, TURNS * it + g)
                    for t, bank in ((T_K, KEY_BANK), (T_V, VALUE_BANK)):
                        for n in range(4):
                            block = tiles[t][:, :, :].rearrange("p r s -> p (r s)")
                            block = block[:, SKIP + (4 * g + n) * P:SKIP + (4 * g + n + 1) * P]
                            last = nc.tensor.matmul(bank[:, n * P:(n + 1) * P], block, ident[:, :],
                                                    start=True, stop=True, is_transpose=True)
                    last.then_inc(turned, 1)

                def score(it, g):
                    pe.wait_ge(key_t_ready, TURNS * it + g + 1)
                    pe.wait_ge(value_t_ready, TURNS * it + g + 1)
                    for n in range(4):
                        last = nc.tensor.matmul(SCORE_BANK[:, 0:P + 1], key_t[:, g % 2, n, :], value_t[:, g % 2, n, :],
                                                start=(g == 0 and n == 0), stop=(g == TURNS - 1 and n == 3))
                    last.then_inc(chunk_scored, 1)

                def attend(it, half, j):
                    pe.wait_ge(scores_masked, 2 * it + half + 1)
                    if half == 0:
                        pe.wait_ge(relu_q_ready, NCH * it + j + 1)
                    else:
                        pe.wait_ge(conv_q_loaded, 16 * (it + 1))
                    pe.wait_ge(den_evac, START + at(it, half, j))
                    pe.wait_ge(divided, START + at(it, half, j))
                    for bank, score in ((DEN_BANK, score_d), (NUM_BANK, score_n)):
                        for y in range(2):
                            q = relu_q[:, :, :].rearrange("p (r x) (a c) -> p a r c x", x=TS, c=TO)
                            last = nc.tensor.matmul(bank[:, y * TS * W:(y + 1) * TS * W], score[:, half, :],
                                                    q[:, bass.ds(2 * j + y, 1), :, :, :], start=True, stop=True)
                    last.then_inc(attended, 1)

                def plain(it, conv_of):
                    pe.wait_ge(w_loaded, 16 * (it + 1))
                    for step in range(FIRST_TURN + TURNS + 1):
                        if step < NCH:
                            qkv(it, step)
                            if conv_of is not None:
                                attend(conv_of, 1, step)
                        if 0 <= step - FIRST_TURN < TURNS:
                            turn(it, step - FIRST_TURN)
                        if 0 <= step - FIRST_TURN - 1:
                            score(it, step - FIRST_TURN - 1)

                def conv(it):
                    with pe.Fori(0, SH // 2) as jj:
                        attend(it, 0, jj)
                        for par in range(2):
                            pe.wait_ge(tiles_loaded[par], SH // 2 * 16 * it + 16 * jj + 16)
                            pe.wait_ge(toeplitz_ready, SH * it + 2 * jj + par + 1)
                            x_q = loaded[:, par, T_Q, :].rearrange("p (a c) -> p a c", c=TG)
                            w = toeplitz[:, par, :, :].rearrange("p t (d m) -> p t d m", m=M)
                            pe.wait_ge(cevac[T_Q], START + SH * it + 2 * jj + par)
                            for d, (a, b) in enumerate(SHIFTS):
                                last = nc.tensor.matmul(banks[T_Q][0:M, 0:TT], w[:, T_Q, d, :], x_q[:, a:a + TO, b:b + TO],
                                                        start=(d == 0), stop=(d == len(SHIFTS) - 1))
                            last.then_inc(cready[T_Q], 1)
                            pe.wait_ge(columns_ready[par], SH // 2 * it + jj + 1)
                            for t in (T_K, T_V):
                                pe.wait_ge(cevac[t], START + SH * it + 2 * jj + par)
                                for h in range(HV):
                                    for d, (a, b) in enumerate(SHIFTS):
                                        last = nc.tensor.matmul(banks[t][:, h * M:(h + 1) * M],
                                                                columns[:, par, t - T_K, h + b, a * HT:(a + TO) * HT],
                                                                w[:, t, d, :], start=(d == 0), stop=(d == len(SHIFTS) - 1))
                                last.then_inc(cready[t] if t == T_K else head_done[par], 1)
                    pe.wait_ge(cevac[T_K], START + SH * (it + 1))
                    pe.wait_ge(cevac[T_V], START + SH * (it + 1))
                    for n in range(HV * PL):
                        last = nc.tensor.matmul(SCORE_BANK[:, 0:P + 1], ckey_t[:, n, :], cvalue_t[:, n, :],
                                                start=(n == 0), stop=(n == HV * PL - 1))
                    last.then_inc(scores_ready, 1)

                def first():
                    for s in head_done:
                        pe.sem_inc(s, START)
                    pe.wait_ge(const_loaded, 32)
                    pe.wait_ge(cleared, 1)
                    plain(0, None)

                def steady(it):
                    conv(it)
                    plain(it + 1, it)

                def final(it):
                    conv(it)
                    for j in range(NCH):
                        attend(it, 1, j)

                pairs(pe, first, steady, final)

            @block.scalar
            def _(act):
                def copy(to, source):
                    return nc.scalar.activation(to, source, ACT.Copy)

                def evacuate(it, j):
                    act.wait_ge(qkv_ready, 3 * NCH * it + 3 * j + T_Q + 1)
                    spread(copy, j, T_Q).then_inc(evac[T_Q], 1)
                    act.wait_ge(qkv_ready, 3 * NCH * it + 3 * j + T_K + 1)
                    spread(copy, j, T_K).then_inc(evac[T_K], 1)

                def value_by_position(it, g):
                    act.wait_ge(turned, TURNS * it + g + 1)
                    act.wait_ge(chunk_scored, TURNS * it + max(g - 1, 0))
                    nc.scalar.activation(value_t[:, g % 2, :, 0:P], VALUE_BANK[:, :].rearrange("p (n m) -> p n m", m=P),
                                         ACT.Copy).then_inc(value_t_ready, 1)

                def denominators(it, half, j):
                    act.wait_ge(attended, at(it, half, j) + 1)
                    act.wait_ge(divided, START + at(it, half, j))
                    nc.scalar.activation(den_sb[:, :], DEN_BANK[:, :], ACT.Copy, bias=EPS_ATT).then_inc(den_evac, 1)

                def plain(it, conv_of):
                    for t in (T_Q, T_K):
                        act.wait_ge(tiles_written[t], 16 * WRITES * it)
                    for step in range(FIRST_TURN + TURNS):
                        if step < NCH:
                            evacuate(it, step)
                            if conv_of is not None:
                                denominators(conv_of, 1, step)
                        if step >= FIRST_TURN:
                            value_by_position(it, step - FIRST_TURN)

                def conv(it):
                    with act.Fori(0, SH // 2) as jj:
                        denominators(it, 0, jj)
                        for par in range(2):
                            act.wait_ge(tiles_loaded[par], SH // 2 * 16 * it + 16 * jj + 16)
                            act.wait_ge(head_done[par], START + SH // 2 * it + jj)
                            for h in range(HV + 1):
                                last = nc.scalar.activation(
                                    columns[:, par, :, h, :].rearrange("p t (a v) -> p t a v", v=HT),
                                    loaded[:, par, T_K:, :].rearrange("p t (a c) -> p t a c", c=TG)[:, :, :, h:h + TO - 1:HV],
                                    ACT.Copy)
                            last.then_inc(columns_ready[par], 1)
                        for par in range(2):
                            act.wait_ge(cready[T_Q], SH * it + 2 * jj + par + 1)
                            act.wait_ge(q_written[par], 16 * START + SH // 2 * 16 * it + 16 * jj)
                            nc.scalar.activation(q_stage[:, par, :], banks[T_Q][0:M, 0:TT], ACT.Relu).then_inc(cevac[T_Q], 1)
                            act.wait_ge(head_done[par], START + SH // 2 * it + jj + 1)
                            to = cvalue_t[:, :, bass.ds((2 * jj + par) * HD, HD)].rearrange("p (s r) o -> p s r o", s=HV)
                            nc.scalar.activation(to, banks[T_V][:, 0:HV * M].rearrange("p (s o r) -> p s r o", o=HD, r=PL),
                                                 ACT.Copy).then_inc(cevac[T_V], 1)

                def first():
                    for s in (cevac[T_Q], cevac[T_V], den_evac):
                        act.sem_inc(s, START)
                    act.wait_ge(cleared, 1)
                    plain(0, None)

                def steady(it):
                    conv(it)
                    plain(it + 1, it)

                def final(it):
                    conv(it)
                    for j in range(NCH):
                        denominators(it, 1, j)

                pairs(act, first, steady, final)

            @block.vector
            def _(dve):
                def keys_by_position(it, g):
                    dve.wait_ge(turned, TURNS * it + g + 1)
                    dve.wait_ge(chunk_scored, TURNS * it + max(g - 1, 0))
                    nc.vector.tensor_scalar(key_t[:, g % 2, :, :].rearrange("p n m -> p (n m)"), KEY_BANK[:, :],
                                            0.0, None, ALU.max).then_inc(key_t_ready, 1)

                def mask_scores(it, half):
                    if half:
                        dve.wait_ge(scores_ready, it + 1)
                    else:
                        dve.wait_ge(chunk_scored, TURNS * (it + 1))
                    nc.vector.tensor_copy(key_sum[:, :], SCORE_BANK[:, P:P + 1]).then_inc(key_sum_ready, 1)
                    nc.vector.tensor_tensor(score_n[:, half, :], SCORE_BANK[:, 0:P], mask[:, :], ALU.mult)
                    dve.wait_ge(key_sum_ready, 2 * it + half + 1)
                    nc.vector.tensor_scalar(score_d[:, half, :], mask[:, :], key_sum[:, 0:1], None,
                                            ALU.mult).then_inc(scores_masked, 1)

                def divide(it, half, j):
                    dve.wait_ge(den_evac, START + at(it, half, j) + 1)
                    nc.vector.reciprocal(den_sb[:, :], den_sb[:, :]).then_inc(inverted, 1)
                    dve.wait_ge(inverted, at(it, half, j) + 1)
                    dve.wait_ge(out_written, 16 * START + 16 * at(it, half, j))
                    nc.vector.tensor_tensor(out_sb[:, :], NUM_BANK[:, :], den_sb[:, :], ALU.mult).then_inc(divided, 1)

                def plain(it, conv_of):
                    dve.wait_ge(tiles_written[T_V], 16 * WRITES * it)
                    for step in range(FIRST_TURN + TURNS):
                        if step < NCH:
                            dve.wait_ge(qkv_ready, 3 * NCH * it + 3 * step + T_V + 1)
                            spread(nc.vector.tensor_copy, step, T_V).then_inc(evac[T_V], 1)
                        if step >= FIRST_TURN:
                            keys_by_position(it, step - FIRST_TURN)
                        if step < NCH:
                            if conv_of is not None:
                                divide(conv_of, 1, step)
                            dve.wait_ge(evac[T_Q], NCH * it + step + 1)
                            for bordered, plain_q in eighths(step):
                                last = nc.vector.tensor_scalar(plain_q, bordered, 0.0, None, ALU.max)
                            last.then_inc(relu_q_ready, 1)
                    mask_scores(it, 0)

                def conv(it):
                    with dve.Fori(0, SH // 2) as jj:
                        divide(it, 0, jj)
                        for par in range(2):
                            dve.wait_ge(cready[T_K], SH * it + 2 * jj + par + 1)
                            to = ckey_t[:, :, bass.ds((2 * jj + par) * HD, HD)].rearrange("p (s r) o -> p s r o", s=HV)
                            nc.vector.tensor_scalar(
                                to, banks[T_K][:, 0:HV * M].rearrange("p (s o r) -> p s r o", o=HD, r=PL), 0.0, None,
                                ALU.max).then_inc(cevac[T_K], 1)
                    mask_scores(it, 1)

                def first():
                    for s in (cevac[T_K], divided):
                        dve.sem_inc(s, START)
                    for t in range(3):
                        nc.vector.memset(tiles[t][:, :, :].rearrange("p r s -> p (r s)"), 0.0)
                    nc.vector.memset(value_t[:, :, :, P:P + 1], 1.0)
                    nc.vector.memset(cvalue_t[:, :, P:P + 1], 1.0).then_inc(cleared, 1)
                    dve.wait_ge(cleared, 1)
                    dve.wait_ge(const_loaded, 32)
                    plain(0, None)

                def steady(it):
                    conv(it)
                    plain(it + 1, it)

                def final(it):
                    conv(it)
                    for j in range(NCH):
                        divide(it, 1, j)

                pairs(dve, first, steady, final)

            @block.gpsimd
            def _(pool):
                with pool.Fori(0, IT) as it:
                    with pool.Fori(0, SH // 2) as jj:
                        for par in range(2):
                            pool.wait_ge(taps_loaded, 16 * (it + 1))
                            pool.wait_ge(head_done[par], START + SH // 2 * it + jj)
                            for t in range(3):
                                g = taps[:, :, :].rearrange("p (j t) n -> p j t n", t=3)[:, 2 * jj + par, t, :]
                                tap = g[:, 0:NTAP].rearrange("p (d r) -> p d r", r=PL)[:, :, None, :].to_broadcast(
                                    [P, len(SHIFTS), HD, PL])
                                point = g[:, NTAP:GT][:, None, :, None].to_broadcast([P, len(SHIFTS), HD, PL])
                                last = nc.gpsimd.tensor_tensor(
                                    toeplitz[:, par, t, :].rearrange("p (d o r) -> p d o r", o=HD, r=PL), tap, point, ALU.mult)
                            last.then_inc(toeplitz_ready, 1)


def project(nc, banks, io, dram):
    with ExitStack() as ctx:
        def sb(name, shape):
            return ctx.enter_context(nc.sbuf_tensor(name, shape, F32))

        def sem(name):
            return ctx.enter_context(nc.semaphore(name))

        w_sb = sb("proj_w", [P, TILES, C])
        att = sb("proj_att", [P, 2, TILES, CH])
        x_sb = sb("proj_x", [P, 2, KT, CH])
        x2_sb = sb("proj_x2", [P, 2, KT, CR * W2])
        vec = sb("proj_vec", [P, len(VEC), KT])
        scale = sb("proj_scale", [P, KT])
        root = sb("proj_root", [P, KT])
        shift = sb("proj_shift", [P, KT])
        eps = sb("proj_eps", [P, 1])
        const_loaded = sem("proj_const_loaded")
        set_up = sem("proj_set_up")
        rooted = sem("proj_rooted")
        scaled = sem("proj_scaled")
        att_loaded = [sem(f"att_loaded{i}") for i in range(2)]
        res_loaded = [sem(f"res_loaded{i}") for i in range(2)]
        projected = sem("projected")
        shifted = sem("shifted")
        summed = [[sem(f"summed{par}{m}") for m in range(KT)] for par in range(2)]
        x2_written = [sem(f"x2_written{i}") for i in range(2)]
        CHUNKS = B * NCH

        def v(name):
            return vec[:, VEC.index(name), :]

        with nc.Block() as block:
            @block.sync
            def _(sp):
                for s in x2_written:
                    sp.sem_inc(s, 16 * START)
                sp.dma_start(w_sb[:, :, :].rearrange("p t o -> p (t o)"), io["projT"]).then_inc(const_loaded, 16)
                sp.dma_start(vec[:, :, :].rearrange("p v m -> p (v m)"), io["vec"]).then_inc(const_loaded, 16)

                def load(i, par):
                    c = 2 * i + par
                    n = (c % NCH) * CH
                    sp.dma_start(att[:, par, :, :], dram["att"][c // NCH].rearrange("t p n -> p t n")[:, :, bass.ds(n, CH)]
                                 ).then_inc(att_loaded[par], 16)
                    sp.dma_start(x_sb[:, par, :, :], io["x"][c // NCH].rearrange("(k p) n -> p k n", p=P)[:, :, bass.ds(n, CH)]
                                 ).then_inc(res_loaded[par], 16)

                def store(i, par):
                    c = 2 * i + par
                    n = (c % NCH) * (CR * W2) + W2
                    for m in range(KT):
                        sp.wait_ge(summed[par][m], START + i + 1)
                    sp.dma_start(dram["x2"][c // NCH].rearrange("m p n -> p m n")[:, :, bass.ds(n, CR * W2)],
                                 x2_sb[:, par, :, :]).then_inc(x2_written[par], 16)

                for par in range(2):
                    load(0, par)
                with sp.Fori(0, CHUNKS // 2 - 1) as i:
                    for par in range(2):
                        store(i, par)
                        load(i + 1, par)
                for par in range(2):
                    store(CHUNKS // 2 - 1, par)
                for par in range(2):
                    sp.wait_ge(x2_written[par], 16 * START + 16 * CHUNKS // 2)

            @block.tensor
            def _(pe):
                pe.wait_ge(const_loaded, 32)
                with pe.Fori(0, CHUNKS // 2) as i:
                    for par in range(2):
                        pe.wait_ge(att_loaded[par], 16 * i + 16)
                        for m in range(KT):
                            pe.wait_ge(summed[par][m], START + i)
                            for k in range(TILES):
                                last = nc.tensor.matmul(banks[KT * par + m][:, :], w_sb[:, k, m * P:(m + 1) * P],
                                                        att[:, par, k, :], start=(k == 0), stop=(k == TILES - 1))
                            last.then_inc(projected, 1)

            @block.scalar
            def _(act):
                act.wait_ge(set_up, 1)
                nc.scalar.activation(root[:, :], v("bn0_var"), ACT.Sqrt, bias=eps[:, 0:1]).then_inc(rooted, 1)
                act.wait_ge(scaled, 3)
                with act.Fori(0, CHUNKS // 2) as i:
                    for par in range(2):
                        act.wait_ge(res_loaded[par], 16 * i + 16)
                        for m in range(KT):
                            nc.scalar.activation(x_sb[:, par, m, :], x_sb[:, par, m, :], ACT.Identity,
                                                 bias=shift[:, m:m + 1]).then_inc(shifted, 1)

            @block.vector
            def _(dve):
                for s in summed[0] + summed[1]:
                    dve.sem_inc(s, START)
                nc.vector.memset(x2_sb[:, :, :, :].rearrange("p a m n -> p (a m n)"), 0.0)
                nc.vector.memset(eps[:, :], EPS_BN)
                dve.wait_ge(const_loaded, 32)
                nc.vector.tensor_copy(shift[:, :], v("bn0_mean")).then_inc(set_up, 1)
                dve.wait_ge(rooted, 1)
                nc.vector.reciprocal(scale[:, :], root[:, :]).then_inc(scaled, 1)
                dve.wait_ge(scaled, 1)
                nc.vector.tensor_tensor(scale[:, :], scale[:, :], v("bn0_gamma"), ALU.mult).then_inc(scaled, 1)
                dve.wait_ge(scaled, 2)
                nc.vector.tensor_tensor(root[:, :], scale[:, :], shift[:, :], ALU.mult).then_inc(rooted, 1)
                dve.wait_ge(rooted, 2)
                nc.vector.tensor_tensor(shift[:, :], v("bn0_beta"), root[:, :], ALU.subtract).then_inc(scaled, 1)
                with dve.Fori(0, CHUNKS // 2) as i:
                    for par in range(2):
                        dve.wait_ge(x2_written[par], 16 * START + 16 * i)
                        for m in range(KT):
                            c = KT * 2 * i + KT * par + m
                            dve.wait_ge(shifted, c + 1)
                            dve.wait_ge(projected, c + 1)
                            nc.vector.scalar_tensor_tensor(
                                out=x2_sb[:, par, m, :].rearrange("p (r w) -> p r w", w=W2)[:, :, 1:W + 1],
                                in0=banks[KT * par + m][:, :].rearrange("p (r w) -> p r w", w=W), scalar=scale[:, m:m + 1],
                                in1=x_sb[:, par, m, :].rearrange("p (r w) -> p r w", w=W),
                                op0=ALU.mult, op1=ALU.add).then_inc(summed[par][m], 1)


def edges(nc, banks, io, dram, out):
    with ExitStack() as ctx:
        def sb(name, shape):
            return ctx.enter_context(nc.sbuf_tensor(name, shape, F32))

        def sem(name):
            return ctx.enter_context(nc.semaphore(name))

        XR = CR + 2
        feat = sb("feat", [P, NE, N])
        xb = sb("xb", [P, KT, XR * W2])
        dx = sb("dx", [P, 2, XR, W])
        side = sb("side", [P, 2, XR, W])
        smooth = sb("smooth", [P, 2, XR, W])
        sobel_h = sb("sobel_h", [P, 2, CR, W])
        sobel_v = sb("sobel_v", [P, 2, CR, W])
        lap = sb("lap", [P, 2, CR, W])
        diag = sb("diag", [P, 2, CR, W])
        lap_sq = sb("lap_sq", [P, 2, CR, W])
        edge = sb("edge", [P, 2, NE, CH])
        w_branch = sb("w_branch", [P, KT, NE, P])
        w_fuse = sb("w_fuse", [P, KT, C])
        w_image = sb("w_image", [P, KT, C])
        w_att1 = sb("w_att1", [P, KT, HID])
        w_att2 = sb("w_att2", [HID, C])
        b_att1 = sb("b_att1", [HID, 1])
        vec = sb("edge_vec", [P, len(VEC), KT])
        bn_scale = sb("bn_scale", [P, NE])
        bn_shift = sb("bn_shift", [P, NE])
        z_shift = sb("z_shift", [P, KT])
        row_sum = sb("row_sum", [P, KT])
        pool_sum = sb("pool_sum", [P, NE, NCH])
        pooled = sb("pooled", [P, NE])
        hidden = sb("hidden", [HID, 1])
        gate = sb("gate", [P, KT])
        mean_w = sb("mean_w", [P, P])
        centred = sb("centred", [P, 2, KT, CH])
        square = sb("square", [P, KT, CH])
        std = sb("std", [P, CH])
        rstd = sb("rstd", [P, CH])
        x_out = sb("x_out", [P, 2, KT, CR * W2])
        eps = sb("edge_eps", [P, 3])

        const_loaded = sem("edge_const_loaded")
        ready = sem("edge_const_ready")
        mean_ready = sem("mean_ready")
        xb_loaded = [sem(f"xb_loaded{k}") for k in range(KT)]
        xb_used = [sem(f"xb_used{k}") for k in range(KT)]
        names = ["side", "vert", "dx", "smooth", "diag", "rows", "sobel_v", "sobel_h", "cross",
                 "squares", "sum", "sum_lap", "edges"]
        done = {n: sem(f"{n}_done") for n in names}
        branched = sem("branched")
        feat_ready = sem("feat_ready")
        pool_summed = sem("pool_summed")
        pooled_ready = sem("pooled_ready")
        hidden_mm = sem("hidden_mm")
        hidden_ready = sem("hidden_ready")
        gate_mm = sem("gate_mm")
        gate_ready = sem("gate_ready")
        image_ready = sem("image_ready")
        fused = sem("fused")
        z_evac = [sem(f"z_evac{m}") for m in range(KT)]
        squared = sem("squared")
        var_ready = sem("var_ready")
        std_ready = sem("std_ready")
        rstd_ready = sem("rstd_ready")
        normed = [sem("normed_v"), sem("normed_p")]
        activated = sem("activated")
        out_ready = sem("out_ready")
        x_out_loaded = [sem(f"x_out_loaded{i}") for i in range(2)]
        stored = [sem(f"out_stored{i}") for i in range(2)]

        Z_BANKS, VAR_BANK = banks[4:8], banks[0]

        def v(name):
            return vec[:, VEC.index(name), :]

        def before(b, j, k):
            return KT * NCH * b + KT * j + max(k - 1, 0)

        with nc.Block() as block:
            @block.sync
            def _(sp):
                for s in stored:
                    sp.sem_inc(s, 16 * START)
                for dst, src in ((w_branch[:, :, :, :].rearrange("p k e o -> p (k e o)"), io["branchT"]),
                                 (w_fuse[:, :, :].rearrange("p k o -> p (k o)"), io["fuseT"]),
                                 (w_att1[:, :, :].rearrange("p k o -> p (k o)"), io["att1T"]),
                                 (w_att2[:, :], io["att2T"]), (b_att1[:, :], io["b_att1"]),
                                 (vec[:, :, :].rearrange("p v m -> p (v m)"), io["vec"])):
                    sp.dma_start(dst, src).then_inc(const_loaded, 16)

                def load_out(b, j):
                    sp.dma_start(x_out[:, j % 2, :, :],
                                 dram["x2"][b].rearrange("m p n -> p m n")[:, :, (CR * j + 1) * W2:(CR * j + 1 + CR) * W2]
                                 ).then_inc(x_out_loaded[j % 2], 16)

                with sp.Fori(0, B) as b:
                    with sp.Fori(0, NCH) as j:
                        for k in range(KT):
                            sp.wait_ge(xb_used[k], START + NCH * b + j)
                            sp.dma_start(xb[:, k, :], dram["x2"][b][k][:, bass.ds(j * (CR * W2), XR * W2)]).then_inc(xb_loaded[k], 16)
                    for j in range(NCH):
                        if j < 2:
                            sp.wait_ge(out_ready, START + KT * NCH * b)
                            load_out(b, j)
                    for j in range(NCH):
                        sp.wait_ge(out_ready, START + KT * NCH * b + KT * (j + 1))
                        sp.dma_start(out[b].rearrange("(m p) n -> p m n", p=P)[:, :, j * CH:(j + 1) * CH],
                                     centred[:, j % 2, :, :]).then_inc(stored[j % 2], 16)
                        if j + 2 < NCH:
                            load_out(b, j + 2)
                for i in range(2):
                    sp.wait_ge(stored[i], 16 * START + 16 * B * NCH // 2)

            @block.tensor
            def _(pe):
                for s in (branched, fused, var_ready):
                    pe.sem_inc(s, START)
                pe.wait_ge(ready, 2)
                for k in range(KT):
                    last = nc.tensor.matmul(banks[4][:, 0:1], mean_w[:, :], v("b_fuse")[:, k:k + 1],
                                            start=(k == 0), stop=(k == KT - 1))
                last.then_inc(mean_ready, 1)

                def fuse(b, j):
                    for m in range(KT):
                        pe.wait_ge(z_evac[m], START + NCH * b + j)
                        for k in range(KT):
                            last = nc.tensor.matmul(Z_BANKS[m][:, :], w_image[:, k, m * P:(m + 1) * P],
                                                    feat[:, k, j * CH:(j + 1) * CH], start=(k == 0), stop=(k == KT - 1))
                        last.then_inc(fused, 1)

                def variance(b, j):
                    pe.wait_ge(std_ready, START + NCH * b + j)
                    for m in range(KT):
                        pe.wait_ge(squared, KT * NCH * b + KT * j + m + 1)
                        last = nc.tensor.matmul(VAR_BANK[:, :], mean_w[:, :], square[:, m, :],
                                                start=(m == 0), stop=(m == KT - 1))
                    last.then_inc(var_ready, 1)

                with pe.Fori(0, B) as b:
                    with pe.Fori(0, NCH) as j:
                        pe.wait_ge(std_ready, START + NCH * b)
                        pe.wait_ge(feat_ready, START + NE * NCH * b + NE * j)
                        for k in range(KT):
                            pe.wait_ge(done["edges"], START + KT * NCH * b + KT * j + k + 1)
                            for e in range(NE):
                                last = nc.tensor.matmul(banks[e][:, :], w_branch[:, k, e, :], edge[:, k % 2, e, :],
                                                        start=(k == 0), stop=(k == KT - 1))
                            last.then_inc(branched, 1)
                    pe.wait_ge(pooled_ready, b + 1)
                    for k in range(KT):
                        last = nc.tensor.matmul(banks[1][0:HID, 0:1], w_att1[:, k, :], pooled[:, k:k + 1],
                                                start=(k == 0), stop=(k == KT - 1))
                    last.then_inc(hidden_mm, 1)
                    pe.wait_ge(hidden_ready, b + 1)
                    for m in range(KT):
                        last = nc.tensor.matmul(banks[2][:, m:m + 1], w_att2[:, m * P:(m + 1) * P], hidden[:, 0:1],
                                                start=True, stop=True)
                    last.then_inc(gate_mm, 1)
                    pe.wait_ge(image_ready, KT * (b + 1))
                    for j in range(NCH + 1):
                        if j < NCH:
                            fuse(b, j)
                        if j >= 1:
                            variance(b, j - 1)

            @block.scalar
            def _(act):
                for s in [done["squares"], done["edges"], feat_ready, std_ready] + z_evac:
                    act.sem_inc(s, START)
                act.wait_ge(ready, 5)

                def squares(b, j, k):
                    s = k % 2
                    n = KT * NCH * b + KT * j + k + 1
                    act.wait_ge(branched, START + before(b, j, k))
                    act.wait_ge(done["sum_lap"], START + before(b, j, k))
                    act.wait_ge(done["diag"], n)
                    nc.scalar.activation(edge[:, s, 2, :].rearrange("p (r w) -> p r w", w=W), diag[:, s, :, :], ACT.Abs)
                    act.wait_ge(done["sobel_h"], n)
                    nc.scalar.activation(sobel_h[:, s, :, :], sobel_h[:, s, :, :], ACT.Square)
                    nc.scalar.activation(sobel_v[:, s, :, :], sobel_v[:, s, :, :], ACT.Square)
                    act.wait_ge(xb_used[k], START + NCH * b + j + 1)
                    nc.scalar.activation(lap_sq[:, s, :, :], lap[:, s, :, :], ACT.Square)
                    nc.scalar.activation(edge[:, s, 1, :].rearrange("p (r w) -> p r w", w=W), lap[:, s, :, :],
                                         ACT.Abs).then_inc(done["squares"], 1)

                def roots(b, j, k):
                    s = k % 2
                    n = KT * NCH * b + KT * j + k + 1
                    act.wait_ge(done["sum"], n)
                    nc.scalar.activation(edge[:, s, 0, :].rearrange("p (r w) -> p r w", w=W), sobel_v[:, s, :, :], ACT.Sqrt,
                                         bias=eps[:, 0:1])
                    act.wait_ge(done["sum_lap"], START + n)
                    nc.scalar.activation(edge[:, s, 3, :].rearrange("p (r w) -> p r w", w=W), lap_sq[:, s, :, :], ACT.Sqrt,
                                         bias=eps[:, 1:2]).then_inc(done["edges"], 1)

                def centre(b, j):
                    act.wait_ge(stored[j % 2], 16 * START + 16 * (NCH // 2) * b + 16 * (j // 2))
                    for m in range(KT):
                        act.wait_ge(fused, START + KT * NCH * b + KT * j + m + 1)
                        if m == 0:
                            act.wait_ge(var_ready, START + NCH * b + j)
                        nc.scalar.activation(square[:, m, :], Z_BANKS[m][:, :], ACT.Square,
                                             bias=z_shift[:, m:m + 1]).then_inc(squared, 1)
                        nc.scalar.activation(centred[:, j % 2, m, :], Z_BANKS[m][:, :], ACT.Identity,
                                             bias=z_shift[:, m:m + 1]).then_inc(z_evac[m], 1)

                def finish(b, j):
                    act.wait_ge(var_ready, START + NCH * b + j + 1)
                    act.wait_ge(rstd_ready, START + NCH * b + j)
                    nc.scalar.activation(std[:, :], VAR_BANK[:, :], ACT.Sqrt, bias=eps[:, 2:3]).then_inc(std_ready, 1)
                    for m in range(KT):
                        act.wait_ge(normed[m % 2], START + KT // 2 * (NCH * b + j) + m // 2 + 1)
                        nc.scalar.activation(centred[:, j % 2, m, :], centred[:, j % 2, m, :], ACT.Gelu,
                                             scale=v("ln_gamma")[:, m:m + 1], bias=v("ln_beta")[:, m:m + 1]).then_inc(activated, 1)

                with act.Fori(0, B) as b:
                    act.wait_ge(fused, START + KT * NCH * b)
                    with act.Fori(0, NCH) as j:
                        for k in range(KT + 1):
                            if k < KT:
                                squares(b, j, k)
                            if k >= 1:
                                roots(b, j, k - 1)
                        act.wait_ge(branched, START + KT * NCH * b + KT * j + KT)
                        for e in range(NE):
                            nc.scalar.activation(feat[:, e, bass.ds(j * CH, CH)], banks[e][:, :], ACT.Gelu,
                                                 scale=bn_scale[:, e:e + 1], bias=bn_shift[:, e:e + 1],
                                                 accum_out=pool_sum[:, e, bass.ds(j, 1)]).then_inc(feat_ready, 1)
                    act.wait_ge(hidden_mm, b + 1)
                    nc.scalar.activation(hidden[:, :], banks[1][0:HID, 0:1], ACT.Gelu, bias=b_att1[:, 0:1]).then_inc(hidden_ready, 1)
                    act.wait_ge(gate_mm, b + 1)
                    for m in range(KT):
                        nc.scalar.activation(gate[:, m:m + 1], banks[2][:, m:m + 1], ACT.Sigmoid,
                                             bias=v("b_att2")[:, m:m + 1]).then_inc(gate_ready, 1)
                    for j in range(NCH + 1):
                        if j < NCH:
                            centre(b, j)
                        if j >= 1:
                            finish(b, j - 1)

            @block.vector
            def _(dve):
                for s in [done["cross"], rstd_ready, normed[0], out_ready] + xb_used:
                    dve.sem_inc(s, START)
                nc.vector.memset(mean_w[:, :], 1.0 / C).then_inc(ready, 1)
                nc.vector.memset(eps[:, 0:1], EPS_GRAD)
                nc.vector.memset(eps[:, 1:2], 2 * EPS_GRAD)
                nc.vector.memset(eps[:, 2:3], EPS_LN)
                dve.wait_ge(const_loaded, 96)
                nc.vector.tensor_scalar(bn_scale[:, :], v("bn1_gamma"), float((1.0 + EPS_BN) ** -0.5), None,
                                        ALU.mult).then_inc(ready, 1)
                dve.wait_ge(ready, 2)
                nc.vector.tensor_tensor(bn_shift[:, :], bn_scale[:, :], v("b_branch"), ALU.mult).then_inc(ready, 1)
                dve.wait_ge(ready, 3)
                nc.vector.tensor_tensor(bn_shift[:, :], bn_shift[:, :], v("bn1_beta"), ALU.add).then_inc(ready, 1)
                dve.wait_ge(mean_ready, 1)
                nc.vector.tensor_scalar(z_shift[:, :], v("b_fuse"), banks[4][:, 0:1], None, ALU.subtract).then_inc(ready, 1)
                nc.vector.tensor_reduce(row_sum[:, :], w_fuse[:, :, :], AX_X, ALU.add).then_inc(ready, 1)
                dve.wait_ge(ready, 6)
                nc.vector.tensor_scalar(row_sum[:, :], row_sum[:, :], 1.0 / C, None, ALU.mult).then_inc(ready, 1)
                dve.wait_ge(ready, 7)
                for k in range(KT):
                    nc.vector.tensor_scalar(w_fuse[:, k, :], w_fuse[:, k, :], row_sum[:, k:k + 1], None,
                                            ALU.subtract).then_inc(ready, 1)

                def stencils(b, j, k):
                    s = k % 2
                    u = KT * NCH * b + KT * j + k
                    x = xb[:, k, :].rearrange("p (r w) -> p r w", w=W2)
                    dve.wait_ge(xb_loaded[k], 16 * NCH * b + 16 * j + 16)
                    nc.vector.tensor_tensor(dx[:, s, :, :], x[:, :, 2:W2], x[:, :, 0:W], ALU.subtract).then_inc(done["dx"], 1)
                    dve.wait_ge(done["side"], u + 1)
                    nc.vector.scalar_tensor_tensor(out=smooth[:, s, :, :], in0=x[:, :, 1:W + 1], scalar=2.0, in1=side[:, s, :, :],
                                                   op0=ALU.mult, op1=ALU.add).then_inc(done["smooth"], 1)
                    dve.wait_ge(done["dx"], u + 1)
                    dve.wait_ge(done["squares"], START + before(b, j, k))
                    nc.vector.tensor_tensor(diag[:, s, :, :], dx[:, s, 2:XR, :], dx[:, s, 0:CR, :], ALU.subtract).then_inc(done["diag"], 1)
                    dve.wait_ge(done["edges"], START + before(b, j, k))
                    nc.vector.tensor_tensor(sobel_h[:, s, :, :], dx[:, s, 2:XR, :], dx[:, s, 0:CR, :], ALU.add).then_inc(done["rows"], 1)
                    dve.wait_ge(done["smooth"], u + 1)
                    nc.vector.tensor_tensor(sobel_v[:, s, :, :], smooth[:, s, 2:XR, :], smooth[:, s, 0:CR, :],
                                            ALU.subtract).then_inc(done["sobel_v"], 1)
                    dve.wait_ge(done["rows"], u + 1)
                    nc.vector.scalar_tensor_tensor(out=sobel_h[:, s, :, :], in0=dx[:, s, 1:XR - 1, :], scalar=2.0,
                                                   in1=sobel_h[:, s, :, :], op0=ALU.mult, op1=ALU.add).then_inc(done["sobel_h"], 1)
                    dve.wait_ge(done["vert"], u + 1)
                    nc.vector.tensor_tensor(lap[:, s, :, :], lap[:, s, :, :], side[:, s, 1:XR - 1, :], ALU.add).then_inc(done["cross"], 1)
                    dve.wait_ge(done["cross"], START + u + 1)
                    nc.vector.scalar_tensor_tensor(out=lap[:, s, :, :], in0=x[:, 1:XR - 1, 1:W + 1], scalar=-4.0,
                                                   in1=lap[:, s, :, :], op0=ALU.mult, op1=ALU.add).then_inc(xb_used[k], 1)

                def norm(b, j):
                    dve.wait_ge(std_ready, START + NCH * b + j + 1)
                    dve.wait_ge(normed[1], START + KT // 2 * (NCH * b + j))
                    nc.vector.reciprocal(rstd[:, :], std[:, :]).then_inc(rstd_ready, 1)
                    dve.wait_ge(rstd_ready, START + NCH * b + j + 1)
                    for m in (0, 2):
                        dve.wait_ge(z_evac[m], START + NCH * b + j + 1)
                        nc.vector.tensor_tensor(centred[:, j % 2, m, :], centred[:, j % 2, m, :], rstd[:, :],
                                                ALU.mult).then_inc(normed[0], 1)

                def residual(b, j):
                    dve.wait_ge(x_out_loaded[j % 2], 16 * (NCH // 2) * b + 16 * (j // 2) + 16)
                    for m in range(KT):
                        dve.wait_ge(activated, KT * NCH * b + KT * j + m + 1)
                        y = centred[:, j % 2, m, :].rearrange("p (r w) -> p r w", w=W)
                        nc.vector.tensor_tensor(y, y, x_out[:, j % 2, m, :].rearrange("p (r w) -> p r w", w=W2)[:, :, 1:W + 1],
                                                ALU.add).then_inc(out_ready, 1)

                with dve.Fori(0, B) as b:
                    with dve.Fori(0, NCH) as j:
                        for k in range(KT):
                            stencils(b, j, k)
                    dve.wait_ge(feat_ready, START + NE * NCH * b + NE * NCH)
                    nc.vector.tensor_reduce(row_sum[:, :], pool_sum[:, :, :], AX_X, ALU.add).then_inc(pool_summed, 1)
                    dve.wait_ge(pool_summed, b + 1)
                    nc.vector.tensor_scalar(pooled[:, :], row_sum[:, :], 1.0 / N, None, ALU.mult).then_inc(pooled_ready, 1)
                    dve.wait_ge(gate_ready, KT * (b + 1))
                    for k in range(KT):
                        nc.vector.tensor_scalar(w_image[:, k, :], w_fuse[:, k, :], gate[:, k:k + 1], None,
                                                ALU.mult).then_inc(image_ready, 1)
                    for j in range(NCH):
                        norm(b, j)
                        residual(b, j)

            @block.gpsimd
            def _(pool):
                def neighbours(b, j, k):
                    s = k % 2
                    x = xb[:, k, :].rearrange("p (r w) -> p r w", w=W2)
                    pool.wait_ge(xb_loaded[k], 16 * NCH * b + 16 * j + 16)
                    pool.wait_ge(done["cross"], START + before(b, j, k))
                    nc.gpsimd.tensor_tensor(side[:, s, :, :], x[:, :, 0:W], x[:, :, 2:W2], ALU.add).then_inc(done["side"], 1)
                    pool.wait_ge(done["squares"], START + before(b, j, k))
                    nc.gpsimd.tensor_tensor(lap[:, s, :, :], x[:, 0:CR, 1:W + 1], x[:, 2:XR, 1:W + 1], ALU.add).then_inc(done["vert"], 1)

                def sums(b, j, k):
                    s = k % 2
                    n = KT * NCH * b + KT * j + k + 1
                    pool.wait_ge(done["squares"], START + n)
                    nc.gpsimd.tensor_tensor(sobel_v[:, s, :, :], sobel_v[:, s, :, :], sobel_h[:, s, :, :], ALU.add).then_inc(done["sum"], 1)
                    pool.wait_ge(done["sum"], n)
                    nc.gpsimd.tensor_tensor(lap_sq[:, s, :, :], lap_sq[:, s, :, :], sobel_v[:, s, :, :], ALU.add).then_inc(done["sum_lap"], 1)

                for s in (done["sum_lap"], normed[1]):
                    pool.sem_inc(s, START)
                with pool.Fori(0, B) as b:
                    with pool.Fori(0, NCH) as j:
                        for k in range(KT + 1):
                            if k < KT:
                                neighbours(b, j, k)
                            if k >= 1:
                                sums(b, j, k - 1)
                    for j in range(NCH):
                        pool.wait_ge(rstd_ready, START + NCH * b + j + 1)
                        for m in (1, 3):
                            pool.wait_ge(z_evac[m], START + NCH * b + j + 1)
                            nc.gpsimd.tensor_tensor(centred[:, j % 2, m, :], centred[:, j % 2, m, :], rstd[:, :],
                                                    ALU.mult).then_inc(normed[1], 1)


def program(nc, io, out):
    dram = {
        "taps": nc.dram_tensor("taps_dram", [HS, P, 3 * SH * GT], F32, kind="Internal").ap(),
        "tiles": nc.dram_tensor("tiles_dram", [3, P, PL, TN], F32, kind="Internal").ap(),
        "conv_q": nc.dram_tensor("conv_q_dram", [SH, M, TT], F32, kind="Internal").ap(),
        "att": nc.dram_tensor("att_dram", [B, TILES, P, N], F32, kind="Internal").ap(),
        "x2": nc.dram_tensor("x2_dram", [B, KT, P, H2 * W2], F32, kind="Internal").ap(),
    }
    with ExitStack() as ctx:
        banks = [ctx.enter_context(nc.psum_tensor(f"bank{i}", [P, CH], F32)) for i in range(8)]
        prepare(nc, banks, io, dram)
        attention(nc, banks, io, dram)
        project(nc, banks, io, dram)
        edges(nc, banks, io, dram, out)


def kernel(x, L0_conv_wq, L0_conv_wk, L0_conv_wv, L0_conv_dw_kernel, L0_conv_pw_kernel, L0_conv_proj_kernel,
           L0_conv_bn_gamma, L0_conv_bn_beta, L0_conv_bn_mean, L0_conv_bn_var, L1_conv_w_branch, L1_conv_b_branch,
           L1_conv_bn_gamma, L1_conv_bn_beta, L1_conv_w_att1, L1_conv_b_att1, L1_conv_w_att2, L1_conv_b_att2,
           L1_conv_w_fuse, L1_conv_b_fuse, L1_conv_ln_gamma, L1_conv_ln_beta):
    import numpy as np
    import concourse.bacc as bacc
    from concourse.bass_utils import run_bass_kernel_spmd

    def a(t):
        return np.asarray(t)

    w = np.concatenate([a(L0_conv_wq), a(L0_conv_wk), a(L0_conv_wv)], 0)
    tap_sel = np.zeros((HD, KS, TS, 2, TS, HD, TS, TS), np.float32)
    row_rep = np.zeros((HD, HD, PL), np.float32)
    for i in range(HD):
        row_rep[i, i, :] = 1
        for sy in range(2):
            for oy in range(TS):
                for ry in range(TS):
                    if 0 <= ry + TS * sy - oy < KS:
                        for rx in range(TS):
                            tap_sel[i, ry + TS * sy - oy, rx, sy, oy, i, ry, rx] = 1
    vectors = [a(L0_conv_bn_gamma), a(L0_conv_bn_beta), a(L0_conv_bn_mean), a(L0_conv_bn_var),
               a(L1_conv_b_branch).reshape(C), a(L1_conv_bn_gamma).reshape(C), a(L1_conv_bn_beta).reshape(C),
               a(L1_conv_b_att2), a(L1_conv_b_fuse), a(L1_conv_ln_gamma), a(L1_conv_ln_beta)]
    arrays = {
        "x": a(x).reshape(B, C, N),
        "wT": w.reshape(HS, SH, 3, HD, KT, P).transpose(0, 5, 4, 2, 1, 3).reshape(HS, P, KT * 3 * P),
        "dwT": a(L0_conv_dw_kernel).reshape(NG, HD, KS, KS).transpose(1, 2, 0, 3).reshape(HD * KS, NG * KS),
        "pwT": a(L0_conv_pw_kernel).reshape(NG, HD, HD).transpose(2, 0, 1).reshape(HD, NG * HD),
        "projT": a(L0_conv_proj_kernel).reshape(C, TILES, P).transpose(2, 1, 0).reshape(P, TILES * C),
        "branchT": a(L1_conv_w_branch).reshape(NE, P, KT, P).transpose(3, 2, 0, 1).reshape(P, KT * NE * P),
        "fuseT": a(L1_conv_w_fuse).reshape(C, KT, P).transpose(2, 1, 0).reshape(P, KT * C),
        "att1T": a(L1_conv_w_att1).reshape(HID, KT, P).transpose(2, 1, 0).reshape(P, KT * HID),
        "att2T": a(L1_conv_w_att2).T,
        "b_att1": a(L1_conv_b_att1).reshape(HID, 1),
        "vec": np.stack(vectors).reshape(len(VEC), KT, P).transpose(2, 0, 1).reshape(P, len(VEC) * KT),
        "tap_sel": tap_sel.reshape(HD * KS, TS * 2 * TS * P),
        "row_rep": row_rep.reshape(HD, P),
        "ident": np.eye(P, dtype=np.float32),
        "head_mask": np.kron(np.eye(SH, dtype=np.float32), np.ones((HD, HD), np.float32)),
    }
    nc = bacc.Bacc("TRN2", target_bir_lowering=False, num_devices=1)
    feeds, io = {}, {}
    for name, value in arrays.items():
        feeds[f"in_{name}"] = np.ascontiguousarray(value)
        io[name] = nc.dram_tensor(f"in_{name}", value.shape, F32, kind="ExternalInput").ap()
    out = nc.dram_tensor("out", (B, C, N), F32, kind="ExternalOutput").ap()
    program(nc, io, out)
    result = run_bass_kernel_spmd(nc, [feeds], core_ids=[0])
    return result.results[0]["out"].reshape(B, C, H, W)
```

```python
from contextlib import ExitStack

import concourse.bass as bass
from concourse import mybir

F32 = mybir.dt.float32
F32R = mybir.dt.float32r
ALU = mybir.AluOpType
ACT = mybir.ActivationFunctionType
AX_X = mybir.AxisListType.X

P = 128
B, C, H, W = 4, 512, 64, 64
N = H * W
KT = C // P
HD = 8
HEADS = C // HD
HS = 4
SH = HEADS // HS
CH = 512
NCH = N // CH
CR = CH // W
KS = 5
HALO = KS // 2
TS = 4
PL = TS * TS
TG = (H + 2 * HALO) // TS
TN = TG * TG
TO = H // TS
TT = TO * TO
HV = TT // P
HT = P // TO
SHIFTS = [(a, b) for a in range(2) for b in range(2)]
M = HD * PL
NTAP = len(SHIFTS) * PL
GT = NTAP + HD
BLOCKS = TN * PL // P
SKIP = TN * PL % P
TURNS = BLOCKS // 4
NG = 3 * HEADS
IT = B * HS
TILES = 2 * HS
EPS_ATT, EPS_BN, EPS_LN, EPS_GRAD = 1e-15, 1e-5, 1e-6, 1e-8
NE = 4
H2, W2 = H + 2, W + 2
HID = C // 8
START = 2
VEC = ["bn0_gamma", "bn0_beta", "bn0_mean", "bn0_var", "b_branch", "bn1_gamma", "bn1_beta",
       "b_att2", "b_fuse", "ln_gamma", "ln_beta"]


def prepare(nc, banks, io, dram):
    with ExitStack() as ctx:
        def sb(name, shape):
            return ctx.enter_context(nc.sbuf_tensor(name, shape, F32))

        def sem(name):
            return ctx.enter_context(nc.semaphore(name))

        dw_sb = sb("dw_sb", [HD * KS, NG * KS])
        pw_sb = sb("pw_sb", [HD, NG * HD])
        sel_sb = sb("sel_sb", [HD * KS, TS, 2 * TS, P])
        rep_sb = sb("rep_sb", [HD, P])
        taps_sb = sb("taps_sb", [P, NG, GT])
        zeros = sb("zeros", [P, KT * W2])
        sel_r = ctx.enter_context(nc.sbuf_tensor("sel_r", [HD * KS, TS, 2 * TS, P], F32R))
        rep_r = ctx.enter_context(nc.sbuf_tensor("rep_r", [HD, P], F32R))
        dw_parts = [ctx.enter_context(nc.sbuf_tensor(f"dw_{n}", [HD * KS, KS * NG], F32R)) for n in ("hi", "lo")]
        pw_parts = [ctx.enter_context(nc.sbuf_tensor(f"pw_{n}", [HD, NG * HD], F32R)) for n in ("hi", "lo")]
        rounded = sem("prep_rounded")
        split = sem("prep_split")
        loaded = sem("prep_loaded")
        zeroed = sem("prep_zeroed")
        product = sem("prep_product")
        copied = sem("prep_copied")
        stored = sem("prep_stored")
        points = [(a, b, oy, ox) for a, b in SHIFTS for oy in range(TS) for ox in range(TS)]
        NP = NTAP // 2
        PC = NG * HD // 3

        with nc.Block() as block:
            @block.sync
            def _(sp):
                sp.dma_start(dw_sb[:, :], io["dwT"]).then_inc(loaded, 16)
                sp.dma_start(pw_sb[:, :], io["pwT"]).then_inc(loaded, 16)
                sp.dma_start(sel_sb[:, :, :, :].rearrange("k r o p -> k (r o p)"), io["tap_sel"]).then_inc(loaded, 16)
                sp.dma_start(rep_sb[:, :], io["row_rep"]).then_inc(loaded, 16)
                sp.wait_ge(zeroed, 1)
                for b in range(B):
                    for row in (0, H2 - 1):
                        sp.dma_start(dram["x2"][b].rearrange("m p n -> p m n")[:, :, row * W2:(row + 1) * W2],
                                     zeros[:, 0:KT * W2].rearrange("p (m w) -> p m w", w=W2)).then_inc(stored, 16)
                sp.wait_ge(copied, NP + 3)
                for hs in range(HS):
                    sp.dma_start(dram["taps"][hs],
                                 taps_sb[:, hs * 3 * SH:(hs + 1) * 3 * SH, :].rearrange("p g t -> p (g t)")).then_inc(stored, 16)
                sp.wait_ge(stored, 16 * (2 * B + HS))

            @block.tensor
            def _(pe):
                pe.wait_ge(split, 4)
                for n in range(NP):
                    if n >= 8:
                        pe.wait_ge(copied, n - 7)
                    for i in range(2):
                        a, b, oy, ox = points[2 * n + i]
                        cols = [(dx, dx - TS * b + ox) for dx in range(KS) if 0 <= dx - TS * b + ox < TS]
                        for dx, rx in cols:
                            for part in range(2):
                                last = nc.tensor.matmul(banks[n % 8][:, i * NG:(i + 1) * NG], sel_r[:, rx, TS * a + oy, :],
                                                        dw_parts[part][:, dx * NG:(dx + 1) * NG],
                                                        start=(dx == cols[0][0] and part == 0),
                                                        stop=(dx == cols[-1][0] and part == 1))
                    last.then_inc(product, 1)
                for n in range(3):
                    pe.wait_ge(copied, NP + n - 7)
                    for part in range(2):
                        last = nc.tensor.matmul(banks[(NP + n) % 8][:, 0:PC], rep_r[:, :],
                                                pw_parts[part][:, n * PC:(n + 1) * PC], start=(part == 0), stop=(part == 1))
                    last.then_inc(product, 1)

            @block.scalar
            def _(act):
                act.wait_ge(loaded, 64)
                nc.scalar.activation(sel_r[:, :, :, :].rearrange("k r o p -> k (r o p)"),
                                     sel_sb[:, :, :, :].rearrange("k r o p -> k (r o p)"), ACT.Copy).then_inc(split, 1)
                nc.scalar.activation(rep_r[:, :], rep_sb[:, :], ACT.Copy).then_inc(split, 1)

            @block.vector
            def _(dve):
                nc.vector.memset(zeros[:, :], 0.0).then_inc(zeroed, 1)
                dve.wait_ge(loaded, 64)
                for n, (source, (hi, lo)) in enumerate(((dw_sb, dw_parts), (pw_sb, pw_parts))):
                    nc.vector.tensor_copy(hi[:, :], source[:, :]).then_inc(rounded, 1)
                    dve.wait_ge(rounded, n + 1)
                    nc.vector.tensor_tensor(lo[:, :], source[:, :], hi[:, :].bitcast(F32), ALU.subtract).then_inc(split, 1)
                for n in range(NP):
                    dve.wait_ge(product, n + 1)
                    nc.vector.tensor_copy(taps_sb[:, :, 2 * n:2 * n + 2],
                                          banks[n % 8][:, 0:2 * NG].rearrange("p (n g) -> p g n", g=NG)).then_inc(copied, 1)
                for n in range(3):
                    dve.wait_ge(product, NP + n + 1)
                    nc.vector.tensor_copy(
                        taps_sb[:, n * NG // 3:(n + 1) * NG // 3, NTAP:GT],
                        banks[(NP + n) % 8][:, 0:PC].rearrange("p (g o) -> p g o", o=HD)).then_inc(copied, 1)


def attention(nc, banks, io, dram):
    with ExitStack() as ctx:
        def sb(name, shape):
            return ctx.enter_context(nc.sbuf_tensor(name, shape, F32))

        def sem(name):
            return ctx.enter_context(nc.semaphore(name))

        XR = 2
        with nc.sbuf_tensor("x_sb", [P, XR, KT, CH], F32) as x_sb:
            pass
        x_lo = ctx.enter_context(nc.sbuf_tensor("x_lo", [P, XR, KT, CH], F32R))
        x_hi = ctx.enter_context(nc.sbuf_tensor("x_hi", [P, XR, KT, CH], F32R))
        with nc.sbuf_tensor("w_sb", [P, KT, 3, P], F32) as w_sb:
            pass
        w_lo = ctx.enter_context(nc.sbuf_tensor("w_lo", [P, KT, 3, P], F32R))
        w_hi = ctx.enter_context(nc.sbuf_tensor("w_hi", [P, KT, 3, P], F32R))
        taps = sb("taps", [P, 3 * SH, GT])
        tiles = [sb(f"{n}_tiles", [P, PL, TN]) for n in "qkv"]
        relu_q = sb("relu_q", [P, PL, TT])
        key_t = sb("key_t", [P, 2, 4, P])
        value_t = sb("value_t", [P, 2, 4, P + 1])
        ckey_t = sb("ckey_t", [P, HV * PL, P])
        cvalue_t = sb("cvalue_t", [P, HV * PL, P + 1])
        loaded = sb("loaded", [P, 2, 3, TN])
        columns = sb("columns", [P, 2, 2, HV + 1, TG * HT])
        toeplitz = sb("toeplitz", [P, 2, 3, len(SHIFTS) * M])
        q_stage = sb("q_stage", [M, 2, TT])
        score_n = sb("score_n", [P, 2, P])
        score_d = sb("score_d", [P, 2, P])
        key_sum = sb("key_sum", [P, 1])
        den_sb = sb("den_sb", [P, CH])
        out_sb = sb("out_sb", [P, CH])
        ident = sb("ident", [P, P])
        mask = sb("mask", [P, P])

        const_loaded = sem("att_const_loaded")
        cleared = sem("att_cleared")
        x_loaded = [sem(f"x_loaded{i}") for i in range(XR)]
        x_rounded = sem("x_rounded")
        x_split = [sem("x_split_v"), sem("x_split_p")]
        w_loaded = sem("w_loaded")
        w_rounded = sem("w_rounded")
        w_split = sem("w_split")
        taps_loaded = sem("taps_loaded")
        qkv_ready = sem("qkv_ready")
        evac = [sem(f"{n}_evacuated") for n in "qkv"]
        relu_q_ready = sem("relu_q_ready")
        turned = sem("turned")
        key_t_ready = sem("key_t_ready")
        value_t_ready = sem("value_t_ready")
        chunk_scored = sem("chunk_scored")
        scores_ready = sem("scores_ready")
        key_sum_ready = sem("key_sum_ready")
        scores_masked = sem("scores_masked")
        attended = sem("attended")
        den_evac = sem("den_evac")
        inverted = sem("inverted")
        divided = sem("divided")
        out_written = sem("out_written")
        tiles_loaded = [sem(f"tiles_loaded{i}") for i in range(2)]
        columns_ready = [sem(f"columns_ready{i}") for i in range(2)]
        head_done = [sem(f"head_done{i}") for i in range(2)]
        toeplitz_ready = sem("toeplitz_ready")
        cready = [sem(f"conv_{n}_ready") for n in "qk"]
        cevac = [sem(f"conv_{n}_evacuated") for n in "qkv"]
        q_written = [sem(f"q_written{i}") for i in range(2)]
        conv_q_loaded = sem("conv_q_loaded")

        T_Q, T_K, T_V = range(3)
        X_DVE, X_POOL = slice(0, KT - 1), slice(KT - 1, KT)
        FIRST_TURN = NCH
        KEY_BANK, VALUE_BANK, SCORE_BANK = banks[3], banks[4], banks[5]
        NUM_BANK, DEN_BANK = banks[6], banks[7]

        def at(it, half, j):
            return 2 * NCH * it + NCH * half + j

        def pairs(eng, first, steady, final):
            first()
            with eng.Fori(0, IT - 1) as it:
                steady(it)
            final(IT - 1)

        def spread(engine_op, j, t):
            for r, n, y, a in ((0, TS - HALO, HALO, 2 * j), (TS - HALO, TS, 0, 2 * j + 1), (CR - HALO, HALO, 0, 2 * j + 2)):
                for x in range(2):
                    last = engine_op(
                        tiles[t][:, :, :].rearrange("p (i h k) (a c) -> p h i k a c", h=2, k=TS // 2, c=TG)
                        [:, 1 - x, y:y + n, :, a, x:x + TO],
                        banks[t][:, :].rearrange("p (i c g k) -> p g i k c", c=TO, g=2, k=TS // 2)[:, x, r:r + n, :, :])
            return last

        def eighths(j):
            for y, x, a in [(y, x, a) for y in range(2) for x in range(2) for a in range(CR // TS)]:
                yield (tiles[0][:, :, :].rearrange("p (g i h k) (a c) -> p g h i k a c", g=2, i=2, h=2, c=TG)
                       [:, 1 - y, 1 - x, :, :, 2 * j + y + a, x:x + TO],
                       relu_q[:, :, :].rearrange("p (g i h k) (a c) -> p g h i k a c", g=2, i=2, h=2, c=TO)
                       [:, y, x, :, :, 2 * j + a, :])

        with nc.Block() as block:
            @block.sync
            def _(sp):
                def load_x(it, j):
                    sp.dma_start(x_sb[:, j % XR, :, :],
                                 io["x"][it // HS].rearrange("(k p) n -> p k n", p=P)[:, :, j * CH:(j + 1) * CH]
                                 ).then_inc(x_loaded[j % XR], 16)

                def load_weights(it):
                    sp.dma_start(w_sb[:, :, :, :].rearrange("p k t m -> p (k t m)"), io["wT"][it % HS]).then_inc(w_loaded, 16)

                def load_taps(it):
                    sp.dma_start(taps[:, :, :].rearrange("p g t -> p (g t)"), dram["taps"][it % HS]).then_inc(taps_loaded, 16)

                def load_tiles(head):
                    for t in range(3):
                        sp.dma_start(loaded[:, head % 2, t, :], tiles[t][head * HD:(head + 1) * HD, :, :]
                                     ).then_inc(tiles_loaded[head % 2], 16)

                def write_q(it, jj, par):
                    sp.wait_ge(cevac[T_Q], START + SH * it + 2 * jj + par + 1)
                    sp.dma_start(dram["conv_q"][2 * jj + par], q_stage[:, par, :]).then_inc(q_written[par], 16)

                def spill(it, half, j):
                    sp.wait_ge(divided, START + at(it, half, j) + 1)
                    sp.dma_start(dram["att"][it // HS][it % HS + HS * half][:, j * CH:(j + 1) * CH],
                                 out_sb[:, :]).then_inc(out_written, 16)

                def plain(it, conv_of):
                    for j in range(XR, NCH):
                        sp.wait_ge(qkv_ready, 3 * (NCH * it + j - XR + 1))
                        load_x(it, j)
                        if conv_of is not None:
                            spill(conv_of, 1, j - XR)
                    if conv_of is not None:
                        spill(conv_of, 1, NCH - 2)
                    for t in range(3):
                        sp.wait_ge(evac[t], NCH * (it + 1))
                    for head in range(2):
                        load_tiles(head)
                    if conv_of is not None:
                        spill(conv_of, 1, NCH - 1)

                def conv(it, last):
                    for jj in range(SH // 2):
                        for par in range(2):
                            write_q(it, jj, par)
                            if jj + 1 < SH // 2:
                                sp.wait_ge(head_done[par], START + SH // 2 * it + jj + 1)
                                load_tiles(2 * (jj + 1) + par)
                        if not last and jj == 1:
                            load_weights(it + 1)
                        if not last and 2 <= jj < 2 + XR:
                            load_x(it + 1, jj - 2)
                        if jj + 1 < SH // 2:
                            spill(it, 0, jj)
                    if not last:
                        sp.wait_ge(toeplitz_ready, SH * (it + 1))
                        load_taps(it + 1)
                    for par in range(2):
                        sp.wait_ge(q_written[par], 16 * START + 16 * (SH // 2) * (it + 1))
                    sp.wait_ge(attended, at(it, 1, 0))
                    sp.dma_start(relu_q[:, :, :],
                                 dram["conv_q"].rearrange("j (o r) s -> (j o) r s", o=HD)).then_inc(conv_q_loaded, 16)
                    spill(it, 0, NCH - 1)

                def first():
                    for s in [out_written] + q_written:
                        sp.sem_inc(s, 16 * START)
                    load_weights(0)
                    for j in range(XR):
                        load_x(0, j)
                    sp.dma_start(ident[:, :], io["ident"]).then_inc(const_loaded, 16)
                    sp.dma_start(mask[:, :], io["head_mask"]).then_inc(const_loaded, 16)
                    load_taps(0)
                    plain(0, None)

                def steady(it):
                    conv(it, False)
                    plain(it + 1, it)

                def final(it):
                    conv(it, True)
                    for j in range(NCH):
                        spill(it, 1, j)
                    sp.wait_ge(out_written, 16 * START + 16 * at(IT, 0, 0))

                pairs(sp, first, steady, final)

            @block.tensor
            def _(pe):
                def qkv(it, j):
                    for part in x_split:
                        pe.wait_ge(part, NCH * it + j + 1)
                    for t in range(3):
                        pe.wait_ge(evac[t], NCH * it + j)
                        for k in range(KT):
                            wh, wl, xh, xl = w_hi[:, k, t, :], w_lo[:, k, t, :], x_hi[:, j % XR, k, :], x_lo[:, j % XR, k, :]
                            nc.tensor.matmul(banks[t][:, :], wh, xh, start=(k == 0), stop=False)
                            nc.tensor.matmul(banks[t][:, :], wl, xh, start=False, stop=False)
                            last = nc.tensor.matmul(banks[t][:, :], wh, xl, start=False, stop=(k == KT - 1))
                        last.then_inc(qkv_ready, 1)

                def turn(it, g):
                    for t in (T_K, T_V):
                        pe.wait_ge(evac[t], NCH * (it + 1))
                    pe.wait_ge(key_t_ready, TURNS * it + g)
                    pe.wait_ge(value_t_ready, TURNS * it + g)
                    for t, bank in ((T_K, KEY_BANK), (T_V, VALUE_BANK)):
                        for n in range(4):
                            block = tiles[t][:, :, :].rearrange("p r s -> p (r s)")
                            block = block[:, SKIP + (4 * g + n) * P:SKIP + (4 * g + n + 1) * P]
                            last = nc.tensor.matmul(bank[:, n * P:(n + 1) * P], block, ident[:, :],
                                                    start=True, stop=True, is_transpose=True)
                    last.then_inc(turned, 1)

                def score(it, g):
                    pe.wait_ge(key_t_ready, TURNS * it + g + 1)
                    pe.wait_ge(value_t_ready, TURNS * it + g + 1)
                    for n in range(4):
                        last = nc.tensor.matmul(SCORE_BANK[:, 0:P + 1], key_t[:, g % 2, n, :], value_t[:, g % 2, n, :],
                                                start=(g == 0 and n == 0), stop=(g == TURNS - 1 and n == 3))
                    last.then_inc(chunk_scored, 1)

                def attend(it, half, j):
                    pe.wait_ge(scores_masked, 2 * it + half + 1)
                    if half == 0:
                        pe.wait_ge(relu_q_ready, NCH * it + j + 1)
                    else:
                        pe.wait_ge(conv_q_loaded, 16 * (it + 1))
                    pe.wait_ge(den_evac, START + at(it, half, j))
                    pe.wait_ge(divided, START + at(it, half, j))
                    for bank, score in ((DEN_BANK, score_d), (NUM_BANK, score_n)):
                        for y in range(2):
                            q = relu_q[:, :, :].rearrange("p (r x) (a c) -> p a r c x", x=TS, c=TO)
                            last = nc.tensor.matmul(bank[:, y * TS * W:(y + 1) * TS * W], score[:, half, :],
                                                    q[:, bass.ds(2 * j + y, 1), :, :, :], start=True, stop=True)
                    last.then_inc(attended, 1)

                def plain(it, conv_of):
                    pe.wait_ge(w_split, it + 1)
                    for step in range(FIRST_TURN + TURNS + 1):
                        if step < NCH:
                            qkv(it, step)
                            if conv_of is not None:
                                attend(conv_of, 1, step)
                        if 0 <= step - FIRST_TURN < TURNS:
                            turn(it, step - FIRST_TURN)
                        if 0 <= step - FIRST_TURN - 1:
                            score(it, step - FIRST_TURN - 1)

                def conv(it):
                    with pe.Fori(0, SH // 2) as jj:
                        for par in range(2):
                            pe.wait_ge(tiles_loaded[par], SH // 2 * 48 * it + 48 * jj + 48)
                            pe.wait_ge(toeplitz_ready, SH * it + 2 * jj + par + 1)
                            x_q = loaded[:, par, T_Q, :].rearrange("p (a c) -> p a c", c=TG)
                            w = toeplitz[:, par, :, :].rearrange("p t (d m) -> p t d m", m=M)
                            pe.wait_ge(cevac[T_Q], START + SH * it + 2 * jj + par)
                            for d, (a, b) in enumerate(SHIFTS):
                                last = nc.tensor.matmul(banks[T_Q][0:M, 0:TT], w[:, T_Q, d, :], x_q[:, a:a + TO, b:b + TO],
                                                        start=(d == 0), stop=(d == len(SHIFTS) - 1))
                            last.then_inc(cready[T_Q], 1)
                            pe.wait_ge(columns_ready[par], SH // 2 * it + jj + 1)
                            for t in (T_K, T_V):
                                pe.wait_ge(cevac[t], START + SH * it + 2 * jj + par)
                                for h in range(HV):
                                    for d, (a, b) in enumerate(SHIFTS):
                                        last = nc.tensor.matmul(banks[t][:, h * M:(h + 1) * M],
                                                                columns[:, par, t - T_K, h + b, a * HT:(a + TO) * HT],
                                                                w[:, t, d, :], start=(d == 0), stop=(d == len(SHIFTS) - 1))
                                last.then_inc(cready[t] if t == T_K else head_done[par], 1)
                        attend(it, 0, jj)
                    pe.wait_ge(cevac[T_K], START + SH * (it + 1))
                    pe.wait_ge(cevac[T_V], START + SH * (it + 1))
                    for n in range(HV * PL):
                        last = nc.tensor.matmul(SCORE_BANK[:, 0:P + 1], ckey_t[:, n, :], cvalue_t[:, n, :],
                                                start=(n == 0), stop=(n == HV * PL - 1))
                    last.then_inc(scores_ready, 1)

                def first():
                    for s in head_done:
                        pe.sem_inc(s, START)
                    pe.wait_ge(const_loaded, 32)
                    plain(0, None)

                def steady(it):
                    conv(it)
                    plain(it + 1, it)

                def final(it):
                    conv(it)
                    for j in range(NCH):
                        attend(it, 1, j)

                pairs(pe, first, steady, final)

            @block.scalar
            def _(act):
                def copy(to, source):
                    return nc.scalar.activation(to, source, ACT.Copy)

                def round_x(it, j):
                    act.wait_ge(x_loaded[j % XR], 16 * (NCH // XR) * it + 16 * (j // XR + 1))
                    if j >= XR:
                        act.wait_ge(qkv_ready, 3 * NCH * it + 3 * (j - XR + 1))
                    for tiles_of in (X_POOL, X_DVE):
                        copy(x_hi[:, j % XR, tiles_of, :], x_sb[:, j % XR, tiles_of, :]).then_inc(x_rounded, 1)

                def evacuate(it, j):
                    act.wait_ge(qkv_ready, 3 * NCH * it + 3 * j + T_Q + 1)
                    spread(copy, j, T_Q).then_inc(evac[T_Q], 1)
                    act.wait_ge(qkv_ready, 3 * NCH * it + 3 * j + T_K + 1)
                    spread(copy, j, T_K).then_inc(evac[T_K], 1)

                def value_by_position(it, g):
                    act.wait_ge(turned, TURNS * it + g + 1)
                    act.wait_ge(chunk_scored, TURNS * it + max(g - 1, 0))
                    nc.scalar.activation(value_t[:, g % 2, :, 0:P], VALUE_BANK[:, :].rearrange("p (n m) -> p n m", m=P),
                                         ACT.Copy).then_inc(value_t_ready, 1)

                def denominators(it, half, j):
                    act.wait_ge(attended, at(it, half, j) + 1)
                    act.wait_ge(divided, START + at(it, half, j))
                    nc.scalar.activation(den_sb[:, :], DEN_BANK[:, :], ACT.Copy, bias=EPS_ATT).then_inc(den_evac, 1)

                def plain(it, conv_of):
                    for step in range(FIRST_TURN + TURNS):
                        if step < NCH:
                            evacuate(it, step)
                            if conv_of is not None:
                                denominators(conv_of, 1, step)
                            if step + XR < NCH:
                                round_x(it, step + XR)
                        if step >= FIRST_TURN:
                            value_by_position(it, step - FIRST_TURN)

                def conv(it):
                    with act.Fori(0, SH // 2) as jj:
                        for par in range(2):
                            act.wait_ge(tiles_loaded[par], SH // 2 * 48 * it + 48 * jj + 48)
                            act.wait_ge(head_done[par], START + SH // 2 * it + jj)
                            for h in range(HV + 1):
                                last = nc.scalar.activation(
                                    columns[:, par, :, h, :].rearrange("p t (a v) -> p t a v", v=HT),
                                    loaded[:, par, T_K:, :].rearrange("p t (a c) -> p t a c", c=TG)[:, :, :, h:h + TO - 1:HV],
                                    ACT.Copy)
                            last.then_inc(columns_ready[par], 1)
                        for par in range(2):
                            act.wait_ge(cready[T_Q], SH * it + 2 * jj + par + 1)
                            act.wait_ge(q_written[par], 16 * START + SH // 2 * 16 * it + 16 * jj)
                            nc.scalar.activation(q_stage[:, par, :], banks[T_Q][0:M, 0:TT], ACT.Relu).then_inc(cevac[T_Q], 1)
                            act.wait_ge(head_done[par], START + SH // 2 * it + jj + 1)
                            to = cvalue_t[:, :, bass.ds((2 * jj + par) * HD, HD)].rearrange("p (s r) o -> p s r o", s=HV)
                            nc.scalar.activation(to, banks[T_V][:, 0:HV * M].rearrange("p (s o r) -> p s r o", o=HD, r=PL),
                                                 ACT.Copy).then_inc(cevac[T_V], 1)
                        denominators(it, 0, jj)

                def first():
                    for s in (cevac[T_Q], cevac[T_V], den_evac):
                        act.sem_inc(s, START)
                    for j in range(XR):
                        round_x(0, j)
                    act.wait_ge(cleared, 4)
                    plain(0, None)

                def steady(it):
                    conv(it)
                    for j in range(XR):
                        round_x(it + 1, j)
                    plain(it + 1, it)

                def final(it):
                    conv(it)
                    for j in range(NCH):
                        denominators(it, 1, j)

                pairs(act, first, steady, final)

            @block.vector
            def _(dve):
                def keys_by_position(it, g):
                    dve.wait_ge(turned, TURNS * it + g + 1)
                    dve.wait_ge(chunk_scored, TURNS * it + max(g - 1, 0))
                    nc.vector.tensor_scalar(key_t[:, g % 2, :, :].rearrange("p n m -> p (n m)"), KEY_BANK[:, :],
                                            0.0, None, ALU.max).then_inc(key_t_ready, 1)

                def mask_scores(it, half):
                    if half:
                        dve.wait_ge(scores_ready, it + 1)
                    else:
                        dve.wait_ge(chunk_scored, TURNS * (it + 1))
                    nc.vector.tensor_copy(key_sum[:, :], SCORE_BANK[:, P:P + 1]).then_inc(key_sum_ready, 1)
                    nc.vector.tensor_tensor(score_n[:, half, :], SCORE_BANK[:, 0:P], mask[:, :], ALU.mult)
                    dve.wait_ge(key_sum_ready, 2 * it + half + 1)
                    nc.vector.tensor_scalar(score_d[:, half, :], mask[:, :], key_sum[:, 0:1], None,
                                            ALU.mult).then_inc(scores_masked, 1)

                def split_x(it, j):
                    dve.wait_ge(x_rounded, 2 * NCH * it + 2 * j + 2)
                    nc.vector.tensor_tensor(x_lo[:, j % XR, X_DVE, :], x_sb[:, j % XR, X_DVE, :],
                                            x_hi[:, j % XR, X_DVE, :].bitcast(F32), ALU.subtract).then_inc(x_split[0], 1)

                def split_weights(it):
                    dve.wait_ge(w_loaded, 16 * (it + 1))
                    nc.vector.tensor_copy(w_hi[:, :, :, :], w_sb[:, :, :, :]).then_inc(w_rounded, 1)
                    dve.wait_ge(w_rounded, it + 1)
                    nc.vector.tensor_tensor(w_lo[:, :, :, :], w_sb[:, :, :, :], w_hi[:, :, :, :].bitcast(F32),
                                            ALU.subtract).then_inc(w_split, 1)

                def divide(it, half, j):
                    dve.wait_ge(den_evac, START + at(it, half, j) + 1)
                    nc.vector.reciprocal(den_sb[:, :], den_sb[:, :]).then_inc(inverted, 1)
                    dve.wait_ge(inverted, at(it, half, j) + 1)
                    dve.wait_ge(out_written, 16 * START + 16 * at(it, half, j))
                    nc.vector.tensor_tensor(out_sb[:, :], NUM_BANK[:, :], den_sb[:, :], ALU.mult).then_inc(divided, 1)

                def plain(it, conv_of):
                    def outputs(step):
                        if conv_of is not None:
                            divide(conv_of, 1, step)
                        dve.wait_ge(evac[T_Q], NCH * it + step + 1)
                        for bordered, plain_q in eighths(step):
                            last = nc.vector.tensor_scalar(plain_q, bordered, 0.0, None, ALU.max)
                        last.then_inc(relu_q_ready, 1)

                    for step in range(NCH):
                        dve.wait_ge(qkv_ready, 3 * NCH * it + 3 * step + T_V + 1)
                        spread(nc.vector.tensor_copy, step, T_V).then_inc(evac[T_V], 1)
                        if step < NCH - 1:
                            outputs(step)
                        if step + XR < NCH:
                            split_x(it, step + XR)
                    for g in range(TURNS):
                        keys_by_position(it, g)
                    outputs(NCH - 1)
                    mask_scores(it, 0)

                def keys_of_heads(it, jj):
                    for par in range(2):
                        dve.wait_ge(cready[T_K], SH * it + 2 * jj + par + 1)
                        to = ckey_t[:, :, bass.ds((2 * jj + par) * HD, HD)].rearrange("p (s r) o -> p s r o", s=HV)
                        nc.vector.tensor_scalar(
                            to, banks[T_K][:, 0:HV * M].rearrange("p (s o r) -> p s r o", o=HD, r=PL), 0.0, None,
                            ALU.max).then_inc(cevac[T_K], 1)

                def conv(it, more):
                    with dve.Fori(0, SH // 2 - 1) as jj:
                        keys_of_heads(it, jj)
                        divide(it, 0, jj)
                    keys_of_heads(it, SH // 2 - 1)
                    if more:
                        split_weights(it + 1)
                        split_x(it + 1, 0)
                    divide(it, 0, SH // 2 - 1)
                    if more:
                        for j in range(1, XR):
                            split_x(it + 1, j)
                    mask_scores(it, 1)

                def first():
                    for s in (cevac[T_K], divided):
                        dve.sem_inc(s, START)
                    split_weights(0)
                    for j in range(XR):
                        split_x(0, j)
                    nc.vector.memset(tiles[T_V][:, :, :], 0.0).then_inc(cleared, 1)
                    nc.vector.memset(value_t[:, :, :, P:P + 1], 1.0)
                    nc.vector.memset(cvalue_t[:, :, P:P + 1], 1.0).then_inc(cleared, 1)
                    dve.wait_ge(cleared, 4)
                    dve.wait_ge(const_loaded, 32)
                    plain(0, None)

                def steady(it):
                    conv(it, True)
                    plain(it + 1, it)

                def final(it):
                    conv(it, False)
                    for j in range(NCH):
                        divide(it, 1, j)

                pairs(dve, first, steady, final)

            @block.gpsimd
            def _(pool):
                def split_x(it, j):
                    pool.wait_ge(x_rounded, 2 * NCH * it + 2 * j + 1)
                    nc.gpsimd.tensor_tensor(x_lo[:, j % XR, X_POOL, :], x_sb[:, j % XR, X_POOL, :],
                                            x_hi[:, j % XR, X_POOL, :].bitcast(F32), ALU.subtract).then_inc(x_split[1], 1)

                def build(it):
                    with pool.Fori(0, SH // 2) as jj:
                        for par in range(2):
                            pool.wait_ge(taps_loaded, 16 * (it + 1))
                            pool.wait_ge(head_done[par], START + SH // 2 * it + jj)
                            for t in range(3):
                                g = taps[:, :, :].rearrange("p (j t) n -> p j t n", t=3)[:, 2 * jj + par, t, :]
                                tap = g[:, 0:NTAP].rearrange("p (d r) -> p d r", r=PL)[:, :, None, :].to_broadcast(
                                    [P, len(SHIFTS), HD, PL])
                                point = g[:, NTAP:GT][:, None, :, None].to_broadcast([P, len(SHIFTS), HD, PL])
                                last = nc.gpsimd.tensor_tensor(
                                    toeplitz[:, par, t, :].rearrange("p (d o r) -> p d o r", o=HD, r=PL), tap, point, ALU.mult)
                            last.then_inc(toeplitz_ready, 1)

                def plain(it):
                    for j in range(NCH):
                        split_x(it, j)

                def first():
                    for j in range(XR):
                        split_x(0, j)
                    for t in (T_Q, T_K):
                        nc.gpsimd.memset(tiles[t][:, :, :], 0.0).then_inc(cleared, 1)
                    for j in range(XR, NCH):
                        split_x(0, j)

                def steady(it):
                    build(it)
                    plain(it + 1)

                pairs(pool, first, steady, build)


def edges(nc, banks, io, dram, out):
    with ExitStack() as ctx:
        def sb(name, shape):
            return ctx.enter_context(nc.sbuf_tensor(name, shape, F32))

        def sem(name):
            return ctx.enter_context(nc.semaphore(name))

        XR = CR + 2
        feat = sb("feat", [P, NE, N])
        xb = sb("xb", [P, KT, XR * W2])
        dx = sb("dx", [P, 2, XR, W])
        side = sb("side", [P, 2, XR, W])
        smooth = sb("smooth", [P, 2, XR, W])
        sobel_h = sb("sobel_h", [P, 2, CR, W])
        sobel_v = sb("sobel_v", [P, 2, CR, W])
        lap_sq = sb("lap_sq", [P, 2, CR, W])
        edge = sb("edge", [P, 2, NE, CH])
        w_branch = sb("w_branch", [P, KT, NE, P])
        w_fuse = sb("w_fuse", [P, KT, C])
        w_image = sb("w_image", [P, KT, C])
        w_att1 = sb("w_att1", [P, KT, HID])
        w_att2 = sb("w_att2", [HID, C])
        b_att1 = sb("b_att1", [HID, 1])
        vec = sb("edge_vec", [P, len(VEC), KT])
        bn_scale = sb("bn_scale", [P, NE])
        bn_shift = sb("bn_shift", [P, NE])
        z_shift = sb("z_shift", [P, KT])
        row_sum = sb("row_sum", [P, KT])
        pool_sum = sb("pool_sum", [P, NE, NCH])
        pooled = sb("pooled", [P, NE])
        hidden = sb("hidden", [HID, 1])
        gate = sb("gate", [P, KT])
        mean_w = sb("mean_w", [P, P])
        centred = sb("centred", [P, 2, KT, CH])
        square = sb("square", [P, KT, CH])
        std = sb("std", [P, CH])
        rstd = sb("rstd", [P, CH])
        x_out = sb("x_out", [P, 2, KT, CR * W2])
        w_proj = sb("w_proj", [P, TILES, C])
        att, x_res, x2_sb = centred, square, x_out[:, 1, :, :]
        scale = sb("proj_scale", [P, KT])
        root = sb("proj_root", [P, KT])
        shift = sb("proj_shift", [P, KT])
        eps = sb("edge_eps", [P, 4])

        const_loaded = sem("edge_const_loaded")
        set_up = sem("proj_set_up")
        rooted = sem("proj_rooted")
        scaled = sem("proj_scaled")
        att_loaded = [sem(f"att_loaded{i}") for i in range(2)]
        att_used = sem("att_used")
        res_loaded = sem("res_loaded")
        projected = sem("projected")
        shifted = sem("shifted")
        summed = sem("summed")
        x2_written = sem("x2_written")
        ready = sem("edge_const_ready")
        mean_ready = sem("mean_ready")
        xb_loaded = [sem(f"xb_loaded{k}") for k in range(KT)]
        xb_used = [sem(f"xb_used{k}") for k in range(KT)]
        names = ["side", "vert", "dx", "smooth", "diag", "rows", "sobel_v", "sobel_h", "cross",
                 "squares", "sum", "sum_lap", "edges"]
        done = {n: sem(f"{n}_done") for n in names}
        branched = sem("branched")
        feat_ready = sem("feat_ready")
        pool_summed = sem("pool_summed")
        pooled_ready = sem("pooled_ready")
        hidden_mm = sem("hidden_mm")
        hidden_ready = sem("hidden_ready")
        gate_mm = sem("gate_mm")
        gate_ready = sem("gate_ready")
        image_ready = sem("image_ready")
        fused = sem("fused")
        z_evac = [sem(f"z_evac{m}") for m in range(KT)]
        squared = sem("squared")
        var_ready = sem("var_ready")
        std_ready = sem("std_ready")
        rstd_ready = sem("rstd_ready")
        normed = [sem("normed_v"), sem("normed_p")]
        activated = sem("activated")
        out_ready = sem("out_ready")
        x_out_loaded = [sem(f"x_out_loaded{i}") for i in range(2)]
        stored = [sem(f"out_stored{i}") for i in range(2)]

        Z_BANKS, VAR_BANK = banks[4:8], banks[0]

        def v(name):
            return vec[:, VEC.index(name), :]

        def before(b, j, k):
            return KT * NCH * b + KT * j + k - 1

        def images(start, edge_maps, fusion):
            def chunks(b, p, eng):
                edge_maps(b, p, 0, True)
                with eng.Fori(1, NCH) as j:
                    edge_maps(b, p, j, False)
                edge_maps(b, p, None, False)

            def run(eng):
                start()
                chunks(None, 0, eng)
                with eng.Fori(0, B - 1) as b:
                    chunks(b, b + 1, eng)
                    fusion(b, b + 1)
                chunks(B - 1, None, eng)
                fusion(B - 1, None)
            return run

        with nc.Block() as block:
            @block.sync
            def _(sp):
                def start():
                    for s in stored:
                        sp.sem_inc(s, 16 * START)
                    for dst, src in ((vec[:, :, :].rearrange("p v m -> p (v m)"), io["vec"]),
                                     (w_proj[:, :, :].rearrange("p t o -> p (t o)"), io["projT"]),
                                     (w_branch[:, :, :, :].rearrange("p k e o -> p (k e o)"), io["branchT"]),
                                     (w_fuse[:, :, :].rearrange("p k o -> p (k o)"), io["fuseT"]),
                                     (w_att1[:, :, :].rearrange("p k o -> p (k o)"), io["att1T"]),
                                     (w_att2[:, :], io["att2T"]), (b_att1[:, :], io["b_att1"])):
                        sp.dma_start(dst, src).then_inc(const_loaded, 16)

                    def load_out(b, j):
                        sp.dma_start(x_out[:, j % 2, :, :],
                                     dram["x2"][b].rearrange("m p n -> p m n")[:, :, (CR * j + 1) * W2:(CR * j + 1 + CR) * W2]
                                     ).then_inc(x_out_loaded[j % 2], 16)

                def load_rows(b, j, first):
                    for k in range(KT):
                        if not first:
                            sp.wait_ge(xb_used[k], START + NCH * b + j)
                        sp.dma_start(xb[:, k, :], dram["x2"][b][k][:, bass.ds(j * (CR * W2), XR * W2)]
                                     ).then_inc(xb_loaded[k], 16)

                def maps(b, p, j, first):
                    if b is not None and j is not None and not first:
                        load_rows(b, j, False)
                    if p is None:
                        return
                    if j is not None:
                        c = NCH * p + j
                        n = bass.ds(j * CH, CH)
                        for i in range(2):
                            if first and b is not None:
                                sp.wait_ge(stored[i], 16 * START + 16 * (NCH // 2) * b)
                            if not first:
                                sp.wait_ge(*((att_used, c), (projected, KT * c))[i])
                            sp.dma_start(att[:, i, :, :], dram["att"][p].rearrange("t p n -> p t n")[:, i * KT:(i + 1) * KT, n]
                                         ).then_inc(att_loaded[i], 16)
                    if not first:
                        last = NCH - 1 if j is None else j - 1
                        sp.wait_ge(summed, KT * NCH * p + KT * (last + 1) + KT)
                        sp.dma_start(dram["x2"][p].rearrange("m p n -> p m n")[:, :, bass.ds(last * (CR * W2) + W2, CR * W2)],
                                     x2_sb).then_inc(x2_written, 16)
                    if j is None and b is None:
                        sp.wait_ge(x2_written, 16 * NCH * p + 16 * NCH)
                        load_rows(p, 0, True)
                    if j is not None:
                        sp.dma_start(x_res[:, :, :], io["x"][p].rearrange("(k p) n -> p k n", p=P)[:, :, n]
                                     ).then_inc(res_loaded, 16)

                def load_out(b, j):
                    sp.dma_start(x_out[:, j % 2, :, :],
                                 dram["x2"][b].rearrange("m p n -> p m n")[:, :, (CR * j + 1) * W2:(CR * j + 1 + CR) * W2]
                                 ).then_inc(x_out_loaded[j % 2], 16)

                def fusion(b, p):
                    sp.wait_ge(out_ready, START + KT * NCH * b)
                    load_out(b, 0)
                    if p is not None:
                        sp.wait_ge(x2_written, 16 * NCH * (p + 1))
                    load_out(b, 1)
                    if p is not None:
                        load_rows(p, 0, True)
                    for j in range(NCH):
                        sp.wait_ge(out_ready, START + KT * NCH * b + KT * (j + 1))
                        sp.dma_start(out[b].rearrange("(m p) n -> p m n", p=P)[:, :, j * CH:(j + 1) * CH],
                                     centred[:, j % 2, :, :]).then_inc(stored[j % 2], 16)
                        if j + 2 < NCH:
                            load_out(b, j + 2)

                images(start, maps, fusion)(sp)
                for i in range(2):
                    sp.wait_ge(stored[i], 16 * START + 16 * B * NCH // 2)

            @block.tensor
            def _(pe):
                def start():
                    for s in (branched, fused, var_ready):
                        pe.sem_inc(s, START)
                    pe.wait_ge(ready, 2)
                    for k in range(KT):
                        last = nc.tensor.matmul(banks[4][:, 0:1], mean_w[:, :], v("b_fuse")[:, k:k + 1],
                                                start=(k == 0), stop=(k == KT - 1))
                    last.then_inc(mean_ready, 1)
                    pe.wait_ge(ready, 5)

                def fuse(b, p, j):
                    if p is not None and j == 0:
                        pe.wait_ge(summed, KT * NCH * (p + 1) + KT)
                    for m in range(KT):
                        pe.wait_ge(z_evac[m], START + NCH * b + j)
                        for k in range(KT):
                            last = nc.tensor.matmul(Z_BANKS[m][:, :], w_image[:, k, m * P:(m + 1) * P],
                                                    feat[:, k, j * CH:(j + 1) * CH], start=(k == 0), stop=(k == KT - 1))
                        last.then_inc(fused, 1)

                def variance(b, j):
                    pe.wait_ge(std_ready, START + NCH * b + j)
                    for m in range(KT):
                        pe.wait_ge(squared, KT * NCH * b + KT * j + m + 1)
                        last = nc.tensor.matmul(VAR_BANK[:, :], mean_w[:, :], square[:, m, :],
                                                start=(m == 0), stop=(m == KT - 1))
                    last.then_inc(var_ready, 1)

                def project(p, j, step):
                    c = NCH * p + j
                    i, ms = step // 2, (0, 1) if step % 2 == 0 else (2, 3)
                    if step % 2 == 0:
                        pe.wait_ge(att_loaded[i], 16 * c + 16)
                    for m in ms:
                        if i == 0:
                            pe.wait_ge(summed, KT * c + m + 1)
                        for k in range(KT):
                            last = nc.tensor.matmul(Z_BANKS[m][:, :], w_proj[:, i * KT + k, m * P:(m + 1) * P],
                                                    att[:, i, k, :], start=(i == 0 and k == 0), stop=(i == 1 and k == KT - 1))
                        if i == 1 and m == ms[0]:
                            last.then_inc(projected, 1)
                    if i == 0:
                        if step % 2:
                            last.then_inc(att_used, 1)
                    else:
                        last.then_inc(projected, 1)

                def maps(b, p, j, first):
                    if j is None:
                        return
                    if b is not None:
                        if first:
                            pe.wait_ge(std_ready, START + NCH * b)
                            if p is not None:
                                for m in range(KT):
                                    pe.wait_ge(z_evac[m], START + NCH * b)
                    for k in range(KT):
                        if p is not None:
                            project(p, j, k)
                        if b is not None:
                            if k == 0:
                                pe.wait_ge(feat_ready, START + NE * NCH * b + NE * j)
                            pe.wait_ge(done["edges"], START + KT * NCH * b + KT * j + k + 1)
                            for e in range(NE):
                                last = nc.tensor.matmul(banks[e][:, :], w_branch[:, k, e, :], edge[:, k % 2, e, :],
                                                        start=(k == 0), stop=(k == KT - 1))
                            last.then_inc(branched, 1)

                def fusion(b, p):
                    pe.wait_ge(pooled_ready, b + 1)
                    for k in range(KT):
                        last = nc.tensor.matmul(banks[1][0:HID, 0:1], w_att1[:, k, :], pooled[:, k:k + 1],
                                                start=(k == 0), stop=(k == KT - 1))
                    last.then_inc(hidden_mm, 1)
                    pe.wait_ge(hidden_ready, b + 1)
                    for m in range(KT):
                        last = nc.tensor.matmul(banks[2][:, m:m + 1], w_att2[:, m * P:(m + 1) * P], hidden[:, 0:1],
                                                start=True, stop=True)
                    last.then_inc(gate_mm, 1)
                    pe.wait_ge(image_ready, KT * (b + 1))
                    for j in range(NCH + 1):
                        if j < NCH:
                            fuse(b, p, j)
                        if j >= 1:
                            variance(b, j - 1)

                images(start, maps, fusion)(pe)

            @block.scalar
            def _(act):
                def start():
                    for s in [done["squares"], done["edges"], feat_ready, std_ready] + z_evac:
                        act.sem_inc(s, START)
                    act.wait_ge(set_up, 1)
                    nc.scalar.activation(root[:, :], v("bn0_var"), ACT.Sqrt, bias=eps[:, 3:4]).then_inc(rooted, 1)
                    act.wait_ge(scaled, 3)
                    act.wait_ge(ready, 5)

                def squares(b, j, k):
                    s = k % 2
                    n = KT * NCH * b + KT * j + k + 1
                    act.wait_ge(branched, START + before(b, j, k))
                    act.wait_ge(done["sum_lap"], START + before(b, j, k))
                    act.wait_ge(done["diag"], n)
                    nc.scalar.activation(edge[:, s, 2, :], edge[:, s, 2, :], ACT.Abs)
                    act.wait_ge(done["sobel_h"], n)
                    nc.scalar.activation(sobel_h[:, s, :, :], sobel_h[:, s, :, :], ACT.Square)
                    nc.scalar.activation(sobel_v[:, s, :, :], sobel_v[:, s, :, :], ACT.Square)
                    act.wait_ge(xb_used[k], START + NCH * b + j + 1)
                    nc.scalar.activation(lap_sq[:, s, :, :], edge[:, s, 1, :].rearrange("p (r w) -> p r w", w=W), ACT.Square)
                    nc.scalar.activation(edge[:, s, 1, :], edge[:, s, 1, :], ACT.Abs).then_inc(done["squares"], 1)

                def roots(b, j, k):
                    s = k % 2
                    n = KT * NCH * b + KT * j + k + 1
                    act.wait_ge(done["sum"], n)
                    nc.scalar.activation(edge[:, s, 0, :].rearrange("p (r w) -> p r w", w=W), sobel_v[:, s, :, :], ACT.Sqrt,
                                         bias=eps[:, 0:1])
                    act.wait_ge(done["sum_lap"], START + n)
                    nc.scalar.activation(edge[:, s, 3, :].rearrange("p (r w) -> p r w", w=W), lap_sq[:, s, :, :], ACT.Sqrt,
                                         bias=eps[:, 1:2]).then_inc(done["edges"], 1)

                def centre(b, j):
                    act.wait_ge(stored[j % 2], 16 * START + 16 * (NCH // 2) * b + 16 * (j // 2))
                    for m in range(KT):
                        act.wait_ge(fused, START + KT * NCH * b + KT * j + m + 1)
                        if m == 0:
                            act.wait_ge(var_ready, START + NCH * b + j)
                        nc.scalar.activation(square[:, m, :], Z_BANKS[m][:, :], ACT.Square,
                                             bias=z_shift[:, m:m + 1]).then_inc(squared, 1)
                        nc.scalar.activation(centred[:, j % 2, m, :], Z_BANKS[m][:, :], ACT.Identity,
                                             bias=z_shift[:, m:m + 1]).then_inc(z_evac[m], 1)

                def finish(b, j):
                    act.wait_ge(var_ready, START + NCH * b + j + 1)
                    act.wait_ge(rstd_ready, START + NCH * b + j)
                    nc.scalar.activation(std[:, :], VAR_BANK[:, :], ACT.Sqrt, bias=eps[:, 2:3]).then_inc(std_ready, 1)
                    for m in range(KT):
                        act.wait_ge(normed[m % 2], START + KT // 2 * (NCH * b + j) + m // 2 + 1)
                        nc.scalar.activation(centred[:, j % 2, m, :], centred[:, j % 2, m, :], ACT.Gelu,
                                             scale=v("ln_gamma")[:, m:m + 1], bias=v("ln_beta")[:, m:m + 1]).then_inc(activated, 1)

                def features(b, j):
                    act.wait_ge(branched, START + KT * NCH * b + KT * j + KT)
                    for e in range(NE):
                        nc.scalar.activation(feat[:, e, bass.ds(j * CH, CH)], banks[e][:, :], ACT.Gelu,
                                             scale=bn_scale[:, e:e + 1], bias=bn_shift[:, e:e + 1],
                                             accum_out=pool_sum[:, e, bass.ds(j, 1)]).then_inc(feat_ready, 1)

                def maps(b, p, j, first):
                    if b is not None and j is None:
                        features(b, NCH - 1)
                    if b is not None and j is not None:
                        if first:
                            act.wait_ge(fused, START + KT * NCH * b)
                        for k in range(KT + 1):
                            if k >= 1:
                                roots(b, j, k - 1)
                            if k < KT:
                                squares(b, j, k)
                            if k == 0 and not first:
                                features(b, j - 1)

                def fusion(b, p):
                    act.wait_ge(hidden_mm, b + 1)
                    nc.scalar.activation(hidden[:, :], banks[1][0:HID, 0:1], ACT.Gelu, bias=b_att1[:, 0:1]).then_inc(hidden_ready, 1)
                    act.wait_ge(gate_mm, b + 1)
                    for m in range(KT):
                        nc.scalar.activation(gate[:, m:m + 1], banks[2][:, m:m + 1], ACT.Sigmoid,
                                             bias=v("b_att2")[:, m:m + 1]).then_inc(gate_ready, 1)
                    for j in range(NCH + 1):
                        if j < NCH:
                            centre(b, j)
                        if j >= 1:
                            finish(b, j - 1)

                images(start, maps, fusion)(act)

            @block.vector
            def _(dve):
                def start():
                    for s in [done["cross"], rstd_ready, normed[0], out_ready] + xb_used:
                        dve.sem_inc(s, START)
                    nc.vector.memset(mean_w[:, :], 1.0 / C).then_inc(ready, 1)
                    nc.vector.memset(eps[:, 0:1], EPS_GRAD)
                    nc.vector.memset(eps[:, 1:2], 2 * EPS_GRAD)
                    nc.vector.memset(eps[:, 2:3], EPS_LN)
                    nc.vector.memset(x2_sb, 0.0)
                    nc.vector.memset(eps[:, 3:4], EPS_BN)
                    dve.sem_inc(summed, KT)
                    dve.wait_ge(const_loaded, 112)
                    nc.vector.tensor_copy(shift[:, :], v("bn0_mean")).then_inc(set_up, 1)
                    dve.wait_ge(rooted, 1)
                    nc.vector.reciprocal(scale[:, :], root[:, :]).then_inc(scaled, 1)
                    dve.wait_ge(scaled, 1)
                    nc.vector.tensor_tensor(scale[:, :], scale[:, :], v("bn0_gamma"), ALU.mult).then_inc(scaled, 1)
                    dve.wait_ge(scaled, 2)
                    nc.vector.tensor_tensor(root[:, :], scale[:, :], shift[:, :], ALU.mult).then_inc(rooted, 1)
                    dve.wait_ge(rooted, 2)
                    nc.vector.tensor_tensor(shift[:, :], v("bn0_beta"), root[:, :], ALU.subtract).then_inc(scaled, 1)
                    nc.vector.tensor_scalar(bn_scale[:, :], v("bn1_gamma"), float((1.0 + EPS_BN) ** -0.5), None,
                                            ALU.mult).then_inc(ready, 1)
                    dve.wait_ge(ready, 2)
                    nc.vector.tensor_tensor(bn_shift[:, :], bn_scale[:, :], v("b_branch"), ALU.mult).then_inc(ready, 1)
                    dve.wait_ge(ready, 3)
                    nc.vector.tensor_tensor(bn_shift[:, :], bn_shift[:, :], v("bn1_beta"), ALU.add).then_inc(ready, 1)
                    dve.wait_ge(mean_ready, 1)
                    nc.vector.tensor_scalar(z_shift[:, :], v("b_fuse"), banks[4][:, 0:1], None, ALU.subtract).then_inc(ready, 1)
                    nc.vector.tensor_reduce(row_sum[:, :], w_fuse[:, :, :], AX_X, ALU.add).then_inc(ready, 1)
                    dve.wait_ge(ready, 6)
                    nc.vector.tensor_scalar(row_sum[:, :], row_sum[:, :], 1.0 / C, None, ALU.mult).then_inc(ready, 1)
                    dve.wait_ge(ready, 7)
                    for k in range(KT):
                        nc.vector.tensor_scalar(w_fuse[:, k, :], w_fuse[:, k, :], row_sum[:, k:k + 1], None,
                                                ALU.subtract).then_inc(ready, 1)

                def stencils(b, j, k):
                    s = k % 2
                    u = KT * NCH * b + KT * j + k
                    x = xb[:, k, :].rearrange("p (r w) -> p r w", w=W2)
                    dve.wait_ge(xb_loaded[k], 16 * NCH * b + 16 * j + 16)
                    nc.vector.tensor_tensor(dx[:, s, :, :], x[:, :, 2:W2], x[:, :, 0:W], ALU.subtract).then_inc(done["dx"], 1)
                    dve.wait_ge(done["side"], u + 1)
                    nc.vector.scalar_tensor_tensor(out=smooth[:, s, :, :], in0=x[:, :, 1:W + 1], scalar=2.0, in1=side[:, s, :, :],
                                                   op0=ALU.mult, op1=ALU.add).then_inc(done["smooth"], 1)
                    dve.wait_ge(done["dx"], u + 1)
                    dve.wait_ge(branched, START + before(b, j, k))
                    maps_of = edge[:, s, :, :].rearrange("p e (r w) -> p e r w", w=W)
                    nc.vector.tensor_tensor(maps_of[:, 2, :, :], dx[:, s, 2:XR, :], dx[:, s, 0:CR, :], ALU.subtract).then_inc(done["diag"], 1)
                    dve.wait_ge(done["edges"], START + before(b, j, k))
                    nc.vector.tensor_tensor(sobel_h[:, s, :, :], dx[:, s, 2:XR, :], dx[:, s, 0:CR, :], ALU.add).then_inc(done["rows"], 1)
                    dve.wait_ge(done["smooth"], u + 1)
                    nc.vector.tensor_tensor(sobel_v[:, s, :, :], smooth[:, s, 2:XR, :], smooth[:, s, 0:CR, :],
                                            ALU.subtract).then_inc(done["sobel_v"], 1)
                    dve.wait_ge(done["rows"], u + 1)
                    nc.vector.scalar_tensor_tensor(out=sobel_h[:, s, :, :], in0=dx[:, s, 1:XR - 1, :], scalar=2.0,
                                                   in1=sobel_h[:, s, :, :], op0=ALU.mult, op1=ALU.add).then_inc(done["sobel_h"], 1)
                    dve.wait_ge(done["vert"], u + 1)
                    nc.vector.tensor_tensor(maps_of[:, 1, :, :], maps_of[:, 1, :, :], side[:, s, 1:XR - 1, :], ALU.add).then_inc(done["cross"], 1)
                    dve.wait_ge(done["cross"], START + u + 1)
                    nc.vector.scalar_tensor_tensor(out=maps_of[:, 1, :, :], in0=x[:, 1:XR - 1, 1:W + 1], scalar=-4.0,
                                                   in1=maps_of[:, 1, :, :], op0=ALU.mult, op1=ALU.add).then_inc(xb_used[k], 1)

                def norm(b, j):
                    dve.wait_ge(std_ready, START + NCH * b + j + 1)
                    dve.wait_ge(normed[1], START + KT // 2 * (NCH * b + j))
                    nc.vector.reciprocal(rstd[:, :], std[:, :]).then_inc(rstd_ready, 1)
                    dve.wait_ge(rstd_ready, START + NCH * b + j + 1)
                    for m in (0, 2):
                        dve.wait_ge(z_evac[m], START + NCH * b + j + 1)
                        nc.vector.tensor_tensor(centred[:, j % 2, m, :], centred[:, j % 2, m, :], rstd[:, :],
                                                ALU.mult).then_inc(normed[0], 1)

                def residual(b, j):
                    dve.wait_ge(x_out_loaded[j % 2], 16 * (NCH // 2) * b + 16 * (j // 2) + 16)
                    for m in range(KT):
                        dve.wait_ge(activated, KT * NCH * b + KT * j + m + 1)
                        y = centred[:, j % 2, m, :].rearrange("p (r w) -> p r w", w=W)
                        nc.vector.tensor_tensor(y, y, x_out[:, j % 2, m, :].rearrange("p (r w) -> p r w", w=W2)[:, :, 1:W + 1],
                                                ALU.add).then_inc(out_ready, 1)

                def add_residual(p, last, ms):
                    c = KT * NCH * p + KT * last
                    if ms[0] == 0:
                        dve.wait_ge(x2_written, 16 * NCH * p + 16 * last)
                    for m in ms:
                        dve.wait_ge(shifted, c + m + 1)
                        dve.wait_ge(projected, c + m + 1)
                        nc.vector.scalar_tensor_tensor(
                            out=x2_sb[:, m, :].rearrange("p (r w) -> p r w", w=W2)[:, :, 1:W + 1],
                            in0=Z_BANKS[m][:, :].rearrange("p (r w) -> p r w", w=W), scalar=scale[:, m:m + 1],
                            in1=x_res[:, m, :].rearrange("p (r w) -> p r w", w=W),
                            op0=ALU.mult, op1=ALU.add).then_inc(summed, 1)

                def maps(b, p, j, first):
                    for k in range(KT):
                        if b is not None and j is not None:
                            stencils(b, j, k)
                        if p is not None and not first and k < 2:
                            add_residual(p, NCH - 1 if j is None else j - 1, (2 * k, 2 * k + 1))

                def fusion(b, p):
                    dve.wait_ge(feat_ready, START + NE * NCH * b + NE * NCH)
                    nc.vector.tensor_reduce(row_sum[:, :], pool_sum[:, :, :], AX_X, ALU.add).then_inc(pool_summed, 1)
                    dve.wait_ge(pool_summed, b + 1)
                    nc.vector.tensor_scalar(pooled[:, :], row_sum[:, :], 1.0 / N, None, ALU.mult).then_inc(pooled_ready, 1)
                    dve.wait_ge(gate_ready, KT * (b + 1))
                    for k in range(KT):
                        nc.vector.tensor_scalar(w_image[:, k, :], w_fuse[:, k, :], gate[:, k:k + 1], None,
                                                ALU.mult).then_inc(image_ready, 1)
                    for j in range(NCH):
                        norm(b, j)
                        residual(b, j)

                images(start, maps, fusion)(dve)

            @block.gpsimd
            def _(pool):
                def neighbours(b, j, k):
                    s = k % 2
                    x = xb[:, k, :].rearrange("p (r w) -> p r w", w=W2)
                    pool.wait_ge(xb_loaded[k], 16 * NCH * b + 16 * j + 16)
                    pool.wait_ge(done["cross"], START + before(b, j, k))
                    nc.gpsimd.tensor_tensor(side[:, s, :, :], x[:, :, 0:W], x[:, :, 2:W2], ALU.add).then_inc(done["side"], 1)

                def verticals(b, j, k):
                    s = k % 2
                    x = xb[:, k, :].rearrange("p (r w) -> p r w", w=W2)
                    pool.wait_ge(branched, START + before(b, j, k))
                    nc.gpsimd.tensor_tensor(edge[:, s, 1, :].rearrange("p (r w) -> p r w", w=W), x[:, 0:CR, 1:W + 1], x[:, 2:XR, 1:W + 1], ALU.add).then_inc(done["vert"], 1)

                def sums(b, j, k):
                    s = k % 2
                    n = KT * NCH * b + KT * j + k + 1
                    pool.wait_ge(done["squares"], START + n)
                    nc.gpsimd.tensor_tensor(sobel_v[:, s, :, :], sobel_v[:, s, :, :], sobel_h[:, s, :, :], ALU.add).then_inc(done["sum"], 1)
                    pool.wait_ge(done["sum"], n)
                    nc.gpsimd.tensor_tensor(lap_sq[:, s, :, :], lap_sq[:, s, :, :], sobel_v[:, s, :, :], ALU.add).then_inc(done["sum_lap"], 1)

                def start():
                    for s in (done["sum_lap"], normed[1]):
                        pool.sem_inc(s, START)
                    pool.wait_ge(scaled, 3)

                def maps(b, p, j, first):
                    if j is None:
                        return
                    for k in range(KT + 1):
                        if k < KT and b is not None:
                            neighbours(b, j, k)
                        if k >= 1 and b is not None:
                            sums(b, j, k - 1)
                        if k < KT and b is not None:
                            verticals(b, j, k)
                        if k >= 1 and p is not None:
                            if k == 1:
                                pool.wait_ge(res_loaded, 16 * NCH * p + 16 * j + 16)
                            nc.gpsimd.tensor_tensor(x_res[:, k - 1, :], x_res[:, k - 1, :],
                                                    shift[:, k - 1:k].to_broadcast([P, CH]), ALU.add).then_inc(shifted, 1)

                def fusion(b, p):
                    for j in range(NCH):
                        pool.wait_ge(rstd_ready, START + NCH * b + j + 1)
                        for m in (1, 3):
                            pool.wait_ge(z_evac[m], START + NCH * b + j + 1)
                            nc.gpsimd.tensor_tensor(centred[:, j % 2, m, :], centred[:, j % 2, m, :], rstd[:, :],
                                                    ALU.mult).then_inc(normed[1], 1)

                images(start, maps, fusion)(pool)


def program(nc, io, out):
    dram = {
        "taps": nc.dram_tensor("taps_dram", [HS, P, 3 * SH * GT], F32, kind="Internal").ap(),
        "conv_q": nc.dram_tensor("conv_q_dram", [SH, M, TT], F32, kind="Internal").ap(),
        "att": nc.dram_tensor("att_dram", [B, TILES, P, N], F32, kind="Internal").ap(),
        "x2": nc.dram_tensor("x2_dram", [B, KT, P, H2 * W2], F32, kind="Internal").ap(),
    }
    with ExitStack() as ctx:
        banks = [ctx.enter_context(nc.psum_tensor(f"bank{i}", [P, CH], F32)) for i in range(8)]
        prepare(nc, banks, io, dram)
        attention(nc, banks, io, dram)
        edges(nc, banks, io, dram, out)


def kernel(x, L0_conv_wq, L0_conv_wk, L0_conv_wv, L0_conv_dw_kernel, L0_conv_pw_kernel, L0_conv_proj_kernel,
           L0_conv_bn_gamma, L0_conv_bn_beta, L0_conv_bn_mean, L0_conv_bn_var, L1_conv_w_branch, L1_conv_b_branch,
           L1_conv_bn_gamma, L1_conv_bn_beta, L1_conv_w_att1, L1_conv_b_att1, L1_conv_w_att2, L1_conv_b_att2,
           L1_conv_w_fuse, L1_conv_b_fuse, L1_conv_ln_gamma, L1_conv_ln_beta):
    import numpy as np
    import concourse.bacc as bacc
    from concourse.bass_utils import run_bass_kernel_spmd

    def a(t):
        return np.asarray(t)

    w = np.concatenate([a(L0_conv_wq), a(L0_conv_wk), a(L0_conv_wv)], 0)
    tap_sel = np.zeros((HD, KS, TS, 2, TS, HD, TS, TS), np.float32)
    row_rep = np.zeros((HD, HD, PL), np.float32)
    for i in range(HD):
        row_rep[i, i, :] = 1
        for sy in range(2):
            for oy in range(TS):
                for ry in range(TS):
                    if 0 <= ry + TS * sy - oy < KS:
                        for rx in range(TS):
                            tap_sel[i, ry + TS * sy - oy, rx, sy, oy, i, ry, rx] = 1
    vectors = [a(L0_conv_bn_gamma), a(L0_conv_bn_beta), a(L0_conv_bn_mean), a(L0_conv_bn_var),
               a(L1_conv_b_branch).reshape(C), a(L1_conv_bn_gamma).reshape(C), a(L1_conv_bn_beta).reshape(C),
               a(L1_conv_b_att2), a(L1_conv_b_fuse), a(L1_conv_ln_gamma), a(L1_conv_ln_beta)]
    arrays = {
        "x": a(x).reshape(B, C, N),
        "wT": w.reshape(HS, SH, 3, HD, KT, P).transpose(0, 5, 4, 2, 1, 3).reshape(HS, P, KT * 3 * P),
        "dwT": a(L0_conv_dw_kernel).reshape(NG, HD, KS, KS).transpose(1, 2, 3, 0).reshape(HD * KS, KS * NG),
        "pwT": a(L0_conv_pw_kernel).reshape(NG, HD, HD).transpose(2, 0, 1).reshape(HD, NG * HD),
        "projT": a(L0_conv_proj_kernel).reshape(C, TILES, P).transpose(2, 1, 0).reshape(P, TILES * C),
        "branchT": a(L1_conv_w_branch).reshape(NE, P, KT, P).transpose(3, 2, 0, 1).reshape(P, KT * NE * P),
        "fuseT": a(L1_conv_w_fuse).reshape(C, KT, P).transpose(2, 1, 0).reshape(P, KT * C),
        "att1T": a(L1_conv_w_att1).reshape(HID, KT, P).transpose(2, 1, 0).reshape(P, KT * HID),
        "att2T": a(L1_conv_w_att2).T,
        "b_att1": a(L1_conv_b_att1).reshape(HID, 1),
        "vec": np.stack(vectors).reshape(len(VEC), KT, P).transpose(2, 0, 1).reshape(P, len(VEC) * KT),
        "tap_sel": tap_sel.reshape(HD * KS, TS * 2 * TS * P),
        "row_rep": row_rep.reshape(HD, P),
        "ident": np.eye(P, dtype=np.float32),
        "head_mask": np.kron(np.eye(SH, dtype=np.float32), np.ones((HD, HD), np.float32)),
    }
    nc = bacc.Bacc("TRN2", target_bir_lowering=False, num_devices=1)
    feeds, io = {}, {}
    for name, value in arrays.items():
        feeds[f"in_{name}"] = np.ascontiguousarray(value)
        io[name] = nc.dram_tensor(f"in_{name}", value.shape, F32, kind="ExternalInput").ap()
    out = nc.dram_tensor("out", (B, C, N), F32, kind="ExternalOutput").ap()
    program(nc, io, out)
    result = run_bass_kernel_spmd(nc, [feeds], core_ids=[0])
    return result.results[0]["out"].reshape(B, C, H, W)
```
